# Optimizing a Trainium2 kernel written in Bass

```python
import numpy as np
import jax
import jax.numpy as jnp

def _softmax(x, axis=-1):
    return jax.nn.softmax(x, axis=axis)

def _gelu(x):
    return jax.nn.gelu(x, approximate=True)

def _silu(x):
    return jax.nn.silu(x)

def _sigmoid(x):
    return jax.nn.sigmoid(x)

def _layernorm(x, axis=-1, eps=1e-05):
    m = jnp.mean(x, axis=axis, keepdims=True)
    v = jnp.var(x, axis=axis, keepdims=True)
    return (x - m) / jnp.sqrt(v + eps)

def _scatter_add(tgt, idx, src, axis=0):
    return tgt.at[idx].add(src)

def _segment_sum(src, seg, n):
    return jax.ops.segment_sum(src, seg, n)
kernel_name = 'mk_lm_tower_d2_tok_ids1024_r4_1fcaa9'

def setup_inputs(seed: int=0):
    np.random.seed(seed)
    _w = jnp.asarray

    def _rec_inputs():
        import jax
        import jax.numpy as jnp
        _rk = jax.random.key(seed)
        x = jax.random.randint(jax.random.fold_in(_rk, 1), (64, 64), 0, 365, jnp.int32)
        return x
    x = _rec_inputs()

    def _L0_tok_setup():
        import jax, jax.numpy as jnp
        import numpy as np
        B, T, D, NUM_DAYS = (128, 64, 256, 365)
        key = jax.random.key(seed)
        k1, k2, k3 = jax.random.split(key, 3)
        days_of_year = jax.random.randint(k1, (B, T), 0, NUM_DAYS)
        W = jax.random.normal(k2, (NUM_DAYS, D), dtype=jnp.float32) * (1.0 / np.sqrt(NUM_DAYS))
        b = jax.random.normal(k3, (D,), dtype=jnp.float32) * 0.01
        return {'days_of_year': days_of_year, 'W': W, 'b': b}
    _L0_tok_all = _L0_tok_setup()
    _L0_tok_in = {k: v for k, v in _L0_tok_all.items() if k in ('W', 'b')}
    del _L0_tok_all

    def _L0_attn_setup():
        import jax, jax.numpy as jnp
        import numpy as np
        D_MODEL = 256
        NUM_HEADS = 16
        D_K = D_MODEL // NUM_HEADS
        MAX_LEN = 256
        BATCH = 8
        SEQ = 256
        key = jax.random.key(seed)
        ks = jax.random.split(key, 12)
        s = 0.02
        inp = {'x': jax.random.normal(ks[0], (BATCH, SEQ, D_MODEL), dtype=jnp.float32), 'Wq': jax.random.normal(ks[1], (D_MODEL, D_MODEL), dtype=jnp.float32) * s, 'bq': jnp.zeros((D_MODEL,), dtype=jnp.float32), 'Wk': jax.random.normal(ks[2], (D_MODEL, D_MODEL), dtype=jnp.float32) * s, 'bk': jnp.zeros((D_MODEL,), dtype=jnp.float32), 'Wv': jax.random.normal(ks[3], (D_MODEL, D_MODEL), dtype=jnp.float32) * s, 'bv': jnp.zeros((D_MODEL,), dtype=jnp.float32), 'Wo': jax.random.normal(ks[4], (D_MODEL, D_MODEL), dtype=jnp.float32) * s, 'bo': jnp.zeros((D_MODEL,), dtype=jnp.float32), 'relative_k': jax.random.normal(ks[5], (2 * MAX_LEN - 1, D_K), dtype=jnp.float32), 'relative_v': jax.random.normal(ks[6], (2 * MAX_LEN - 1, D_K), dtype=jnp.float32)}
        return inp
    _L0_attn_all = _L0_attn_setup()
    _L0_attn_in = {k: v for k, v in _L0_attn_all.items() if k in ('Wq', 'bq', 'Wk', 'bk', 'Wv', 'bv', 'Wo', 'bo', 'relative_k', 'relative_v')}
    del _L0_attn_all

    def _L0_ffn_setup():
        import jax, jax.numpy as jnp
        import numpy as np
        BEST_K = 2

        def _expert(xf, w1, w3, w2):
            return jax.nn.silu(xf @ w1) * (xf @ w3) @ w2
        key = jax.random.key(seed)
        ks = jax.random.split(key, 9)
        E, S_sh, D, H = (8, 2, 256, 128)
        B, S = (2, 512)
        w = lambda k, shape: jax.random.normal(k, shape, dtype=jnp.float32) * 0.02
        return {'x': jax.random.normal(ks[0], (B, S, D), dtype=jnp.float32), 'router_w': w(ks[1], (D, E)), 'router_b': jnp.zeros((E,), dtype=jnp.float32), 'routed_w1': w(ks[2], (E, D, H)), 'routed_w3': w(ks[3], (E, D, H)), 'routed_w2': w(ks[4], (E, H, D)), 'shared_w1': w(ks[5], (S_sh, D, H)), 'shared_w3': w(ks[6], (S_sh, D, H)), 'shared_w2': w(ks[7], (S_sh, H, D))}
    _L0_ffn_all = _L0_ffn_setup()
    _L0_ffn_in = {k: v for k, v in _L0_ffn_all.items() if k in ('router_w', 'router_b', 'routed_w1', 'routed_w3', 'routed_w2', 'shared_w1', 'shared_w3', 'shared_w2')}
    del _L0_ffn_all

    def _L1_attn_setup():
        import jax, jax.numpy as jnp
        import numpy as np
        B, T, DM = (2, 512, 256)
        DH = 128
        NH = DM // DH
        ROTARY_BASE = 10000.0

        def fractional_rope(x, base):
            dh = x.shape[-1]
            rot, skip = jnp.split(x, 2, axis=-1)
            width = rot.shape[-1]
            half = width // 2
            t = rot.shape[-2]
            positions = jnp.arange(t)[:, None]
            dims = jnp.arange(half)
            ang_freqs = jnp.power(base, -dims / half)[None, :]
            radians = positions * ang_freqs
            cos = jnp.cos(radians).astype(x.dtype)
            sin = jnp.sin(radians).astype(x.dtype)
            even, odd = jnp.split(rot, 2, axis=-1)
            r_even = even * cos - odd * sin
            r_odd = even * sin + odd * cos
            return jnp.concatenate([r_even, r_odd, skip], axis=-1)
        key = jax.random.key(seed)
        ks = jax.random.split(key, 5)
        scale = (1.0 / DM) ** 0.5
        x = jax.random.normal(ks[0], (B, T, DM), dtype=jnp.float32)
        wq = jax.random.normal(ks[1], (NH, DM, DH), dtype=jnp.float32) * scale
        wk = jax.random.normal(ks[2], (NH, DM, DH), dtype=jnp.float32) * scale
        wv = jax.random.normal(ks[3], (NH, DM, DH), dtype=jnp.float32) * scale
        wo = jax.random.normal(ks[4], (NH * DH, DM), dtype=jnp.float32) * (1.0 / (NH * DH)) ** 0.5
        return {'x': x, 'wq': wq, 'wk': wk, 'wv': wv, 'wo': wo}
    _L1_attn_all = _L1_attn_setup()
    _L1_attn_in = {k: v for k, v in _L1_attn_all.items() if k in ('wq', 'wk', 'wv', 'wo')}
    del _L1_attn_all

    def _L1_ffn_setup():
        import jax, jax.numpy as jnp
        import numpy as np
        H, KVH, HD, D = (8, 2, 128, 256)
        E, TOPK, FFN = (8, 2, 896)
        THETA, EPS = (1000000.0, 1e-05)
        NBITS, GS = (4, 128)
        QMAX = float(2 ** NBITS - 1)
        NEG = -1e+30

        def qgroup(w):
            shp = w.shape
            w2 = w.reshape(-1, GS)
            wmax = jnp.max(w2, -1, keepdims=True)
            wmin = jnp.min(w2, -1, keepdims=True)
            scales = jnp.clip(wmax - wmin, 1e-05, None) / QMAX
            base = jnp.clip(jnp.round(-wmin / scales), 0.0, QMAX)
            wq = (jnp.clip(jnp.round(w2 / scales) + base, 0.0, QMAX) - base) * scales
            return wq.reshape(shp)

        def rms(x, g):
            return x * jax.lax.rsqrt(jnp.mean(x * x, -1, keepdims=True) + EPS) * g

        def rot_half(x):
            h = x.shape[-1] // 2
            return jnp.concatenate([-x[..., h:], x[..., :h]], axis=-1)
        key = jax.random.key(seed)
        ks = jax.random.split(key, 12)
        B, S = (2, 256)
        n = lambda k, s: 0.02 * jax.random.normal(k, s, dtype=jnp.float32)
        return {'hidden_states': jax.random.normal(ks[0], (B, S, D), dtype=jnp.float32), 'w_q': n(ks[1], (H * HD, D)), 'w_k': n(ks[2], (KVH * HD, D)), 'w_v': n(ks[3], (KVH * HD, D)), 'w_o': n(ks[4], (D, H * HD)), 'g1': jnp.ones((D,), jnp.float32), 'g2': jnp.ones((D,), jnp.float32), 'w_gate': n(ks[5], (E, D)), 'w1': n(ks[6], (E, FFN, D)), 'w3': n(ks[7], (E, FFN, D)), 'w2': n(ks[8], (E, D, FFN))}
    _L1_ffn_all = _L1_ffn_setup()
    _L1_ffn_in = {k: v for k, v in _L1_ffn_all.items() if k in ('w_q', 'w_k', 'w_v', 'w_o', 'g1', 'g2', 'w_gate', 'w1', 'w3', 'w2')}
    del _L1_ffn_all
    return {'x': x, 'L0_tok_W': _L0_tok_in['W'], 'L0_tok_b': _L0_tok_in['b'], 'L0_attn_Wq': _L0_attn_in['Wq'], 'L0_attn_bq': _L0_attn_in['bq'], 'L0_attn_Wk': _L0_attn_in['Wk'], 'L0_attn_bk': _L0_attn_in['bk'], 'L0_attn_Wv': _L0_attn_in['Wv'], 'L0_attn_bv': _L0_attn_in['bv'], 'L0_attn_Wo': _L0_attn_in['Wo'], 'L0_attn_bo': _L0_attn_in['bo'], 'L0_attn_relative_k': _L0_attn_in['relative_k'], 'L0_attn_relative_v': _L0_attn_in['relative_v'], 'L0_ffn_router_w': _L0_ffn_in['router_w'], 'L0_ffn_router_b': _L0_ffn_in['router_b'], 'L0_ffn_routed_w1': _L0_ffn_in['routed_w1'], 'L0_ffn_routed_w3': _L0_ffn_in['routed_w3'], 'L0_ffn_routed_w2': _L0_ffn_in['routed_w2'], 'L0_ffn_shared_w1': _L0_ffn_in['shared_w1'], 'L0_ffn_shared_w3': _L0_ffn_in['shared_w3'], 'L0_ffn_shared_w2': _L0_ffn_in['shared_w2'], 'L1_attn_wq': _L1_attn_in['wq'], 'L1_attn_wk': _L1_attn_in['wk'], 'L1_attn_wv': _L1_attn_in['wv'], 'L1_attn_wo': _L1_attn_in['wo'], 'L1_ffn_w_q': _L1_ffn_in['w_q'], 'L1_ffn_w_k': _L1_ffn_in['w_k'], 'L1_ffn_w_v': _L1_ffn_in['w_v'], 'L1_ffn_w_o': _L1_ffn_in['w_o'], 'L1_ffn_g1': _L1_ffn_in['g1'], 'L1_ffn_g2': _L1_ffn_in['g2'], 'L1_ffn_w_gate': _L1_ffn_in['w_gate'], 'L1_ffn_w1': _L1_ffn_in['w1'], 'L1_ffn_w3': _L1_ffn_in['w3'], 'L1_ffn_w2': _L1_ffn_in['w2']}

def reference(x, L0_tok_W, L0_tok_b, L0_attn_Wq, L0_attn_bq, L0_attn_Wk, L0_attn_bk, L0_attn_Wv, L0_attn_bv, L0_attn_Wo, L0_attn_bo, L0_attn_relative_k, L0_attn_relative_v, L0_ffn_router_w, L0_ffn_router_b, L0_ffn_routed_w1, L0_ffn_routed_w3, L0_ffn_routed_w2, L0_ffn_shared_w1, L0_ffn_shared_w3, L0_ffn_shared_w2, L1_attn_wq, L1_attn_wk, L1_attn_wv, L1_attn_wo, L1_ffn_w_q, L1_ffn_w_k, L1_ffn_w_v, L1_ffn_w_o, L1_ffn_g1, L1_ffn_g2, L1_ffn_w_gate, L1_ffn_w1, L1_ffn_w3, L1_ffn_w2):
    import jax
    import jax.numpy as jnp

    def _L0_tok_ref(days_of_year, W, b):
        import jax, jax.numpy as jnp
        import numpy as np
        B, T, D, NUM_DAYS = (128, 64, 256, 365)
        return W[days_of_year] + b

    def _L0_attn_ref(x, Wq, bq, Wk, bk, Wv, bv, Wo, bo, relative_k, relative_v):
        import jax, jax.numpy as jnp
        import numpy as np
        D_MODEL = 256
        NUM_HEADS = 16
        D_K = D_MODEL // NUM_HEADS
        MAX_LEN = 256
        BATCH = 8
        SEQ = 256
        B, L, D = x.shape
        H, dk = (NUM_HEADS, D_K)
        Q = (x @ Wq.T + bq).reshape(B, L, H, dk).transpose(0, 2, 1, 3)
        K = (x @ Wk.T + bk).reshape(B, L, H, dk).transpose(0, 2, 1, 3)
        V = (x @ Wv.T + bv).reshape(B, L, H, dk).transpose(0, 2, 1, 3)
        rel_pos = jnp.arange(L)[None, :] - jnp.arange(L)[:, None] + (MAX_LEN - 1)
        rel_k = relative_k[rel_pos]
        rel_v = relative_v[rel_pos]
        scale = 1.0 / np.sqrt(dk).astype(np.float32)
        scores = jnp.einsum('bhld,bhrd->bhlr', Q, K) * scale
        scores = scores + jnp.einsum('bhld,lrd->bhlr', Q, rel_k)
        attn = jax.nn.softmax(scores, axis=-1)
        out = jnp.einsum('bhlr,bhrd->bhld', attn, V)
        out = out + jnp.einsum('bhlr,lrd->bhld', attn, rel_v)
        out = out.transpose(0, 2, 1, 3).reshape(B, L, D)
        return out @ Wo.T + bo

    def _L0_ffn_ref(x, router_w, router_b, routed_w1, routed_w3, routed_w2, shared_w1, shared_w3, shared_w2):
        import jax, jax.numpy as jnp
        import numpy as np
        BEST_K = 2

        def _expert(xf, w1, w3, w2):
            return jax.nn.silu(xf @ w1) * (xf @ w3) @ w2
        B, S, D = x.shape
        T = B * S
        xf = x.reshape(T, D)
        logits = xf @ router_w + router_b
        topk_vals, topk_idx = jax.lax.top_k(logits, BEST_K)
        sparse = jnp.full_like(logits, -jnp.inf)
        sparse = sparse.at[jnp.arange(T)[:, None], topk_idx].set(topk_vals)
        gates = jax.nn.softmax(sparse, axis=-1)
        routed = jax.vmap(_expert, in_axes=(None, 0, 0, 0))(xf, routed_w1, routed_w3, routed_w2)
        routed_out = jnp.einsum('etd,te->td', routed, gates)
        shared_out = jax.vmap(_expert, in_axes=(None, 0, 0, 0))(xf, shared_w1, shared_w3, shared_w2).sum(axis=0)
        return (routed_out + shared_out).reshape(B, S, D)

    def _L1_attn_ref(x, wq, wk, wv, wo):
        import jax, jax.numpy as jnp
        import numpy as np
        B, T, DM = (2, 512, 256)
        DH = 128
        NH = DM // DH
        ROTARY_BASE = 10000.0

        def fractional_rope(x, base):
            dh = x.shape[-1]
            rot, skip = jnp.split(x, 2, axis=-1)
            width = rot.shape[-1]
            half = width // 2
            t = rot.shape[-2]
            positions = jnp.arange(t)[:, None]
            dims = jnp.arange(half)
            ang_freqs = jnp.power(base, -dims / half)[None, :]
            radians = positions * ang_freqs
            cos = jnp.cos(radians).astype(x.dtype)
            sin = jnp.sin(radians).astype(x.dtype)
            even, odd = jnp.split(rot, 2, axis=-1)
            r_even = even * cos - odd * sin
            r_odd = even * sin + odd * cos
            return jnp.concatenate([r_even, r_odd, skip], axis=-1)
        b, t, dm = x.shape
        q = jnp.einsum('btd,hdk->bhtk', x, wq)
        k = jnp.einsum('btd,hdk->bhtk', x, wk)
        v = jnp.einsum('btd,hdk->bhtk', x, wv)
        q = fractional_rope(q, ROTARY_BASE)
        k = fractional_rope(k, ROTARY_BASE)
        inv_sqrt_dh = DH ** (-0.5)
        q = q * inv_sqrt_dh
        k = k * inv_sqrt_dh
        s = jnp.einsum('bhik,bhjk->bhij', q, k)
        i = jnp.arange(t)[:, None]
        j = jnp.arange(t)[None, :]
        mask = jnp.less(i, j).astype(s.dtype)
        s = s - 1e+30 * mask
        p = jax.nn.softmax(s, axis=-1)
        o = jnp.einsum('bhij,bhjv->bihv', p, v)
        o = jnp.reshape(o, (b, t, NH * DH))
        return jnp.einsum('bto,od->btd', o, wo)

    def _L1_ffn_ref(hidden_states, w_q, w_k, w_v, w_o, g1, g2, w_gate, w1, w3, w2):
        import jax, jax.numpy as jnp
        import numpy as np
        H, KVH, HD, D = (8, 2, 128, 256)
        E, TOPK, FFN = (8, 2, 896)
        THETA, EPS = (1000000.0, 1e-05)
        NBITS, GS = (4, 128)
        QMAX = float(2 ** NBITS - 1)
        NEG = -1e+30

        def qgroup(w):
            shp = w.shape
            w2 = w.reshape(-1, GS)
            wmax = jnp.max(w2, -1, keepdims=True)
            wmin = jnp.min(w2, -1, keepdims=True)
            scales = jnp.clip(wmax - wmin, 1e-05, None) / QMAX
            base = jnp.clip(jnp.round(-wmin / scales), 0.0, QMAX)
            wq = (jnp.clip(jnp.round(w2 / scales) + base, 0.0, QMAX) - base) * scales
            return wq.reshape(shp)

        def rms(x, g):
            return x * jax.lax.rsqrt(jnp.mean(x * x, -1, keepdims=True) + EPS) * g

        def rot_half(x):
            h = x.shape[-1] // 2
            return jnp.concatenate([-x[..., h:], x[..., :h]], axis=-1)
        B, S, _ = hidden_states.shape
        T = B * S
        xn = rms(hidden_states, g1)
        q = (xn @ qgroup(w_q).T).reshape(B, S, H, HD).transpose(0, 2, 1, 3)
        k = (xn @ qgroup(w_k).T).reshape(B, S, KVH, HD).transpose(0, 2, 1, 3)
        v = (xn @ qgroup(w_v).T).reshape(B, S, KVH, HD).transpose(0, 2, 1, 3)
        k = qgroup(k)
        pos = jnp.arange(S, dtype=jnp.float32)
        inv = 1.0 / THETA ** (jnp.arange(0, HD, 2, dtype=jnp.float32) / HD)
        freqs = pos[:, None] * inv[None, :]
        emb = jnp.concatenate([freqs, freqs], axis=-1)
        cos = jnp.cos(emb)[None, None]
        sin = jnp.sin(emb)[None, None]
        q = q * cos + rot_half(q) * sin
        k = k * cos + rot_half(k) * sin
        rep = H // KVH
        k = jnp.repeat(k, rep, axis=1)
        v = jnp.repeat(v, rep, axis=1)
        v = qgroup(v)
        scores = jnp.einsum('bhqd,bhkd->bhqk', q, k) / np.float32(np.sqrt(HD))
        causal = jnp.tril(jnp.ones((S, S), dtype=bool))
        scores = jnp.where(causal[None, None], scores, NEG)
        attn = jax.nn.softmax(scores, axis=-1)
        o = jnp.einsum('bhqk,bhkd->bhqd', attn, v).transpose(0, 2, 1, 3).reshape(B, S, H * HD)
        h = hidden_states + o @ qgroup(w_o).T
        hn = rms(h, g2).reshape(T, D)
        logits = hn @ w_gate.T
        probs = jax.nn.softmax(logits, axis=-1)
        tv, ti = jax.lax.top_k(probs, TOPK)
        tv = tv / jnp.sum(tv, axis=-1, keepdims=True)
        rw = jnp.zeros((T, E), hn.dtype).at[jnp.arange(T)[:, None], ti].set(tv)
        moe = jnp.zeros((T, D), hn.dtype)
        for e in range(E):
            up = jax.nn.silu(hn @ qgroup(w1[e]).T) * (hn @ qgroup(w3[e]).T)
            moe = moe + rw[:, e:e + 1] * (up @ qgroup(w2[e]).T)
        return h + moe.reshape(B, S, D)
    h = _L0_tok_ref(x, L0_tok_W, L0_tok_b)
    h = h + _L0_attn_ref(_layernorm(h, axis=-1), L0_attn_Wq, L0_attn_bq, L0_attn_Wk, L0_attn_bk, L0_attn_Wv, L0_attn_bv, L0_attn_Wo, L0_attn_bo, L0_attn_relative_k, L0_attn_relative_v)
    h = h + _L0_ffn_ref(_layernorm(h, axis=-1), L0_ffn_router_w, L0_ffn_router_b, L0_ffn_routed_w1, L0_ffn_routed_w3, L0_ffn_routed_w2, L0_ffn_shared_w1, L0_ffn_shared_w3, L0_ffn_shared_w2)
    h = h + _L1_attn_ref(_layernorm(h, axis=-1), L1_attn_wq, L1_attn_wk, L1_attn_wv, L1_attn_wo)
    h = h + _L1_ffn_ref(_layernorm(h, axis=-1), L1_ffn_w_q, L1_ffn_w_k, L1_ffn_w_v, L1_ffn_w_o, L1_ffn_g1, L1_ffn_g2, L1_ffn_w_gate, L1_ffn_w1, L1_ffn_w3, L1_ffn_w2)
    return h

_drawn_inputs = setup_inputs


def setup_inputs(seed=0):
    import zlib

    import numpy as np

    out = dict(_drawn_inputs(seed))
    spreads = {'L0_attn_bq': (0.0, 0.1),
     'L0_attn_bk': (0.0, 0.8),
     'L0_attn_bv': (0.0, 0.1),
     'L0_attn_bo': (0.0, 0.1),
     'L0_ffn_router_b': (0.0, 0.557),
     'L1_ffn_g1': (1.0, 0.6),
     'L1_ffn_g2': (1.0, 0.6)}
    factors = {'L1_attn_wq': 3.696,
     'L1_attn_wk': 3.89,
     'L1_ffn_w_q': 8.0,
     'L1_ffn_w_k': 8.0,
     'L1_ffn_w_gate': 4.533,
     'L1_ffn_w1': 4.267,
     'L1_ffn_w3': 4.253,
     'L1_ffn_w2': 4.064}
    for name, (base, spread) in spreads.items():
        noise = np.random.default_rng([zlib.crc32(name.encode()), seed]).standard_normal(out[name].shape)
        drawn = base * np.exp(spread * noise) if base else spread * noise
        out[name] = jnp.asarray(drawn.astype(out[name].dtype))
    for name, factor in factors.items():
        out[name] = (out[name] * factor).astype(out[name].dtype)
    return out
```

```python
import numpy as np
import concourse.bass as bass
from concourse import mybir
from contextlib import ExitStack

F32 = mybir.dt.float32
F16 = mybir.dt.float16
I32 = mybir.dt.int32
U32 = mybir.dt.uint32
ALU = mybir.AluOpType
ACT = mybir.ActivationFunctionType
AX = mybir.AxisListType

P = 128
SEQ = 64
TOKENS = 64 * SEQ
TILES = TOKENS // P
U = 4
CHUNKS = TILES // U
CT = U * P
D = 256
KD = D // P
EPS = 1e-5
WS = 256.0
ROUND = 12582912.0
NEG = -1e30


class Stage:

    def __init__(self, core, name, per=U, base=0):
        self.sem, self.per, self.base = core.sem(name), per, base

    def value(self, c, k):
        return c * self.per + (self.base + k + 1)


class Loads:

    def __init__(self, core, name, slots=U, parts=1):
        self.parts = parts
        self.sems = [core.sem(f"{name}_{k}") for k in range(slots)]

    def value(self, c):
        return (c + 1) * (16 * self.parts)


class Banks:

    def __init__(self, core, jobs):
        self.core, self.at, self.uses = core, {}, [0] * 8
        for n, bank in jobs:
            assert n not in self.at, n
            self.at[n] = (bank, self.uses[bank])
            self.uses[bank] += 1
        self.base = list(core.bank_uses)

    def tile(self, job):
        return self.core.psum[self.at[job][0]]

    def full(self, job):
        return self.core.full[self.at[job][0]]

    def drained(self, job):
        return self.core.drained[self.at[job][0]]

    def n_full(self, c, job):
        b, k = self.at[job]
        return c * self.uses[b] + (self.base[b] + k + 1)

    def n_free(self, c, job):
        b, k = self.at[job]
        return c * self.uses[b] + (self.base[b] + k + 1)

    def n_out(self, c, job):
        return self.n_free(c, job) + 1

    def close(self, chunks):
        for b in range(8):
            self.core.bank_uses[b] += chunks * self.uses[b]


def ring(jobs, banks):
    return [(j, banks[i % len(banks)]) for i, j in enumerate(jobs)]


class Core:

    def __init__(self, nc, ctx):
        self.nc, self.ctx, self.of_phase = nc, ctx, []
        self.psum = [ctx.enter_context(nc.psum_tensor(f"bank{b}", [P, 512], F32)) for b in range(8)]
        self.full = [self.sem(f"bank{b}_full") for b in range(8)]
        self.drained = [self.sem(f"bank{b}_drained") for b in range(8)]
        self.sync_waits = self.sem("sync_waits_passed")
        self.vector_waits = self.sem("vector_waits_passed")
        self.tensor_waits = self.sem("tensor_waits_passed")
        self.of_phase = []
        self.bank_uses = [0] * 8
        self.ident = self.sb("ident", [P, P], F32)
        self.mhalf = self.sb("minus_half", [P, U], F32)
        self.eps = self.sb("eps", [P, U], F32)

    def sem(self, name):
        self.of_phase.append(self.nc.alloc_semaphore(name))
        return self.of_phase[-1]

    def end_phase(self):
        self.nc.clear_and_free_semaphores(self.of_phase)
        self.nc.all_engine_barrier()
        self.of_phase = []

    def sb(self, name, shape, dt):
        return self.ctx.enter_context(self.nc.sbuf_tensor(name, shape, dt))


def chunk_ends(core, phase, engines):
    return {n: core.sem(f"{phase}_{n}_chunks_ended") for n in engines}


class Norm:

    def __init__(self, core, phase, sb, per_xn=U):
        nc = core.nc
        self.core = core
        self.st = sb(f"{phase}_stats", [P, U, 6], F32)
        self.mv = sb(f"{phase}_mean_var", [P, U, 2], F32)
        self.ve = sb(f"{phase}_var_eps", [P, U], F32)
        self.rs = sb(f"{phase}_rstd", [P, U], F32)
        self.xn = sb(f"{phase}_xn", [P, U, D], F32)
        self.s_st = Stage(core, f"{phase}_stats_done")
        self.s_mv = Stage(core, f"{phase}_mean_var_done")
        self.s_ve = Stage(core, f"{phase}_var_eps_done", 1)
        self.s_rs = Stage(core, f"{phase}_rstd_done", 1)
        self.s_xn = Stage(core, f"{phase}_xn_done", per_xn)

    def vector(self, dve, c, rows):
        self.vector_stats(dve, c, rows)
        self.vector_rows(dve, c, rows)

    def vector_stats(self, dve, c, rows):
        nc = self.core.nc
        dve.sem_inc(self.core.vector_waits, 1)
        for u in range(U):
            nc.vector.bn_stats(self.st[:, u, :], rows(c, u)).then_inc(self.s_st.sem, 1)
        for u in range(U):
            dve.wait_ge(self.s_st.sem, self.s_st.value(c, u))
            dve.sem_inc(self.core.vector_waits, 1)
            nc.vector.bn_aggr(self.mv[:, u, :], self.st[:, u, :]).then_inc(self.s_mv.sem, 1)

    def vector_rows(self, dve, c, rows):
        nc = self.core.nc
        dve.wait_ge(self.s_rs.sem, self.s_rs.value(c, 0))
        for u in range(U):
            nc.vector.tensor_scalar(self.xn[:, u, :], rows(c, u), self.mv[:, u, 0:1], self.rs[:, u:u + 1],
                                    ALU.subtract, ALU.mult).then_inc(self.s_xn.sem, 1)

    def gpsimd(self, pool, c):
        nc = self.core.nc
        pool.wait_ge(self.s_mv.sem, self.s_mv.value(c, U - 1))
        nc.gpsimd.tensor_tensor(self.ve[:, :], self.mv[:, :, 1], self.core.eps[:, :], ALU.add).then_inc(self.s_ve.sem, 1)
        pool.wait_ge(self.s_ve.sem, self.s_ve.value(c, 0))
        nc.gpsimd.tensor_tensor(self.rs[:, :], self.ve[:, :], self.core.mhalf[:, :], ALU.pow).then_inc(self.s_rs.sem, 1)


class Transposed:

    def __init__(self, core, phase, sb, job="x"):
        self.core, self.job = core, job
        self.xh = sb(f"{phase}_xh", [P, KD, CT], F16)
        self.xl = sb(f"{phase}_xl", [P, KD, CT], F16)
        self.s_xh = Stage(core, f"{phase}_xh_done", KD)

    def tensor(self, pe, c, banks, xn, s_xn, bc=None):
        nc, bc = self.core.nc, c if bc is None else bc
        for kd in range(KD):
            pe.wait_ge(banks.drained((self.job, kd)), banks.n_free(bc, (self.job, kd)))
            for u in range(U):
                pe.wait_ge(s_xn.sem, s_xn.value(c, u))
                last = nc.tensor.transpose(banks.tile((self.job, kd))[:, u * P:(u + 1) * P],
                                           xn[:, u, kd * P:(kd + 1) * P], self.core.ident[:, :])
            last.then_inc(banks.full((self.job, kd)), 1)

    def scalar(self, act, c, banks, bc=None):
        bc = c if bc is None else bc
        for kd in range(KD):
            act.wait_ge(banks.full((self.job, kd)), banks.n_full(bc, (self.job, kd)))
            self.core.nc.scalar.activation(self.xh[:, kd, :], banks.tile((self.job, kd))[:, :], ACT.Copy)\
                .then_inc(self.s_xh.sem, 1)

    def vector(self, dve, c, banks, bc=None):
        for kd in range(KD):
            dve.wait_ge(self.s_xh.sem, self.s_xh.value(c, kd))
            self.core.nc.vector.tensor_tensor(self.xl[:, kd, :], banks.tile((self.job, kd))[:, :],
                                                            self.xh[:, kd, :], ALU.subtract)\
                .then_inc(banks.drained((self.job, kd)), 1)


def three(nc, out, a, b, start, stop):
    nc.tensor.matmul(out, a[0], b[0], start=start, stop=False)
    nc.tensor.matmul(out, a[0], b[1], start=False, stop=False)
    return nc.tensor.matmul(out, a[1], b[0], start=False, stop=stop)


def prepare(core, a):
    nc = core.nc
    Z = 13
    assert MTILES * MT % (Z * P) == 0
    with ExitStack() as ctx:
        idx = ctx.enter_context(nc.sbuf_tensor("token_ids", [P, TILES], I32))
        zero = ctx.enter_context(nc.sbuf_tensor("zero_rows", [P, Z * D], F32))
        loaded = core.sem("ids_loaded")
        gathered = core.sem("rows_gathered")
        filled = core.sem("constants_filled")
        zeroed = core.sem("zeros_filled")
        cleared = core.sem("expert_rows_cleared")
        with nc.Block() as block:
            @block.sync
            def _(sp):
                sp.dma_start(idx[:, :], a["x"]).then_inc(loaded, 16)
                sp.dma_start(core.ident[:, :], a["ident"]).then_inc(loaded, 16)
                sp.wait_ge(zeroed, 1)
                n = MTILES * MT // (Z * P)
                for i in range(n):
                    sp.dma_start(a["rows_in"][i * Z * P:(i + 1) * Z * P, :].rearrange("(p z) d -> p (z d)", z=Z), zero[:, :])\
                        .then_inc(cleared, 16)
                sp.wait_ge(cleared, 16 * n)

            @block.vector
            def _(dve):
                nc.vector.memset(zero[:, :], 0.0).then_inc(zeroed, 1)
                nc.vector.memset(core.h[:, TILES:TILES + U, :], 0.0)

            @block.gpsimd
            def _(pool):
                pool.memset(core.mhalf[:, :], -0.5).then_inc(filled, 1)
                pool.memset(core.eps[:, :], EPS).then_inc(filled, 1)
                pool.wait_ge(loaded, 32)
                for t in range(TILES):
                    pool.indirect_dma_start(out=core.h[:, t, :], out_offset=None, in_=a["L0_tok_W"],
                                            in_offset=bass.IndirectOffsetOnAxis(ap=idx[:, t:t + 1], axis=0))\
                        .then_inc(gathered, 16)
                pool.wait_ge(gathered, 16 * TILES)

            @block.tensor
            def _(pe):
                for b in range(8):
                    pe.sem_inc(core.drained[b], 1)
    core.end_phase()


def attn0(core, a):
    nc = core.nc
    H, DK = 16, 16
    HB = P // DK
    M = 2 * SEQ
    with ExitStack() as ctx:
        def sb(name, shape, dt):
            return ctx.enter_context(nc.sbuf_tensor(name, shape, dt))

        stage = sb("a0_stage", [P, 4, KD, D], F32)
        wh = sb("a0_wh", [P, 4, KD, D], F16)
        wl = sb("a0_wl", [P, 4, KD, D], F16)
        tokb = sb("a0_tokb", [P, D], F32)
        bv = sb("a0_bv", [P, D], F32)
        bo = sb("a0_bo", [P, D], F32)
        bqk = sb("a0_bqk", [P, 2, KD], F32)
        hmask = sb("a0_head_mask", [P, HB], F32)
        vmask = sb("a0_v_mask", [P, D], F32)
        relk = sb("a0_relk", [P, M], F32)
        rk = sb("a0_relk_diag", [P, M, HB], F32)
        rv = sb("a0_relv", [P, 2, 2 * DK], F32)
        nrm = Norm(core, "a0", sb)
        xt = Transposed(core, "a0", sb)
        q = sb("a0_q", [P, KD, CT], F32)
        k = sb("a0_k", [P, KD, CT], F32)
        kdg = sb("a0_k_diag", [P, 2 * U, KD, HB, SEQ], F32)
        v2 = sb("a0_v2", [P, 2 * U, D], F32)
        qr = sb("a0_qr", [P, U, M, H], F32)
        srel = sb("a0_srel", [P, U, SEQ, H], F32)
        s = sb("a0_s", [P, U, H, SEQ], F32)
        pp = qr
        mx = sb("a0_max", [P, U, H], F32)
        sm = sb("a0_sum", [P, U, H], F32)
        rc = sb("a0_rsum", [P, U, H], F32)
        at = sb("a0_at", [P, U, H // 2, P], F32)
        pt = kdg[:, :, :, :, :].rearrange("p b k h r -> p (b k h r)").rearrange("p (u h t) -> p u h t", u=U, h=H)
        oh = sb("a0_oh", [P, U, KD, P], F16)
        ol = sb("a0_ol", [P, U, KD, P], F16)

        jobs = ring([("x", kd) for kd in range(KD)] + [("q", i) for i in range(4)] + [("v", i) for i in range(U)]
                    + [("qr", u, i) for u in range(U) for i in range(4)]
                    + [("s", u, i) for u in range(U) for i in range(2)]
                    + [(n, v, i) for u in range(U + 1) for n, v, m in (("at", u, 2), ("pt", u, 4), ("o", u, 1), ("y", u - 1, 1))
                       if 0 <= v < U for i in range(m)], range(8))
        bk = Banks(core, jobs)
        ends = chunk_ends(core, "a0", ["pe", "act", "dve", "pool", "sp"])
        loaded = core.sem("a0_loaded")
        wh_done = core.sem("a0_wh_done")
        w_done = core.sem("a0_w_done")
        masks = core.sem("a0_rk_done")
        pz = core.sem("a0_zeros_filled")
        pzo = core.sem("a0_zeros_stored")
        s_hb = Stage(core, "a0_h_biased")
        s_vb = Stage(core, "a0_v_masked", 2 * U)
        s_kdd = Stage(core, "a0_k_diag_even_done", U)
        s_kdp = Stage(core, "a0_k_diag_odd_done", U)
        s_qo = Loads(core, "a0_qr_stored")
        s_sr = Loads(core, "a0_srel_loaded", U, 2)
        s_mx = Stage(core, "a0_max_done")
        s_sub = Stage(core, "a0_sub_done")
        s_ex = Stage(core, "a0_exp_done")
        s_sm = Stage(core, "a0_sum_done")
        s_rc = Stage(core, "a0_rsum_done")
        s_pr = Stage(core, "a0_probs_done")
        s_rh = Stage(core, "a0_probs_by_distance_done")
        s_po = Loads(core, "a0_probs_stored", U, 2)
        s_pp = Loads(core, "a0_skewed_loaded")
        s_oh = Stage(core, "a0_oh_done")
        s_hy = Stage(core, "a0_h_added")

        def row(c, u):
            return core.h[:, bass.ds(c * U + u, 1), :].rearrange("p a d -> p (a d)")

        def k_diag(eng, t):
            return eng.tensor_tensor(kdg[:, t, :, :, :],
                                     k[:, :, t * SEQ:(t + 1) * SEQ].unsqueeze(2).to_broadcast([P, KD, HB, SEQ]),
                                     hmask[:, :].unsqueeze(1).unsqueeze(3).to_broadcast([P, KD, HB, SEQ]), ALU.mult)

        def heads(x):
            return x.rearrange("p r h -> p h r")

        def copy_qr(copy, u, i):
            kd, m = i // 2, i % 2
            return copy(qr[:, u, m * SEQ:(m + 1) * SEQ, kd * HB:(kd + 1) * HB],
                        bk.tile(("qr", u, i))[:, :].rearrange("p (m h) -> p m h", h=HB))

        def total(dve, c, u):
            dve.wait_ge(s_ex.sem, s_ex.value(c, u))
            nc.vector.tensor_reduce(sm[:, u, :], s[:, u, :, :], AX.X, ALU.add).then_inc(s_sm.sem, 1)
            dve.wait_ge(s_sm.sem, s_sm.value(c, u))
            nc.vector.reciprocal(rc[:, u, :], sm[:, u, :]).then_inc(s_rc.sem, 1)

        def project(pe, c, u):
            pe.wait_ge(bk.drained(("o", u, 0)), bk.n_out(c, ("o", u, 0)))
            pe.wait_ge(bk.drained(("y", u, 0)), bk.n_free(c, ("y", u, 0)))
            for kd in range(KD):
                last = three(nc, bk.tile(("y", u, 0))[:, 0:D], (oh[:, u, kd, :], ol[:, u, kd, :]),
                             (wh[:, 3, kd, :], wl[:, 3, kd, :]), kd == 0, kd == KD - 1)
            last.then_inc(bk.full(("y", u, 0)), 1)

        def add_y(dve, c, u):
            dve.wait_ge(bk.full(("y", u, 0)), bk.n_full(c, ("y", u, 0)))
            nc.vector.scalar_tensor_tensor(row(c, u), bk.tile(("y", u, 0))[:, 0:D], 1 / WS, row(c, u),
                                                      ALU.mult, ALU.add)\
                .then_inc(bk.drained(("y", u, 0)), 1)
            dve.wait_ge(bk.drained(("y", u, 0)), bk.n_out(c, ("y", u, 0)))
            nc.vector.tensor_tensor(row(c, u), row(c, u), bo[:, :], ALU.add).then_inc(s_hy.sem, 1)

        with nc.Block() as block:
            @block.sync
            def _(sp):
                for i, w in enumerate(("L0_attn_Wq", "L0_attn_Wk", "L0_attn_Wv", "L0_attn_Wo")):
                    sp.dma_start(stage[:, i, :, :], a[w].rearrange("(k p) n -> p k n", p=P)).then_inc(loaded, 16)
                sp.dma_start(tokb[:, :], a["L0_tok_b"].partition_broadcast(P)).then_inc(loaded, 16)
                sp.dma_start(bv[:, :], a["L0_attn_bv"].partition_broadcast(P)).then_inc(loaded, 16)
                sp.dma_start(bo[:, :], a["L0_attn_bo"].partition_broadcast(P)).then_inc(loaded, 16)
                sp.dma_start(bqk[:, :, :], a["bqk"]).then_inc(loaded, 16)
                sp.dma_start(hmask[:, :], a["head_mask"]).then_inc(loaded, 16)
                sp.dma_start(vmask[:, :], a["v_mask"]).then_inc(loaded, 16)
                sp.dma_start(relk[:, :], a["relk"]).then_inc(loaded, 16)
                sp.dma_start(rv[:, :, :], a["relv"]).then_inc(loaded, 16)
                sp.wait_ge(pz, 1)
                for u in range(U):
                    sp.dma_start(a["skew"][u], qr[:, u, :, :].rearrange("p m h -> p (m h)")).then_inc(pzo, 16)
                sp.wait_ge(pzo, 16 * U)
                with sp.Fori(0, CHUNKS) as c:
                    for u in range(U):
                        tile = sp.snap(c * U + u)
                        for i in range(4):
                            sp.wait_ge(bk.drained(("qr", u, i)), bk.n_out(c, ("qr", u, i)))
                            sp.sem_inc(core.sync_waits, 1)
                        sp.dma_start(a["qr"][bass.ds(tile, 1)].rearrange("a p n -> (a p) n"),
                                     qr[:, u, :, :].rearrange("p m h -> p (m h)")).then_inc(s_qo.sems[u], 16)
                    for u in range(U):
                        starts = [sp.snap((c * U + u) * (P * M * H) + b * SEQ * M * H + (SEQ - 1) * H) for b in range(2)]
                        sp.wait_ge(s_qo.sems[u], s_qo.value(c))
                        sp.sem_inc(core.sync_waits, 1)
                        for b in range(2):
                            src = a["qr_flat"][bass.ds(starts[b], SEQ * (M * H - H))]
                            sp.dma_start(srel[b * SEQ:(b + 1) * SEQ, u, :, :].rearrange("p r h -> p (r h)"),
                                         src.rearrange("(l n) -> l n", n=M * H - H)[:, 0:SEQ * H])\
                                .then_inc(s_sr.sems[u], 16)
                    for u in range(U):
                        sp.wait_ge(s_rh.sem, s_rh.value(c, u))
                        sp.sem_inc(core.sync_waits, 1)
                        for b in range(2):
                            base = u * P * M * H + b * SEQ * M * H + (SEQ - 1) * H
                            dst = a["skew_flat"][base:base + SEQ * (M * H - H)]
                            sp.dma_start(dst.rearrange("(l n) -> l n", n=M * H - H)[:, 0:SEQ * H],
                                         srel[b * SEQ:(b + 1) * SEQ, u, :, :].rearrange("p r h -> p (r h)"))\
                                .then_inc(s_po.sems[u], 16)
                        sp.wait_ge(s_po.sems[u], s_po.value(c))
                        sp.sem_inc(core.sync_waits, 1)
                        sp.dma_start(pp[:, u, :, :].rearrange("p m h -> p (m h)"), a["skew"][u]).then_inc(s_pp.sems[u], 16)
                    for u in range(U):
                        sp.wait_ge(s_pp.sems[u], s_pp.value(c))
                        sp.sem_inc(core.sync_waits, 1)
                    sp.sem_inc(ends["sp"], 1)
                    for n in ends:
                        if n != "sp":
                            sp.wait_ge(ends[n], c + 1)
                            sp.sem_inc(core.sync_waits, 1)

            @block.gpsimd
            def _(pool):
                pool.memset(qr[:, :, :, :].rearrange("p u m h -> p (u m h)"), 0.0).then_inc(pz, 1)
                pool.wait_ge(loaded, 12 * 16)
                nc.gpsimd.tensor_tensor(rk[:, :, :], relk[:, :].unsqueeze(2).to_broadcast([P, M, HB]),
                                        hmask[:, :].unsqueeze(1).to_broadcast([P, M, HB]), ALU.mult).then_inc(masks, 1)
                pool.wait_ge(pzo, 16 * U)
                with pool.Fori(0, CHUNKS) as c:
                    nrm.gpsimd(pool, c)
                    for t in range(2 * U):
                        if t % 2 == 0:
                            pool.wait_ge(bk.drained(("v", t // 2)), bk.n_out(c, ("v", t // 2)))
                        nc.gpsimd.tensor_tensor(v2[:, t, :], v2[:, t, :], vmask[:, :], ALU.mult).then_inc(s_vb.sem, 1)
                    for t in range(2 * U):
                        if t == 0:
                            pool.wait_ge(bk.drained(("q", 2)), bk.n_out(c, ("q", 2)))
                            pool.wait_ge(bk.drained(("q", 3)), bk.n_out(c, ("q", 3)))
                        if t % 2:
                            k_diag(nc.gpsimd, t).then_inc(s_kdp.sem, 1)
                    for u in range(U):
                        pool.wait_ge(s_rc.sem, s_rc.value(c, u))
                        nc.gpsimd.tensor_tensor(s[:, u, :, :], s[:, u, :, :],
                                                rc[:, u, :].unsqueeze(2).to_broadcast([P, H, SEQ]), ALU.mult)\
                            .then_inc(s_pr.sem, 1)
                    pool.drain().then_inc(ends["pool"], 1)
                    for n in ends:
                        if n != "pool":
                            pool.wait_ge(ends[n], c + 1)

            @block.scalar
            def _(act):
                act.wait_ge(loaded, 12 * 16)
                flat = "p w k n -> p (w k n)"
                nc.scalar.activation(wh[:, :, :, :].rearrange(flat), stage[:, :, :, :].rearrange(flat), ACT.Copy,
                                     scale=WS).then_inc(wh_done, 1)
                with act.Fori(0, CHUNKS) as c:
                    xt.scalar(act, c, bk)
                    for i in range(4):
                        dst = (q, k)[i // KD]
                        act.wait_ge(bk.full(("q", i)), bk.n_full(c, ("q", i)))
                        nc.scalar.activation(dst[:, i % KD, :], bk.tile(("q", i))[:, :], ACT.Identity,
                                                        bias=bqk[:, i // KD, i % KD:i % KD + 1], scale=1 / WS)\
                            .then_inc(bk.drained(("q", i)), 1)
                    for u in range(U):
                        for i in (0, 2):
                            act.wait_ge(bk.full(("qr", u, i)), bk.n_full(c, ("qr", u, i)))
                            copy_qr(nc.scalar.copy, u, i).then_inc(bk.drained(("qr", u, i)), 1)
                    for u in range(U):
                        act.wait_ge(s_sub.sem, s_sub.value(c, u))
                        nc.scalar.activation(s[:, u, :, :], s[:, u, :, :], ACT.Exp).then_inc(s_ex.sem, 1)
                    for u in range(U):
                        act.wait_ge(s_pr.sem, s_pr.value(c, u))
                        nc.scalar.copy(heads(srel[:, u, :, :]), s[:, u, :, :]).then_inc(s_rh.sem, 1)
                    for u in range(U):
                        act.wait_ge(bk.full(("at", u, 0)), bk.n_full(c, ("at", u, 0)))
                        nc.scalar.copy(at[:, u, 0:4, :].rearrange("p h t -> p (h t)"),
                                                  bk.tile(("at", u, 0))[:, :])\
                            .then_inc(bk.drained(("at", u, 0)), 1)
                        for i in range(3):
                            act.wait_ge(bk.full(("pt", u, i)), bk.n_full(c, ("pt", u, i)))
                            nc.scalar.copy(pt[:, u, 4 * i:4 * i + 4, :].rearrange("p h t -> p (h t)"),
                                                      bk.tile(("pt", u, i))[:, :])\
                                .then_inc(bk.drained(("pt", u, i)), 1)
                        act.wait_ge(bk.full(("o", u, 0)), bk.n_full(c, ("o", u, 0)))
                        nc.scalar.copy(oh[:, u, :, :].rearrange("p k t -> p (k t)"), bk.tile(("o", u, 0))[:, 0:D])\
                            .then_inc(s_oh.sem, 1)
                    act.drain().then_inc(ends["act"], 1)
                    for n in ends:
                        if n != "act":
                            act.wait_ge(ends[n], c + 1)

            @block.vector
            def _(dve):
                dve.wait_ge(loaded, 12 * 16)
                dve.wait_ge(wh_done, 1)
                flat = "p w k n -> p (w k n)"
                nc.vector.scalar_tensor_tensor(wl[:, :, :, :].rearrange(flat), stage[:, :, :, :].rearrange(flat), WS,
                                               wh[:, :, :, :].rearrange(flat), ALU.mult, ALU.subtract).then_inc(w_done, 1)
                with dve.Fori(0, CHUNKS) as c:
                    for u in range(U):
                        nc.vector.tensor_tensor(row(c, u), row(c, u), tokb[:, :], ALU.add).then_inc(s_hb.sem, 1)
                    dve.wait_ge(s_hb.sem, s_hb.value(c, U - 1))
                    nrm.vector(dve, c, row)
                    xt.vector(dve, c, bk)
                    for i in range(U):
                        dve.wait_ge(bk.full(("v", i)), bk.n_full(c, ("v", i)))
                        nc.vector.scalar_tensor_tensor(
                            v2[:, 2 * i:2 * i + 2, :], bk.tile(("v", i))[:, :].rearrange("p (b n) -> p b n", b=2), 1 / WS,
                            bv[:, :].unsqueeze(1).to_broadcast([P, 2, D]), ALU.mult, ALU.add)\
                            .then_inc(bk.drained(("v", i)), 1)
                    dve.wait_ge(bk.drained(("q", 2)), bk.n_out(c, ("q", 2)))
                    dve.wait_ge(bk.drained(("q", 3)), bk.n_out(c, ("q", 3)))
                    for t in range(0, 2 * U, 2):
                        k_diag(nc.vector, t).then_inc(s_kdd.sem, 1)
                    for u in range(U):
                        for i in (1, 3):
                            dve.wait_ge(bk.full(("qr", u, i)), bk.n_full(c, ("qr", u, i)))
                            copy_qr(nc.vector.tensor_copy, u, i).then_inc(bk.drained(("qr", u, i)), 1)
                    for u in range(U):
                        dve.wait_ge(s_sr.sems[u], s_sr.value(c))
                        for i in range(KD):
                            dve.wait_ge(bk.full(("s", u, i)), bk.n_full(c, ("s", u, i)))
                            hs = slice(i * HB, (i + 1) * HB)
                            nc.vector.scalar_tensor_tensor(
                                s[:, u, hs, :], bk.tile(("s", u, i))[:, :].rearrange("p (h r) -> p h r", h=HB),
                                DK ** -0.5, heads(srel[:, u, :, hs]), ALU.mult, ALU.add)\
                                .then_inc(bk.drained(("s", u, i)), 1)
                        for i in range(KD):
                            dve.wait_ge(bk.drained(("s", u, i)), bk.n_out(c, ("s", u, i)))
                        nc.vector.tensor_reduce(mx[:, u, :], s[:, u, :, :], AX.X, ALU.max).then_inc(s_mx.sem, 1)
                        dve.wait_ge(s_mx.sem, s_mx.value(c, u))
                        nc.vector.tensor_tensor(s[:, u, :, :], s[:, u, :, :],
                                                mx[:, u, :].unsqueeze(2).to_broadcast([P, H, SEQ]), ALU.subtract)\
                            .then_inc(s_sub.sem, 1)
                        if u:
                            total(dve, c, u - 1)
                    total(dve, c, U - 1)
                    for u in range(U):
                        dve.wait_ge(bk.full(("at", u, 1)), bk.n_full(c, ("at", u, 1)))
                        nc.vector.tensor_copy(at[:, u, 4:8, :].rearrange("p h t -> p (h t)"),
                                                         bk.tile(("at", u, 1))[:, :])\
                            .then_inc(bk.drained(("at", u, 1)), 1)
                        dve.wait_ge(bk.full(("pt", u, 3)), bk.n_full(c, ("pt", u, 3)))
                        nc.vector.tensor_copy(pt[:, u, 12:16, :].rearrange("p h t -> p (h t)"),
                                                         bk.tile(("pt", u, 3))[:, :])\
                            .then_inc(bk.drained(("pt", u, 3)), 1)
                        if u:
                            add_y(dve, c, u - 1)
                        dve.wait_ge(s_oh.sem, s_oh.value(c, u))
                        nc.vector.tensor_tensor(ol[:, u, :, :].rearrange("p k t -> p (k t)"),
                                                           bk.tile(("o", u, 0))[:, 0:D],
                                                           oh[:, u, :, :].rearrange("p k t -> p (k t)"), ALU.subtract)\
                            .then_inc(bk.drained(("o", u, 0)), 1)
                    add_y(dve, c, U - 1)
                    dve.drain().then_inc(ends["dve"], 1)
                    for n in ends:
                        if n != "dve":
                            dve.wait_ge(ends[n], c + 1)

            @block.tensor
            def _(pe):
                pe.wait_ge(w_done, 1)
                pe.wait_ge(masks, 1)
                with pe.Fori(0, CHUNKS) as c:
                    xt.tensor(pe, c, bk, nrm.xn, nrm.s_xn)
                    for kd in range(KD):
                        pe.wait_ge(bk.drained(("x", kd)), bk.n_out(c, ("x", kd)))
                    for i in range(4):
                        w, o = i // KD, i % KD
                        pe.wait_ge(bk.drained(("q", i)), bk.n_free(c, ("q", i)))
                        for kd in range(KD):
                            last = three(nc, bk.tile(("q", i))[:, :],
                                         (wh[:, w, kd, o * P:(o + 1) * P], wl[:, w, kd, o * P:(o + 1) * P]),
                                         (xt.xh[:, kd, :], xt.xl[:, kd, :]), kd == 0, kd == KD - 1)
                        last.then_inc(bk.full(("q", i)), 1)
                    for i in range(U):
                        pe.wait_ge(bk.drained(("v", i)), bk.n_free(c, ("v", i)))
                        for b in range(2):
                            t = 2 * i + b
                            for e in range(2):
                                for kd in range(KD):
                                    x2 = [x[:, kd, t * SEQ:(t + 1) * SEQ] for x in (xt.xh, xt.xl)]
                                    last = three(nc, bk.tile(("v", i))[e * SEQ:(e + 1) * SEQ, b * D:(b + 1) * D], x2,
                                                 (wh[:, 2, kd, :], wl[:, 2, kd, :]), kd == 0, kd == KD - 1)
                        last.then_inc(bk.full(("v", i)), 1)
                    for kd in range(KD):
                        pe.wait_ge(bk.drained(("q", kd)), bk.n_out(c, ("q", kd)))
                    for u in range(U):
                        for i in range(4):
                            kd, m = i // 2, i % 2
                            pe.wait_ge(bk.drained(("qr", u, i)), bk.n_free(c, ("qr", u, i)))
                            nc.tensor.matmul(bk.tile(("qr", u, i))[:, :], q[:, kd, u * P:(u + 1) * P],
                                                       rk[:, m * SEQ:(m + 1) * SEQ, :].rearrange("p m h -> p (m h)"),
                                                       start=True, stop=True)\
                                .then_inc(bk.full(("qr", u, i)), 1)
                    for u in range(U):
                        pe.wait_ge(s_kdd.sem, s_kdd.value(c, u))
                        pe.wait_ge(s_kdp.sem, s_kdp.value(c, u))
                        for i in range(KD):
                            pe.wait_ge(bk.drained(("s", u, i)), bk.n_free(c, ("s", u, i)))
                            for b in range(2):
                                t = 2 * u + b
                                last = nc.tensor.matmul(bk.tile(("s", u, i))[b * SEQ:(b + 1) * SEQ, :],
                                                        q[:, i, t * SEQ:(t + 1) * SEQ],
                                                        kdg[:, t, i, :, :].rearrange("p h r -> p (h r)"),
                                                        start=True, stop=True)
                            last.then_inc(bk.full(("s", u, i)), 1)
                    for u in range(U):
                        pe.wait_ge(s_pr.sem, s_pr.value(c, u))
                        for i in range(2):
                            pe.wait_ge(bk.drained(("at", u, i)), bk.n_free(c, ("at", u, i)))
                            for j in range(4):
                                hh = 2 * (4 * i + j)
                                last = nc.tensor.transpose(bk.tile(("at", u, i))[:, j * P:(j + 1) * P],
                                                           s[:, u, hh:hh + 2, :].rearrange("p h r -> p (h r)"), core.ident[:, :])
                            last.then_inc(bk.full(("at", u, i)), 1)
                        pe.wait_ge(s_pp.sems[u], s_pp.value(c))
                        for i in range(4):
                            pe.wait_ge(bk.drained(("pt", u, i)), bk.n_free(c, ("pt", u, i)))
                            for j in range(4):
                                last = nc.tensor.transpose(bk.tile(("pt", u, i))[:, j * P:(j + 1) * P],
                                                           pp[:, u, :, 4 * i + j], core.ident[:, :])
                            last.then_inc(bk.full(("pt", u, i)), 1)
                        for i in range(2):
                            pe.wait_ge(bk.drained(("at", u, i)), bk.n_out(c, ("at", u, i)))
                        for i in range(4):
                            pe.wait_ge(bk.drained(("pt", u, i)), bk.n_out(c, ("pt", u, i)))
                        pe.wait_ge(s_vb.sem, s_vb.value(c, 2 * u + 1))
                        pe.wait_ge(bk.drained(("o", u, 0)), bk.n_free(c, ("o", u, 0)))
                        for j in range(H // 2):
                            g, kd = j % 4, j // 4
                            out = bk.tile(("o", u, 0))[32 * g:32 * g + 32, kd * P:(kd + 1) * P]
                            for e in range(2):
                                nc.tensor.matmul(out, rv[:, e, :], pt[:, u, 2 * j + e, :], start=(e == 0), stop=False,
                                                 tile_position=(0, 32 * g))
                            for b in range(2):
                                last = nc.tensor.matmul(out[:, b * SEQ:(b + 1) * SEQ], v2[:, 2 * u + b, 32 * j:32 * j + 32],
                                                        at[:, u, j, b * SEQ:(b + 1) * SEQ], start=False, stop=(b == 1),
                                                        tile_position=(0, 32 * g))
                        last.then_inc(bk.full(("o", u, 0)), 1)
                        if u:
                            project(pe, c, u - 1)
                    project(pe, c, U - 1)
                    pe.drain().then_inc(ends["pe"], 1)
                    for n in ends:
                        if n != "pe":
                            pe.wait_ge(ends[n], c + 1)
        bk.close(CHUNKS)
    core.end_phase()


QMAX = 15.0


class Quant:

    def __init__(self, core, name, sb, groups, parts=1):
        self.core, self.name, self.G = core, name, groups
        self.mx = sb(f"{name}_max", [P, groups], F32)
        self.mn = sb(f"{name}_min", [P, groups], F32)
        self.s = sb(f"{name}_scale", [P, groups], F32)
        self.inv = sb(f"{name}_inv_scale", [P, groups], F32)
        self.base = sb(f"{name}_base", [P, groups], F32)
        self.shift = sb(f"{name}_base_less_round", [P, groups], F32)
        self.parts = parts
        self.s_red = Stage(core, f"{name}_extremes", 2 * parts)
        self.s_small = Stage(core, f"{name}_scales", 8)
        self.s_w1 = Stage(core, f"{name}_rounded", groups)
        self.s_w2 = Stage(core, f"{name}_shifted", groups)
        self.s_w3 = Stage(core, f"{name}_quantised", groups)

    def extremes(self, dve, c, x, part):
        v, n = self.core.nc.vector, self.G // self.parts
        gs = slice(part * n, (part + 1) * n)
        v.tensor_reduce(self.mx[:, gs], x[:, gs, :], AX.X, ALU.max).then_inc(self.s_red.sem, 1)
        v.tensor_reduce(self.mn[:, gs], x[:, gs, :], AX.X, ALU.min).then_inc(self.s_red.sem, 1)

    def scales(self, dve, c):
        v = self.core.nc.vector
        mx, mn, s, inv, base, shift = (t[:, :] for t in (self.mx, self.mn, self.s, self.inv, self.base, self.shift))
        dve.wait_ge(self.s_red.sem, self.s_red.value(c, 2 * self.parts - 1))
        v.tensor_tensor(s, mx, mn, ALU.subtract).then_inc(self.s_small.sem, 1)
        dve.wait_ge(self.s_small.sem, self.s_small.value(c, 0))
        v.tensor_scalar(s, s, 1e-5, 1 / QMAX, ALU.max, ALU.mult).then_inc(self.s_small.sem, 1)
        dve.wait_ge(self.s_small.sem, self.s_small.value(c, 1))
        v.reciprocal(inv, s).then_inc(self.s_small.sem, 1)
        dve.wait_ge(self.s_small.sem, self.s_small.value(c, 2))
        v.tensor_tensor(base, mn, inv, ALU.mult).then_inc(self.s_small.sem, 1)
        dve.wait_ge(self.s_small.sem, self.s_small.value(c, 3))
        v.tensor_scalar(base, base, -1.0, ROUND, ALU.mult, ALU.add).then_inc(self.s_small.sem, 1)
        dve.wait_ge(self.s_small.sem, self.s_small.value(c, 4))
        v.tensor_scalar(base, base, ROUND, 0.0, ALU.subtract, ALU.max).then_inc(self.s_small.sem, 1)
        dve.wait_ge(self.s_small.sem, self.s_small.value(c, 5))
        v.tensor_scalar(base, base, QMAX, None, ALU.min).then_inc(self.s_small.sem, 1)
        dve.wait_ge(self.s_small.sem, self.s_small.value(c, 6))
        v.tensor_scalar(shift, base, ROUND, None, ALU.subtract).then_inc(self.s_small.sem, 1)

    def rounded(self, dve, c, x):
        dve.wait_ge(self.s_small.sem, self.s_small.value(c, 7))
        for g in range(self.G):
            self.core.nc.vector.tensor_scalar(x[:, g, :], x[:, g, :], self.inv[:, g:g + 1], ROUND, ALU.mult, ALU.add)\
                .then_inc(self.s_w1.sem, 1)

    def digits(self, dve, c, x, groups):
        v = self.core.nc.vector
        for g in groups:
            dve.wait_ge(self.s_w1.sem, self.s_w1.value(c, g))
            v.tensor_scalar(x[:, g, :], x[:, g, :], self.shift[:, g:g + 1], 0.0, ALU.add, ALU.max).then_inc(self.s_w2.sem, 1)
        for g in groups:
            dve.wait_ge(self.s_w2.sem, self.s_w2.value(c, g))
            v.tensor_scalar(x[:, g, :], x[:, g, :], QMAX, self.base[:, g:g + 1], ALU.min, ALU.subtract)\
                .then_inc(self.s_w3.sem, 1)

    def vector(self, dve, c, x):
        for part in range(self.parts):
            self.extremes(dve, c, x, part)
        self.scales(dve, c)
        self.rounded(dve, c, x)
        self.digits(dve, c, x, range(self.G))


FFN = 896
FB = FFN // P
E1 = 8
W13 = 2 * KD * FFN
WX = W13 + FB * D
MT = 256
MTILES = 2 * TOKENS // MT + E1 - 1


class ExpertWeights:

    G = 6 * FB
    PART = 2 * FB

    def __init__(self, core, sb, bank):
        self.core = core
        self.st = sb("ew_stage", [P, self.G, P], F32)
        self.wt = sb("ew_turned", [P, 2, WX], F16)
        self.magic = sb("ew_round", [P, 1], F32)
        self.qn = Quant(core, "ew", sb, self.G, parts=6)
        self.moves = []
        for w in range(2):
            for kd in range(KD):
                for f0, n in ((0, 4), (4, 3)):
                    self.moves.append(((w * KD + kd) * FFN + f0 * P, [(w * FB + f0 + i) * KD + kd for i in range(n)]))
        for f0 in range(0, FB, 2):
            fs = range(f0, min(f0 + 2, FB))
            self.moves.append((W13 + f0 * D, [4 * FB + db * FB + f for f in fs for db in range(KD)]))
        self.jobs = [(("m", i), bank) for i in range(len(self.moves))]
        self.s_in = Loads(core, "ew_loaded", 1, 4)
        self.s_sc = Stage(core, "ew_scaled", self.G)
        self.s_hi = Stage(core, "ew_high_done", len(self.moves))
        self.s_out = core.sem("ew_stored")

    def groups(self, part):
        return range(part * self.PART, (part + 1) * self.PART)

    def load(self, sp, c, bk, a):
        e = sp.snap(c)
        last = ("m", len(self.moves) - 1)
        sp.wait_ge(bk.full(last), bk.n_full(c - 1, last))
        sp.sem_inc(self.core.sync_waits, 1)
        for i, n in enumerate(("w1", "w3")):
            sp.dma_start(self.st[:, i * 2 * FB:(i + 1) * 2 * FB, :].rearrange("p (f k) n -> p f (k n)", f=FB),
                         a["L1_ffn_" + n][bass.ds(e, 1)].rearrange("a (f p) n -> p (a f) n", p=P))\
                .then_inc(self.s_in.sems[0], 16)
        for db in range(KD):
            sp.dma_start(self.st[:, (4 + db) * FB:(5 + db) * FB, :].rearrange("p f n -> p (f n)"),
                         a["L1_ffn_w2"][bass.ds(e, 1), db * P:(db + 1) * P, :].rearrange("a p n -> (a p) n"))\
                .then_inc(self.s_in.sems[0], 16)

    def store(self, sp, c, bk, a):
        e = sp.snap(c)
        last = ("m", len(self.moves) - 1)
        sp.wait_ge(bk.drained(last), bk.n_out(c, last))
        sp.sem_inc(self.core.sync_waits, 1)
        sp.dma_start(a["wx"][bass.ds(e, 1)].rearrange("a p n -> (a p) n"),
                     self.wt[:, :, :].rearrange("p s n -> p (s n)")).then_inc(self.s_out, 16)

    def rounded(self, act, c, part):
        act.wait_ge(self.qn.s_small.sem, self.qn.s_small.value(c, 7))
        for g in self.groups(part):
            self.core.nc.scalar.activation(self.st[:, g, :], self.st[:, g, :], ACT.Identity, bias=self.magic[:, :],
                                           scale=self.qn.inv[:, g:g + 1]).then_inc(self.qn.s_w1.sem, 1)

    def scaled(self, act, c, part):
        for g in self.groups(part):
            act.wait_ge(self.qn.s_w3.sem, self.qn.s_w3.value(c, g))
            self.core.nc.scalar.activation(self.st[:, g, :], self.st[:, g, :], ACT.Copy, scale=self.qn.s[:, g:g + 1])\
                .then_inc(self.s_sc.sem, 1)

    def turn(self, pe, c, bk, i):
        gs = self.moves[i][1]
        pe.wait_ge(bk.drained(("m", i)), bk.n_free(c, ("m", i)))
        pe.wait_ge(self.s_sc.sem, self.s_sc.value(c, max(gs)))
        for j, g in enumerate(gs):
            last = self.core.nc.tensor.transpose(bk.tile(("m", i))[:, j * P:(j + 1) * P], self.st[:, g, :],
                                                 self.core.ident[:, :])
        last.then_inc(bk.full(("m", i)), 1)

    def high(self, act, c, bk, i):
        at, gs = self.moves[i]
        if i == 0:
            act.wait_ge(self.s_out, c * 16 + 1)
        act.wait_ge(bk.full(("m", i)), bk.n_full(c, ("m", i)))
        self.core.nc.scalar.activation(self.wt[:, 0, at:at + len(gs) * P], bk.tile(("m", i))[:, 0:len(gs) * P],
                                       ACT.Copy, scale=WS).then_inc(self.s_hi.sem, 1)

    def low(self, dve, c, bk, i):
        at, gs = self.moves[i]
        cols = slice(at, at + len(gs) * P)
        dve.wait_ge(self.s_hi.sem, self.s_hi.value(c, i))
        self.core.nc.vector.scalar_tensor_tensor(self.wt[:, 1, cols], bk.tile(("m", i))[:, 0:len(gs) * P], WS,
                                                 self.wt[:, 0, cols], ALU.mult, ALU.subtract)\
            .then_inc(bk.drained(("m", i)), 1)


GS = 64.0


class TopTwo:

    def __init__(self, core, phase, sb):
        self.core = core
        self.lg = sb(f"{phase}_logits", [P, U, 16], F32)
        self.top = sb(f"{phase}_top8", [P, U, 8], F32)
        self.want = sb(f"{phase}_two_values", [P, U, 8], F32)
        self.rest = sb(f"{phase}_replaced", [P, U, 16], F32)
        self.ex = sb(f"{phase}_gate_exp", [P, U, 8], F32)
        self.gates = sb(f"{phase}_gates", [P, U, 8], F32)
        self.mask = sb(f"{phase}_two_mask", [P, U, 8], F32)
        self.sm = sb(f"{phase}_gate_sum", [P, U], F32)
        self.rc = sb(f"{phase}_gate_rsum", [P, U], F32)
        self.s_top = Stage(core, f"{phase}_top8_done")
        self.s_want = Stage(core, f"{phase}_two_values_done", 1)
        self.s_rest = Stage(core, f"{phase}_replaced_done")
        self.s_sub = Stage(core, f"{phase}_logits_minus_max", 1)
        self.s_ex = Stage(core, f"{phase}_gate_exp_done", 1)
        self.s_sel = Stage(core, f"{phase}_two_selected", 2)
        self.s_sm = Stage(core, f"{phase}_gate_sum_done", 2)
        self.s_g = Stage(core, f"{phase}_gates_done", 1)

    def prepare(self, dve):
        self.core.nc.vector.memset(self.want[:, :, :], 3e38)
        self.core.nc.vector.memset(self.lg[:, :, 8:16], 3e38)

    def wide(self, x):
        return x.unsqueeze(2).to_broadcast([P, U, 8])

    def vector(self, dve, c, bank, bias, banks, job):
        nc = self.core.nc
        lg = self.lg[:, :, 0:8]
        ps = bank[:, 0:8 * U].rearrange("p (u e) -> p u e", u=U)
        dve.wait_ge(banks.full(job), banks.n_full(c, job))
        if bias is None:
            nc.vector.tensor_scalar(lg, ps, 1 / WS, None, ALU.mult).then_inc(banks.drained(job), 1)
        else:
            nc.vector.scalar_tensor_tensor(lg, ps, 1 / WS, bias, ALU.mult, ALU.add).then_inc(banks.drained(job), 1)
        dve.wait_ge(banks.drained(job), banks.n_out(c, job))
        dve.sem_inc(self.core.vector_waits, 1)
        for u in range(U):
            nc.vector.max(self.top[:, u, :], self.lg[:, u, 0:8]).then_inc(self.s_top.sem, 1)
        dve.wait_ge(self.s_top.sem, self.s_top.value(c, U - 1))
        nc.vector.tensor_copy(self.want[:, :, 0:2], self.top[:, :, 0:2]).then_inc(self.s_want.sem, 1)
        nc.vector.tensor_tensor(self.ex[:, :, :], lg, self.top[:, :, 0:1].to_broadcast([P, U, 8]), ALU.subtract)\
            .then_inc(self.s_sub.sem, 1)
        dve.wait_ge(self.s_want.sem, self.s_want.value(c, 0))
        dve.sem_inc(self.core.vector_waits, 1)
        for u in range(U):
            nc.vector.match_replace(self.rest[:, u, :], self.want[:, u, :], self.lg[:, u, :], NEG)\
                .then_inc(self.s_rest.sem, 1)
        dve.wait_ge(self.s_rest.sem, self.s_rest.value(c, U - 1))
        nc.vector.tensor_tensor(self.mask[:, :, :], self.rest[:, :, 0:8], lg, ALU.not_equal).then_inc(self.s_sel.sem, 1)
        dve.wait_ge(self.s_sel.sem, self.s_sel.value(c, 0))
        dve.wait_ge(self.s_ex.sem, self.s_ex.value(c, 0))
        nc.vector.tensor_tensor(self.gates[:, :, :], self.mask[:, :, :], self.ex[:, :, :], ALU.mult)\
            .then_inc(self.s_sel.sem, 1)
        dve.wait_ge(self.s_sel.sem, self.s_sel.value(c, 1))
        nc.vector.tensor_reduce(self.sm[:, :], self.gates[:, :, :], AX.X, ALU.add).then_inc(self.s_sm.sem, 1)
        dve.wait_ge(self.s_sm.sem, self.s_sm.value(c, 0))
        nc.vector.reciprocal(self.rc[:, :], self.sm[:, :]).then_inc(self.s_sm.sem, 1)
        dve.wait_ge(self.s_sm.sem, self.s_sm.value(c, 1))
        nc.vector.tensor_tensor(self.gates[:, :, :], self.gates[:, :, :], self.wide(self.rc[:, :]), ALU.mult)\
            .then_inc(self.s_g.sem, 1)

    def scalar(self, act, c):
        act.wait_ge(self.s_sub.sem, self.s_sub.value(c, 0))
        self.core.nc.scalar.activation(self.ex[:, :, :], self.ex[:, :, :], ACT.Exp).then_inc(self.s_ex.sem, 1)


def ffn0(core, a):
    nc = core.nc
    E, R, HD = 10, 8, 128
    SL = 5
    AHEAD = 2
    with ExitStack() as ctx:
        def sb(name, shape, dt):
            return ctx.enter_context(nc.sbuf_tensor(name, shape, dt))

        st13 = sb("f0_stage13", [P, 2, E, KD, HD], F32)
        st2 = sb("f0_stage2", [P, E, D], F32)
        w13h = sb("f0_w13h", [P, 2, E, KD, HD], F16)
        w13l = sb("f0_w13l", [P, 2, E, KD, HD], F16)
        w2h = sb("f0_w2h", [P, E, D], F16)
        w2l = sb("f0_w2l", [P, E, D], F16)
        str_ = sb("f0_stage_router", [P, KD, R], F32)
        rwh = sb("f0_rwh", [P, KD, R], F16)
        rwl = sb("f0_rwl", [P, KD, R], F16)
        rb = sb("f0_router_b", [P, R], F32)
        sel = sb("f0_expert_rows", [2 * R, R, P], F16)
        identh = sb("f0_ident16", [P, P], F16)
        nrm = Norm(core, "f0", sb)
        xt = Transposed(core, "f0", sb)
        top = TopTwo(core, "f0", sb)
        g2 = sb("f0_gates_split", [P, U, 2 * R], F16)
        gs = sb("f0_gates_scaled", [P, U, R], F32)
        gt = sb("f0_gates_t", [2 * R, CT], F16)
        sil = sb("f0_silu", [P, SL, CT], F32)
        uu = sb("f0_u", [P, SL, CT], F32)
        uh = sb("f0_uh", [P, SL, CT], F16)
        ul = sb("f0_ul", [P, SL, CT], F16)
        ew = ExpertWeights(core, sb, 5)

        order = [("g",), ("p1", 0), ("p3", 0), ("p1", 1), ("p3", 1), ("gt",), ("gb", 0), ("gb", 1)]
        for e in range(AHEAD, E):
            order += [("p1", e), ("p3", e)] + ([("gb", e)] if e < R else [])
        order += [("x", 0), ("x", 1)]
        jobs = ring(order, range(5))
        bk0 = Banks(core, jobs[-2:])
        bk0.close(1)
        bk = Banks(core, jobs + [(("y", 0), 6), (("y", 1), 7)] + ew.jobs)
        turns = {(4, 0): 0, (4, 1): 1, (4, 2): 2, (5, 0): 3, (5, 1): 4, (5, 2): 5, (6, 0): 6, (6, 1): 7,
                 (6, 2): 8, (7, 0): 9, (7, 1): 10, (7, 2): 11}
        loaded = core.sem("f0_loaded")
        magic = core.sem("f0_round_constant_filled")
        act_waits = core.sem("f0_scalar_waits_passed")
        wh_done = core.sem("f0_wh_done")
        w_done = core.sem("f0_w_done")
        s_gs = Stage(core, "f0_gates_scaled_done", 1)
        s_gh = Stage(core, "f0_gates_high_done", 1)
        s_gl = Stage(core, "f0_gates_low_done", 1)
        s_uh = Stage(core, "f0_uh_done", E)
        s_ul = Stage(core, "f0_ul_done", E, base=E)
        s_ye = Stage(core, "f0_down_done", E - 1, base=E - 1)

        def row(c, u):
            return core.h[:, bass.ds(c * U + u, 1), :].rearrange("p a d -> p (a d)")

        def before(c, e):
            return (c, e - SL) if e >= SL else (c - 1, e + SL)

        def flat(x):
            return x.rearrange("p w e k n -> p (w e k n)")

        def flat3(x):
            return x.rearrange("p e n -> p (e n)")

        with nc.Block() as block:
            @block.sync
            def _(sp):
                for i, n in enumerate(("w1", "w3")):
                    sp.dma_start(st13[:, i, 0:R, :, :], a["L0_ffn_routed_" + n].rearrange("e (k p) n -> p e k n", p=P))\
                        .then_inc(loaded, 16)
                    sp.dma_start(st13[:, i, R:E, :, :], a["L0_ffn_shared_" + n].rearrange("e (k p) n -> p e k n", p=P))\
                        .then_inc(loaded, 16)
                sp.dma_start(st2[:, 0:R, :], a["L0_ffn_routed_w2"].rearrange("e p n -> p e n")).then_inc(loaded, 16)
                sp.dma_start(st2[:, R:E, :], a["L0_ffn_shared_w2"].rearrange("e p n -> p e n")).then_inc(loaded, 16)
                sp.dma_start(str_[:, :, :], a["L0_ffn_router_w"].rearrange("(k p) n -> p k n", p=P)).then_inc(loaded, 16)
                sp.dma_start(rb[:, :], a["L0_ffn_router_b"].partition_broadcast(P)).then_inc(loaded, 16)
                sp.dma_start(sel[:, :, :], a["expert_rows"]).then_inc(loaded, 16)
                sp.dma_start(identh[:, :], a["ident16"]).then_inc(loaded, 16)

                sp.sem_inc(ew.s_out, 1)
                with sp.Fori(0, CHUNKS) as c:
                    ew.load(sp, c, bk, a)
                    ew.store(sp, c, bk, a)
                sp.wait_ge(ew.s_out, CHUNKS * 16 + 1)

            @block.gpsimd
            def _(pool):
                pool.sem_inc(s_ul.sem, E)
                nrm.gpsimd(pool, 0)
                with pool.Fori(0, CHUNKS) as c:
                    for e in range(E):
                        if e == 6:
                            nrm.gpsimd(pool, c + 1)
                        pool.wait_ge(s_uh.sem, s_uh.value(c, e))
                        nc.gpsimd.tensor_tensor(ul[:, e % SL, :], uu[:, e % SL, :], uh[:, e % SL, :], ALU.subtract)\
                            .then_inc(s_ul.sem, 1)

            @block.scalar
            def _(act):
                act.wait_ge(loaded, 10 * 16)
                nc.scalar.activation(rwh[:, :, :], str_[:, :, :], ACT.Copy, scale=WS).then_inc(wh_done, 1)
                nc.scalar.activation(flat(w13h[:, :, :, :, :]), flat(st13[:, :, :, :, :]), ACT.Copy, scale=WS).then_inc(wh_done, 1)
                nc.scalar.activation(flat3(w2h[:, :, :]), flat3(st2[:, :, :]), ACT.Copy, scale=WS).then_inc(wh_done, 1)
                xt.scalar(act, 0, bk0)
                act.wait_ge(magic, 1)
                with act.Fori(0, CHUNKS) as c:
                    top.scalar(act, c)
                    act.wait_ge(s_gs.sem, s_gs.value(c, 0))
                    nc.scalar.activation(g2[:, :, 0:R], gs[:, :, :], ACT.Copy).then_inc(s_gh.sem, 1)
                    for e in range(E):
                        for (step, place), i in turns.items():
                            if step + AHEAD == e and place == 0:
                                ew.high(act, c, bk, i)
                        pc, p = before(c, e)
                        act.wait_ge(bk.drained(("p3", p)), bk.n_out(pc, ("p3", p)))
                        act.sem_inc(act_waits, 1)
                        act.wait_ge(bk.full(("p1", e)), bk.n_full(c, ("p1", e)))
                        nc.scalar.activation(sil[:, e % SL, :], bk.tile(("p1", e))[:, :], ACT.Silu, scale=1 / WS)\
                            .then_inc(bk.drained(("p1", e)), 1)
                        if e == 0:
                            act.wait_ge(bk.full(("gt",)), bk.n_full(c, ("gt",)))
                            nc.scalar.activation(gt[:, :], bk.tile(("gt",))[:, :].bitcast(F16)[0:2 * R, 0:CT], ACT.Copy)\
                                .then_inc(bk.drained(("gt",)), 1)
                        if 3 <= e <= 5:
                            ew.rounded(act, c, e - 3)
                        made = ("gb", e) if e < R else ("p3", e)
                        act.wait_ge(bk.drained(made), bk.n_out(c, made))
                        act.sem_inc(act_waits, 1)
                        if p == E - 1:
                            act.wait_ge(bk.full(("y", 1)), bk.n_full(pc, ("y", 1)))
                        else:
                            act.wait_ge(s_ye.sem, s_ye.value(pc, p))
                        nc.scalar.copy(uh[:, e % SL, :], uu[:, e % SL, :]).then_inc(s_uh.sem, 1)
                        if 5 <= e <= 7:
                            ew.scaled(act, c, e - 5)
                        for (step, place), i in turns.items():
                            if step + AHEAD == e and place > 0:
                                ew.high(act, c, bk, i)
                    xt.scalar(act, c + 1, bk, c)

            @block.vector
            def _(dve):
                top.prepare(dve)
                dve.wait_ge(wh_done, 3)
                nc.vector.scalar_tensor_tensor(rwl[:, :, :], str_[:, :, :], WS, rwh[:, :, :], ALU.mult, ALU.subtract)\
                    .then_inc(w_done, 1)
                nc.vector.scalar_tensor_tensor(flat(w13l[:, :, :, :, :]), flat(st13[:, :, :, :, :]), WS,
                                               flat(w13h[:, :, :, :, :]), ALU.mult, ALU.subtract).then_inc(w_done, 1)
                nc.vector.scalar_tensor_tensor(flat3(w2l[:, :, :]), flat3(st2[:, :, :]), WS, flat3(w2h[:, :, :]),
                                               ALU.mult, ALU.subtract).then_inc(w_done, 1)
                nc.vector.memset(ew.magic[:, :], ROUND).then_inc(magic, 1)
                nrm.vector(dve, 0, row)
                xt.vector(dve, 0, bk0)
                with dve.Fori(0, CHUNKS) as c:
                    top.vector(dve, c, bk.tile(("g",)), rb[:, :].unsqueeze(1).to_broadcast([P, U, R]), bk, ("g",))
                    dve.wait_ge(top.s_g.sem, top.s_g.value(c, 0))
                    nc.vector.tensor_scalar(gs[:, :, :], top.gates[:, :, :], GS, None, ALU.mult).then_inc(s_gs.sem, 1)
                    dve.wait_ge(s_gh.sem, s_gh.value(c, 0))
                    nc.vector.tensor_tensor(g2[:, :, R:2 * R], gs[:, :, :], g2[:, :, 0:R], ALU.subtract).then_inc(s_gl.sem, 1)
                    for e in range(E):
                        for (step, place), i in turns.items():
                            if step + AHEAD == e and place == 0:
                                ew.low(dve, c, bk, i)
                        dve.wait_ge(bk.drained(("p1", e)), bk.n_out(c, ("p1", e)))
                        dve.wait_ge(bk.full(("p3", e)), bk.n_full(c, ("p3", e)))
                        pc, p = before(c, e)
                        dve.wait_ge(s_ul.sem, s_ul.value(pc, p))
                        nc.vector.scalar_tensor_tensor(uu[:, e % SL, :], sil[:, e % SL, :], (1 if e < R else GS) / WS,
                                                       bk.tile(("p3", e))[:, :], ALU.mult, ALU.mult)\
                            .then_inc(bk.drained(("p3", e)), 1)
                        if e < R:
                            dve.wait_ge(bk.drained(("p3", e)), bk.n_out(c, ("p3", e)))
                            dve.wait_ge(bk.full(("gb", e)), bk.n_full(c, ("gb", e)))
                            nc.vector.tensor_tensor(uu[:, e % SL, :], uu[:, e % SL, :], bk.tile(("gb", e))[:, :], ALU.mult)\
                                .then_inc(bk.drained(("gb", e)), 1)
                        if e < 3:
                            if e == 0:
                                dve.wait_ge(ew.s_in.sems[0], ew.s_in.value(c))
                            ew.qn.extremes(dve, c, ew.st[:, :, :], 2 * e)
                            ew.qn.extremes(dve, c, ew.st[:, :, :], 2 * e + 1)
                        if e == 2:
                            ew.qn.scales(dve, c)
                        if 4 <= e <= 6:
                            ew.qn.digits(dve, c, ew.st[:, :, :], ew.groups(e - 4))
                        if e == 5:
                            nrm.vector_stats(dve, c + 1, row)
                        if e == 7:
                            nrm.vector_rows(dve, c + 1, row)
                        for (step, place), i in turns.items():
                            if step + AHEAD == e and place > 0:
                                ew.low(dve, c, bk, i)
                    xt.vector(dve, c + 1, bk, c)
                    for i in range(2):
                        rows = core.h[:, bass.ds(c * U + 2 * i, 2), :]
                        dve.wait_ge(bk.full(("y", i)), bk.n_full(c, ("y", i)))
                        nc.vector.scalar_tensor_tensor(rows, bk.tile(("y", i))[:, :].rearrange("p (u d) -> p u d", u=2),
                                                       1 / (WS * GS), rows, ALU.mult, ALU.add)\
                            .then_inc(bk.drained(("y", i)), 1)

            @block.tensor
            def _(pe):
                pe.wait_ge(w_done, 3)

                def up(c, e):
                    for i, n in enumerate(("p1", "p3")):
                        pe.wait_ge(bk.drained((n, e)), bk.n_free(c, (n, e)))
                        for kd in range(KD):
                            last = three(nc, bk.tile((n, e))[:, :], (w13h[:, i, e, kd, :], w13l[:, i, e, kd, :]),
                                         (xt.xh[:, kd, :], xt.xl[:, kd, :]), kd == 0, kd == KD - 1)
                        last.then_inc(bk.full((n, e)), 1)

                def spread(c, e):
                    pe.wait_ge(bk.drained(("gb", e)), bk.n_free(c, ("gb", e)))
                    nc.tensor.matmul(bk.tile(("gb", e))[:, :], sel[:, e, :], gt[:, :], start=True, stop=True)\
                        .then_inc(bk.full(("gb", e)), 1)

                def down(c, e):
                    pe.wait_ge(s_ul.sem, s_ul.value(c, e))
                    for u in range(U):
                        i = u // 2
                        if e == 0 and u % 2 == 0:
                            pe.wait_ge(bk.drained(("y", i)), bk.n_free(c, ("y", i)))
                        last = three(nc, bk.tile(("y", i))[:, (u % 2) * D:(u % 2 + 1) * D],
                                     (uh[:, e % SL, u * P:(u + 1) * P], ul[:, e % SL, u * P:(u + 1) * P]),
                                     (w2h[:, e, :], w2l[:, e, :]), e == 0 and u % 2 == 0, e == E - 1 and u % 2 == 1)
                        if e == E - 1 and u % 2:
                            last.then_inc(bk.full(("y", i)), 1)
                    if e < E - 1:
                        last.then_inc(s_ye.sem, 1)

                def weights(c, step, place):
                    if (step, place) in turns:
                        ew.turn(pe, c, bk, turns[step, place])

                pe.sem_inc(s_ye.sem, E - 1)
                xt.tensor(pe, 0, bk0, nrm.xn, nrm.s_xn)
                for kd in range(KD):
                    pe.wait_ge(bk0.drained(("x", kd)), bk0.n_out(0, ("x", kd)))
                with pe.Fori(0, CHUNKS) as c:
                    for kd in range(KD):
                        pe.wait_ge(bk.drained(("x", kd)), bk.n_out(c - 1, ("x", kd)))
                    pe.sem_inc(core.tensor_waits, 1)
                    pe.wait_ge(bk.drained(("g",)), bk.n_free(c, ("g",)))
                    for u in range(U):
                        for kd in range(KD):
                            last = three(nc, bk.tile(("g",))[:, u * R:(u + 1) * R],
                                         (xt.xh[:, kd, u * P:(u + 1) * P], xt.xl[:, kd, u * P:(u + 1) * P]),
                                         (rwh[:, kd, :], rwl[:, kd, :]), kd == 0, kd == KD - 1)
                    last.then_inc(bk.full(("g",)), 1)
                    for e in range(AHEAD):
                        up(c, e)
                    pe.wait_ge(bk.drained(("gt",)), bk.n_free(c, ("gt",)))
                    pe.wait_ge(s_gh.sem, s_gh.value(c, 0))
                    pe.wait_ge(s_gl.sem, s_gl.value(c, 0))
                    for u in range(U):
                        last = nc.tensor.transpose(bk.tile(("gt",))[:, :].bitcast(F16)[0:2 * R, u * P:(u + 1) * P],
                                                   g2[:, u, :], identh[:, :])
                    last.then_inc(bk.full(("gt",)), 1)
                    pe.wait_ge(bk.drained(("gt",)), bk.n_out(c, ("gt",)))
                    for e in range(AHEAD):
                        spread(c, e)
                    for e in range(E):
                        weights(c, e, 0)
                        if e + AHEAD < E:
                            up(c, e + AHEAD)
                        if e + AHEAD < R:
                            spread(c, e + AHEAD)
                        weights(c, e, 1)
                        if e + AHEAD == E:
                            xt.tensor(pe, c + 1, bk, nrm.xn, nrm.s_xn, c)
                        down(c, e)
                        weights(c, e, 2)
        bk.close(CHUNKS)
    core.end_phase()


def attn1(core, a):
    nc = core.nc
    NH, DH, ROT = 2, 128, 32
    with ExitStack() as ctx:
        def sb(name, shape, dt):
            return ctx.enter_context(nc.sbuf_tensor(name, shape, dt))

        st = sb("a1_stage", [P, KD, 3, NH, DH], F32)
        sto = sb("a1_stage_wo", [P, KD, D], F32)
        wh = sb("a1_wh", [P, KD, 3, NH, DH], F16)
        wl = sb("a1_wl", [P, KD, 3, NH, DH], F16)
        woh = sb("a1_woh", [P, KD, D], F16)
        wol = sb("a1_wol", [P, KD, D], F16)
        rot = sb("a1_cos_sin", [P, 3, 2 * ROT], F32)
        mask = sb("a1_mask", [P, P], F32)
        nrm = Norm(core, "a1", sb)
        xt = Transposed(core, "a1", sb)
        qk = sb("a1_qk", [P, U, 2 * NH, DH], F32)
        v = sb("a1_v", [P, U, NH * DH], F32)
        tc = sb("a1_cos_part", [P, U, 2 * NH, 2 * ROT], F32)
        ts = sb("a1_sin_part", [P, U, 2 * NH, 2 * ROT], F32)
        qt = sb("a1_qt", [P, U, 2 * NH, P], F32)
        s = sb("a1_s", [P, U, NH, P], F32)
        nm = sb("a1_minus_max", [P, U, NH], F32)
        sm = sb("a1_sum", [P, U, NH], F32)
        rc = sb("a1_rsum", [P, U, NH], F32)
        pt = sb("a1_pt", [P, U, NH, P], F32)
        oh = sb("a1_oh", [P, U, NH, P], F16)
        ol = sb("a1_ol", [P, U, NH, P], F16)

        jobs = [("x", kd) for kd in range(KD)]
        jobs += [(n, u) for u in range(U) for n in ("qk", "v")]
        for n in ("t", "s", "pt", "o", "y"):
            jobs += [(n, u) for u in range(U)]
        bk = Banks(core, ring(jobs, range(8)))
        ends = chunk_ends(core, "a1", ["pe", "act", "dve", "pool"])
        loaded = core.sem("a1_loaded")
        wh_done = core.sem("a1_wh_done")
        w_done = core.sem("a1_w_done")
        s_ts = Stage(core, "a1_sin_parts_done", 3 * U)
        s_qr = Stage(core, "a1_rotated")
        s_nm = Stage(core, "a1_minus_max_done")
        s_ex = Stage(core, "a1_exp_done", NH * U)
        s_rc = Stage(core, "a1_rsum_done")
        s_pr = Stage(core, "a1_probs_done")
        s_oh = Stage(core, "a1_oh_done")

        def row(c, u):
            return core.h[:, bass.ds(c * U + u, 1), :].rearrange("p a d -> p (a d)")

        def flat(x):
            return x.rearrange("p k w h n -> p (k w h n)")

        def flat2(x):
            return x.rearrange("p a b -> p (a b)")

        with nc.Block() as block:
            @block.sync
            def _(sp):
                for i, n in enumerate(("wq", "wk", "wv")):
                    for h in range(NH):
                        sp.dma_start(st[:, :, i, h, :], a["L1_attn_" + n][h].rearrange("(k p) n -> p k n", p=P))\
                            .then_inc(loaded, 16)
                sp.dma_start(sto[:, :, :], a["L1_attn_wo"].rearrange("(k p) n -> p k n", p=P)).then_inc(loaded, 16)
                sp.dma_start(rot[:, :, :], a["rot_a1"]).then_inc(loaded, 16)
                sp.dma_start(mask[:, :], a["causal_mask"]).then_inc(loaded, 16)

            @block.gpsimd
            def _(pool):
                pool.wait_ge(loaded, 9 * 16)
                with pool.Fori(0, CHUNKS) as c:
                    nrm.gpsimd(pool, c)
                    for u in range(U):
                        pool.wait_ge(bk.drained(("qk", u)), bk.n_out(c, ("qk", u)))
                        nc.gpsimd.tensor_tensor(ts[:, u, :, 0:ROT], qk[:, u, :, ROT:2 * ROT],
                                                rot[:, 1, 0:ROT].unsqueeze(1).to_broadcast([P, 2 * NH, ROT]), ALU.mult)\
                            .then_inc(s_ts.sem, 1)
                        nc.gpsimd.tensor_tensor(ts[:, u, :, ROT:2 * ROT], qk[:, u, :, 0:ROT],
                                                rot[:, 2, 0:ROT].unsqueeze(1).to_broadcast([P, 2 * NH, ROT]), ALU.mult)\
                            .then_inc(s_ts.sem, 1)
                        nc.gpsimd.tensor_tensor(tc[:, u, :, :], qk[:, u, :, 0:2 * ROT],
                                                rot[:, 0, :].unsqueeze(1).to_broadcast([P, 2 * NH, 2 * ROT]), ALU.mult)\
                            .then_inc(s_ts.sem, 1)
                    for u in range(U):
                        pool.wait_ge(s_rc.sem, s_rc.value(c, u))
                        nc.gpsimd.tensor_tensor(s[:, u, :, :], s[:, u, :, :],
                                                rc[:, u, :].unsqueeze(2).to_broadcast([P, NH, P]), ALU.mult)\
                            .then_inc(s_pr.sem, 1)
                    pool.drain().then_inc(ends["pool"], 1)
                    for n in ends:
                        if n != "pool":
                            pool.wait_ge(ends[n], c + 1)

            @block.scalar
            def _(act):
                act.wait_ge(loaded, 9 * 16)
                nc.scalar.activation(flat(wh[:, :, :, :, :]), flat(st[:, :, :, :, :]), ACT.Copy, scale=WS).then_inc(wh_done, 1)
                nc.scalar.activation(flat2(woh[:, :, :]), flat2(sto[:, :, :]), ACT.Copy, scale=WS).then_inc(wh_done, 1)
                with act.Fori(0, CHUNKS) as c:
                    xt.scalar(act, c, bk)
                    for u in range(U):
                        act.wait_ge(bk.full(("qk", u)), bk.n_full(c, ("qk", u)))
                        nc.scalar.activation(qk[:, u, :, :].rearrange("p h n -> p (h n)"), bk.tile(("qk", u))[:, :],
                                                        ACT.Copy, scale=1 / WS)\
                            .then_inc(bk.drained(("qk", u)), 1)
                        act.wait_ge(bk.full(("v", u)), bk.n_full(c, ("v", u)))
                        nc.scalar.activation(v[:, u, :], bk.tile(("v", u))[:, 0:D], ACT.Copy, scale=1 / WS)\
                            .then_inc(bk.drained(("v", u)), 1)
                    for u in range(U):
                        act.wait_ge(bk.full(("t", u)), bk.n_full(c, ("t", u)))
                        nc.scalar.copy(flat2(qt[:, u, :, :]), bk.tile(("t", u))[:, :]).then_inc(bk.drained(("t", u)), 1)
                    for u in range(U):
                        act.wait_ge(s_nm.sem, s_nm.value(c, u))
                        for h in range(NH):
                            nc.scalar.activation(s[:, u, h, :], s[:, u, h, :], ACT.Exp, bias=nm[:, u, h:h + 1],
                                                 accum_out=sm[:, u, h:h + 1]).then_inc(s_ex.sem, 1)
                    for u in range(U):
                        act.wait_ge(bk.full(("o", u)), bk.n_full(c, ("o", u)))
                        nc.scalar.copy(flat2(oh[:, u, :, :]), bk.tile(("o", u))[:, 0:D]).then_inc(s_oh.sem, 1)
                    act.drain().then_inc(ends["act"], 1)
                    for n in ends:
                        if n != "act":
                            act.wait_ge(ends[n], c + 1)

            @block.vector
            def _(dve):
                dve.wait_ge(wh_done, 2)
                nc.vector.scalar_tensor_tensor(flat(wl[:, :, :, :, :]), flat(st[:, :, :, :, :]), WS, flat(wh[:, :, :, :, :]),
                                               ALU.mult, ALU.subtract).then_inc(w_done, 1)
                nc.vector.scalar_tensor_tensor(flat2(wol[:, :, :]), flat2(sto[:, :, :]), WS, flat2(woh[:, :, :]),
                                               ALU.mult, ALU.subtract).then_inc(w_done, 1)
                with dve.Fori(0, CHUNKS) as c:
                    nrm.vector(dve, c, row)
                    xt.vector(dve, c, bk)
                    for u in range(U):
                        dve.wait_ge(s_ts.sem, s_ts.value(c, 3 * u + 2))
                        nc.vector.tensor_tensor(qk[:, u, :, 0:2 * ROT], tc[:, u, :, :], ts[:, u, :, :], ALU.add)\
                            .then_inc(s_qr.sem, 1)
                    for u in range(U):
                        dve.wait_ge(bk.full(("s", u)), bk.n_full(c, ("s", u)))
                        nc.vector.scalar_tensor_tensor(
                            s[:, u, :, :], bk.tile(("s", u))[:, 0:NH * P].rearrange("p (h t) -> p h t", h=NH), 1 / DH,
                            mask[:, :].unsqueeze(1).to_broadcast([P, NH, P]), ALU.mult, ALU.add)\
                            .then_inc(bk.drained(("s", u)), 1)
                        dve.wait_ge(bk.drained(("s", u)), bk.n_out(c, ("s", u)))
                        nc.vector.tensor_reduce(nm[:, u, :], s[:, u, :, :], AX.X, ALU.max, negate=True).then_inc(s_nm.sem, 1)
                    for u in range(U):
                        dve.wait_ge(s_ex.sem, s_ex.value(c, NH * u + 1))
                        nc.vector.reciprocal(rc[:, u, :], sm[:, u, :]).then_inc(s_rc.sem, 1)
                    for u in range(U):
                        dve.wait_ge(bk.full(("pt", u)), bk.n_full(c, ("pt", u)))
                        nc.vector.tensor_copy(flat2(pt[:, u, :, :]), bk.tile(("pt", u))[:, 0:NH * P])\
                            .then_inc(bk.drained(("pt", u)), 1)
                    for u in range(U):
                        dve.wait_ge(s_oh.sem, s_oh.value(c, u))
                        nc.vector.tensor_tensor(flat2(ol[:, u, :, :]), bk.tile(("o", u))[:, 0:D],
                                                           flat2(oh[:, u, :, :]), ALU.subtract)\
                            .then_inc(bk.drained(("o", u)), 1)
                    for u in range(U):
                        dve.wait_ge(bk.full(("y", u)), bk.n_full(c, ("y", u)))
                        nc.vector.scalar_tensor_tensor(row(c, u), bk.tile(("y", u))[:, 0:D], 1 / WS, row(c, u),
                                                                  ALU.mult, ALU.add)\
                            .then_inc(bk.drained(("y", u)), 1)
                    dve.drain().then_inc(ends["dve"], 1)
                    for n in ends:
                        if n != "dve":
                            dve.wait_ge(ends[n], c + 1)

            @block.tensor
            def _(pe):
                pe.wait_ge(w_done, 2)
                with pe.Fori(0, CHUNKS) as c:
                    xt.tensor(pe, c, bk, nrm.xn, nrm.s_xn)
                    for kd in range(KD):
                        pe.wait_ge(bk.drained(("x", kd)), bk.n_out(c, ("x", kd)))
                    for u in range(U):
                        for n, w, m in (("qk", 0, 4 * DH), ("v", 2, 2 * DH)):
                            pe.wait_ge(bk.drained((n, u)), bk.n_free(c, (n, u)))
                            for kd in range(KD):
                                ws = [x[:, kd, w:(2 if w == 0 else 3), :, :].rearrange("p w h n -> p (w h n)") for x in (wh, wl)]
                                last = three(nc, bk.tile((n, u))[:, 0:m],
                                             (xt.xh[:, kd, u * P:(u + 1) * P], xt.xl[:, kd, u * P:(u + 1) * P]),
                                             ws, kd == 0, kd == KD - 1)
                            last.then_inc(bk.full((n, u)), 1)
                    for u in range(U):
                        pe.wait_ge(bk.drained(("t", u)), bk.n_free(c, ("t", u)))
                        pe.wait_ge(s_qr.sem, s_qr.value(c, u))
                        pe.wait_ge(bk.drained(("v", u)), bk.n_out(c, ("v", u)))
                        for i in range(2 * NH):
                            last = nc.tensor.transpose(bk.tile(("t", u))[:, i * P:(i + 1) * P], qk[:, u, i, :], core.ident[:, :])
                        last.then_inc(bk.full(("t", u)), 1)
                    for u in range(U):
                        pe.wait_ge(bk.drained(("t", u)), bk.n_out(c, ("t", u)))
                        pe.wait_ge(bk.drained(("s", u)), bk.n_free(c, ("s", u)))
                        for h in range(NH):
                            last = nc.tensor.matmul(bk.tile(("s", u))[:, h * P:(h + 1) * P], qt[:, u, h, :], qt[:, u, NH + h, :],
                                                    start=True, stop=True)
                        last.then_inc(bk.full(("s", u)), 1)
                    for u in range(U):
                        pe.wait_ge(s_pr.sem, s_pr.value(c, u))
                        pe.wait_ge(bk.drained(("pt", u)), bk.n_free(c, ("pt", u)))
                        for h in range(NH):
                            last = nc.tensor.transpose(bk.tile(("pt", u))[:, h * P:(h + 1) * P], s[:, u, h, :], core.ident[:, :])
                        last.then_inc(bk.full(("pt", u)), 1)
                    for u in range(U):
                        pe.wait_ge(bk.drained(("pt", u)), bk.n_out(c, ("pt", u)))
                        pe.wait_ge(bk.drained(("o", u)), bk.n_free(c, ("o", u)))
                        for h in range(NH):
                            last = nc.tensor.matmul(bk.tile(("o", u))[:, h * P:(h + 1) * P], v[:, u, h * DH:(h + 1) * DH],
                                                    pt[:, u, h, :], start=True, stop=True)
                        last.then_inc(bk.full(("o", u)), 1)
                    for u in range(U):
                        pe.wait_ge(bk.drained(("o", u)), bk.n_out(c, ("o", u)))
                        pe.wait_ge(bk.drained(("y", u)), bk.n_free(c, ("y", u)))
                        for h in range(NH):
                            last = three(nc, bk.tile(("y", u))[:, 0:D], (oh[:, u, h, :], ol[:, u, h, :]),
                                         (woh[:, h, :], wol[:, h, :]), h == 0, h == NH - 1)
                        last.then_inc(bk.full(("y", u)), 1)
                    pe.drain().then_inc(ends["pe"], 1)
                    for n in ends:
                        if n != "pe":
                            pe.wait_ge(ends[n], c + 1)
        bk.close(CHUNKS)
    core.end_phase()


def block1_weights(core, a, wh, wl, woh, wol):
    nc = core.nc
    with ExitStack() as ctx:
        def sb(name, shape, dt):
            return ctx.enter_context(nc.sbuf_tensor(name, shape, dt))

        st = sb("bw_stage", [P, 40, P], F32)
        qn = Quant(core, "bw", sb, 40)
        moves = []
        for kd in range(KD):
            for f in range(0, 12, 4):
                moves.append((wh[:, kd, f * P:(f + 4) * P], wl[:, kd, f * P:(f + 4) * P], [2 * (f + i) + kd for i in range(4)]))
        for g in range(0, 8, 2):
            moves.append((woh[:, g:g + 2, :].rearrange("p g n -> p (g n)"), wol[:, g:g + 2, :].rearrange("p g n -> p (g n)"),
                          [24 + 8 * db + g + i for i in range(2) for db in range(2)]))
        bk = Banks(core, ring([("m", i) for i in range(len(moves))], range(8)))
        loaded = core.sem("bw_loaded")
        scaled = core.sem("bw_scaled")
        s_hi = Stage(core, "bw_high_done", len(moves))
        with nc.Block() as block:
            @block.sync
            def _(sp):
                for at, n, rows in ((0, "w_q", 8), (16, "w_k", 2), (20, "w_v", 2)):
                    sp.dma_start(st[:, at:at + 2 * rows, :].rearrange("p (r g) k -> p r (g k)", r=rows),
                                 a["L1_ffn_" + n].rearrange("(r p) n -> p r n", p=P)).then_inc(loaded, 16)
                sp.dma_start(st[:, 24:40, :].rearrange("p (r g) k -> p r (g k)", r=2),
                             a["L1_ffn_w_o"].rearrange("(r p) n -> p r n", p=P)).then_inc(loaded, 16)

            @block.vector
            def _(dve):
                dve.wait_ge(loaded, 64)
                qn.vector(dve, 0, st[:, :, :])
                for i, (hi, lo, _) in enumerate(moves):
                    dve.wait_ge(s_hi.sem, s_hi.value(0, i))
                    nc.vector.scalar_tensor_tensor(lo, bk.tile(("m", i))[:, :], WS, hi, ALU.mult, ALU.subtract)\
                        .then_inc(bk.drained(("m", i)), 1)

            @block.scalar
            def _(act):
                for g in range(40):
                    act.wait_ge(qn.s_w3.sem, qn.s_w3.value(0, g))
                    nc.scalar.activation(st[:, g, :], st[:, g, :], ACT.Copy, scale=qn.s[:, g:g + 1]).then_inc(scaled, 1)
                for i, (hi, lo, _) in enumerate(moves):
                    act.wait_ge(bk.full(("m", i)), bk.n_full(0, ("m", i)))
                    nc.scalar.activation(hi, bk.tile(("m", i))[:, :], ACT.Copy, scale=WS).then_inc(s_hi.sem, 1)

            @block.tensor
            def _(pe):
                for i, (_, _, groups) in enumerate(moves):
                    pe.wait_ge(bk.drained(("m", i)), bk.n_free(0, ("m", i)))
                    pe.wait_ge(scaled, max(groups) + 1)
                    for j, g in enumerate(groups):
                        last = nc.tensor.transpose(bk.tile(("m", i))[:, j * P:(j + 1) * P], st[:, g, :], core.ident[:, :])
                    last.then_inc(bk.full(("m", i)), 1)
        bk.close(1)
    core.end_phase()


def block1(core, a, hn, gates, masks):
    nc = core.nc
    H, KVH, HD = 8, 2, 128
    with ExitStack() as ctx:
        def sb(name, shape, dt):
            return ctx.enter_context(nc.sbuf_tensor(name, shape, dt))

        NQ = H + 2 * KVH
        wh = sb("b1_wh", [P, KD, NQ * HD], F16)
        wl = sb("b1_wl", [P, KD, NQ * HD], F16)
        woh = sb("b1_woh", [P, H, D], F16)
        wol = sb("b1_wol", [P, H, D], F16)
        block1_weights(core, a, wh, wl, woh, wol)

        stg = sb("b1_stage_gate", [P, KD, 8], F32)
        wgh = sb("b1_gate_high", [P, KD, 8], F16)
        wgl = sb("b1_gate_low", [P, KD, 8], F16)
        rot = sb("b1_cos_sin", [P, 2, HD], F32)
        mask = sb("b1_mask", [P, P], F32)
        g1 = sb("b1_g1", [P, D], F32)
        g2 = sb("b1_g2", [P, D], F32)
        nrm = Norm(core, "b1", sb)
        xt = Transposed(core, "b1", sb)
        xt2 = Transposed(core, "b1b", sb, "x2")
        top = TopTwo(core, "b1", sb)
        qn = Quant(core, "b1kv", sb, U * 2 * KVH)
        xr = sb("b1_xr", [P, U, D], F32)
        ssq = sb("b1_sum_squares", [P, 2, U], F32)
        rms = sb("b1_rms", [P, 2, U], F32)
        inv_d = sb("b1_one_over_d", [P, U], F32)
        qk = sb("b1_qk", [P, U, H + KVH, HD], F32)
        kv = sb("b1_kv", [P, U, 2 * KVH, HD], F32)
        vq = sb("b1_v", [P, U, KVH, HD], F32)
        ts = sb("b1_sin_part", [P, 2, H + KVH, HD], F32)
        qt = sb("b1_qt", [P, U, H + KVH, P], F32)
        s = sb("b1_s", [P, U, H, P], F32)
        nm = sb("b1_minus_max", [P, U, H], F32)
        sm = sb("b1_sum", [P, U, H], F32)
        rc = sb("b1_rsum", [P, U, H], F32)
        pt = qk[:, :, 0:H, :]
        oh = sb("b1_oh", [P, 2, H, P], F16)
        ol = sb("b1_ol", [P, 2, H, P], F16)

        jobs = [("x", kd) for kd in range(KD)]
        projected = [("kv", u) for u in range(U)] + [(n, u) for u in range(U) for n in ("q0", "q1")]
        jobs += projected
        jobs += [(n, u) for u in range(U) for n in ("tk", "tq0", "tq1")]
        jobs += [(n, u) for u in range(U) for n in ("s0", "s1")]
        jobs += [(n, v) for u in range(U + 1) for n, v in (("p0", u), ("p1", u), ("o0", u), ("o1", u), ("y", u - 1)) if 0 <= v < U]
        jobs += [("x2", kd) for kd in range(KD)] + [("g",)]
        bk = Banks(core, ring(jobs, range(8)))
        ends = chunk_ends(core, "b1", ["pe", "act", "dve", "pool"])
        loaded = core.sem("b1_loaded")
        wh_done = core.sem("b1_wh_done")
        w_done = core.sem("b1_w_done")
        filled = core.sem("b1_one_over_d_filled")
        s_sq = Stage(core, "b1_squares_done", 2 * U)
        s_rm = Stage(core, "b1_rms_done", 6)
        s_xr = Stage(core, "b1_xr_done")
        s_kq = Stage(core, "b1_k_scaled")
        s_vq = Stage(core, "b1_v_scaled")
        s_ts = Stage(core, "b1_sin_parts_done", 2 * U)
        s_cq = Stage(core, "b1_cos_parts_done")
        s_rq = Stage(core, "b1_rotated")
        s_nm = Stage(core, "b1_minus_max_done", 2 * U)
        s_ex = Stage(core, "b1_exp_done", H * U)
        s_rc = Stage(core, "b1_rsum_done")
        s_pr = Stage(core, "b1_probs_done")
        s_oh = Stage(core, "b1_oh_done", 2 * U)
        s_hn = Stage(core, "b1_hn_done")
        s_ga = Stage(core, "b1_gates_kept", 2)
        s_hr = Stage(core, "b1_hn_kept", 1)
        s_rs = Stage(core, "b1_h_added")

        def row(c, u, t=core.h):
            return t[:, bass.ds(c * U + u, 1), :].rearrange("p a d -> p (a d)")

        def flat2(x):
            return x.rearrange("p a b -> p (a b)")

        def halves(x):
            return x.rearrange("p h (f n) -> p h f n", f=2)

        def root_mean(pool, c, i):
            pool.wait_ge(s_sq.sem, s_sq.value(c, U * i + U - 1))
            ms = rms[:, i, :]
            nc.gpsimd.tensor_tensor(ms, ssq[:, i, :], inv_d[:, :], ALU.mult).then_inc(s_rm.sem, 1)
            pool.wait_ge(s_rm.sem, s_rm.value(c, 3 * i))
            nc.gpsimd.tensor_tensor(ms, ms, core.eps[:, :], ALU.add).then_inc(s_rm.sem, 1)
            pool.wait_ge(s_rm.sem, s_rm.value(c, 3 * i + 1))
            nc.gpsimd.tensor_tensor(ms, ms, core.mhalf[:, :], ALU.pow).then_inc(s_rm.sem, 1)

        with nc.Block() as block:
            @block.sync
            def _(sp):
                sp.dma_start(stg[:, :, :], a["w_gate_t"].rearrange("(k p) e -> p k e", p=P)).then_inc(loaded, 16)
                sp.dma_start(rot[:, :, :], a["rot_b1"]).then_inc(loaded, 16)
                sp.dma_start(mask[:, :], a["causal_mask"]).then_inc(loaded, 16)
                sp.dma_start(g1[:, :], a["L1_ffn_g1"].partition_broadcast(P)).then_inc(loaded, 16)
                sp.dma_start(g2[:, :], a["L1_ffn_g2"].partition_broadcast(P)).then_inc(loaded, 16)

            @block.gpsimd
            def _(pool):
                pool.memset(inv_d[:, :], 1 / D).then_inc(filled, 1)
                pool.wait_ge(loaded, 5 * 16)
                pool.wait_ge(filled, 1)
                with pool.Fori(0, CHUNKS) as c:
                    nrm.gpsimd(pool, c)
                    root_mean(pool, c, 0)
                    for u in range(U):
                        if u == 0:
                            for v in range(U):
                                pool.wait_ge(s_kq.sem, s_kq.value(c, v))
                        if u >= 2:
                            pool.wait_ge(s_rq.sem, s_rq.value(c, u - 2))
                        pool.wait_ge(bk.drained(("q0", u)), bk.n_out(c, ("q0", u)))
                        pool.wait_ge(bk.drained(("q1", u)), bk.n_out(c, ("q1", u)))
                        for f in range(2):
                            nc.gpsimd.tensor_tensor(halves(ts[:, u % 2, :, :])[:, :, f, :], halves(qk[:, u, :, :])[:, :, 1 - f, :],
                                                    rot[:, 1, f * 64:(f + 1) * 64].unsqueeze(1).to_broadcast([P, H + KVH, 64]),
                                                    ALU.mult).then_inc(s_ts.sem, 1)
                    for u in range(U):
                        pool.wait_ge(s_rc.sem, s_rc.value(c, u))
                        nc.gpsimd.tensor_tensor(s[:, u, :, :], s[:, u, :, :],
                                                rc[:, u, :].unsqueeze(2).to_broadcast([P, H, P]), ALU.mult).then_inc(s_pr.sem, 1)
                    root_mean(pool, c, 1)
                    pool.drain().then_inc(ends["pool"], 1)
                    for n in ends:
                        if n != "pool":
                            pool.wait_ge(ends[n], c + 1)

            @block.scalar
            def _(act):
                act.wait_ge(loaded, 5 * 16)
                nc.scalar.activation(wgh[:, :, :], stg[:, :, :], ACT.Copy, scale=WS).then_inc(wh_done, 1)
                with act.Fori(0, CHUNKS) as c:
                    for u in range(U):
                        act.wait_ge(nrm.s_xn.sem, nrm.s_xn.value(c, u))
                        nc.scalar.activation(xr[:, u, :], nrm.xn[:, u, :], ACT.Square, accum_out=ssq[:, 0, u:u + 1])\
                            .then_inc(s_sq.sem, 1)
                    xt.scalar(act, c, bk)
                    for n, u in projected:
                        act.wait_ge(bk.full((n, u)), bk.n_full(c, (n, u)))
                        dst = flat2(kv[:, u, :, :]) if n == "kv" else flat2(qk[:, u, 4 * int(n[1]):4 * int(n[1]) + 4, :])
                        nc.scalar.activation(dst, bk.tile((n, u))[:, :], ACT.Copy, scale=1 / WS)\
                            .then_inc(bk.drained((n, u)), 1)
                    for u in range(U):
                        for i in range(2 * KVH):
                            g = u * 2 * KVH + i
                            act.wait_ge(qn.s_w3.sem, qn.s_w3.value(c, g))
                            dst = qk[:, u, H + i, :] if i < KVH else vq[:, u, i - KVH, :]
                            ins = nc.scalar.activation(dst, kv[:, u, i, :], ACT.Copy, scale=qn.s[:, g:g + 1])
                            if i == KVH - 1:
                                ins.then_inc(s_kq.sem, 1)
                            if i == 2 * KVH - 1:
                                ins.then_inc(s_vq.sem, 1)
                    for u in range(U):
                        act.wait_ge(bk.full(("tq0", u)), bk.n_full(c, ("tq0", u)))
                        nc.scalar.copy(flat2(qt[:, u, 0:4, :]), bk.tile(("tq0", u))[:, :])\
                            .then_inc(bk.drained(("tq0", u)), 1)
                    for u in range(U):
                        for h in range(H):
                            if h % 4 == 0:
                                act.wait_ge(s_nm.sem, s_nm.value(c, 2 * u + h // 4))
                            nc.scalar.activation(s[:, u, h, :], s[:, u, h, :], ACT.Exp, bias=nm[:, u, h:h + 1],
                                                 accum_out=sm[:, u, h:h + 1]).then_inc(s_ex.sem, 1)
                    for u in range(U):
                        act.wait_ge(bk.full(("p0", u)), bk.n_full(c, ("p0", u)))
                        nc.scalar.copy(flat2(pt[:, u, 0:4, :]), bk.tile(("p0", u))[:, :]).then_inc(bk.drained(("p0", u)), 1)
                        for i in range(2):
                            if u >= 2 and i == 0:
                                act.wait_ge(bk.full(("y", u - 2)), bk.n_full(c, ("y", u - 2)))
                            act.wait_ge(bk.full((f"o{i}", u)), bk.n_full(c, (f"o{i}", u)))
                            nc.scalar.copy(flat2(oh[:, u % 2, 4 * i:4 * i + 4, :]), bk.tile((f"o{i}", u))[:, :])\
                                .then_inc(s_oh.sem, 1)
                    for u in range(U):
                        act.wait_ge(s_rs.sem, s_rs.value(c, u))
                        nc.scalar.activation(xr[:, u, :], nrm.xn[:, u, :], ACT.Square, accum_out=ssq[:, 1, u:u + 1])\
                            .then_inc(s_sq.sem, 1)
                    xt2.scalar(act, c, bk)
                    top.scalar(act, c)
                    act.drain().then_inc(ends["act"], 1)
                    for n in ends:
                        if n != "act":
                            act.wait_ge(ends[n], c + 1)

            @block.vector
            def _(dve):
                top.prepare(dve)
                dve.wait_ge(wh_done, 1)
                nc.vector.scalar_tensor_tensor(wgl[:, :, :], stg[:, :, :], WS, wgh[:, :, :], ALU.mult, ALU.subtract)\
                    .then_inc(w_done, 1)
                with dve.Fori(0, CHUNKS) as c:
                    nrm.vector(dve, c, row)
                    dve.wait_ge(s_rm.sem, s_rm.value(c, 2))
                    for u in range(U):
                        nc.vector.scalar_tensor_tensor(xr[:, u, :], nrm.xn[:, u, :], rms[:, 0, u:u + 1], g1[:, :],
                                                       ALU.mult, ALU.mult).then_inc(s_xr.sem, 1)
                    xt.vector(dve, c, bk)
                    for u in range(U):
                        dve.wait_ge(bk.drained(("kv", u)), bk.n_out(c, ("kv", u)))
                    qn.vector(dve, c, kv[:, :, :, :].rearrange("p u i n -> p (u i) n"))
                    for u in range(U):
                        dve.wait_ge(s_ts.sem, s_ts.value(c, 2 * u + 1))
                        nc.vector.tensor_tensor(qk[:, u, :, :], qk[:, u, :, :],
                                                rot[:, 0, :].unsqueeze(1).to_broadcast([P, H + KVH, HD]), ALU.mult)\
                            .then_inc(s_cq.sem, 1)
                        dve.wait_ge(s_cq.sem, s_cq.value(c, u))
                        nc.vector.tensor_tensor(qk[:, u, :, :], qk[:, u, :, :], ts[:, u % 2, :, :], ALU.add)\
                            .then_inc(s_rq.sem, 1)
                    for u in range(U):
                        dve.wait_ge(bk.full(("tk", u)), bk.n_full(c, ("tk", u)))
                        nc.vector.tensor_copy(flat2(qt[:, u, H:H + KVH, :]), bk.tile(("tk", u))[:, 0:KVH * P])\
                            .then_inc(bk.drained(("tk", u)), 1)
                        dve.wait_ge(bk.full(("tq1", u)), bk.n_full(c, ("tq1", u)))
                        nc.vector.tensor_copy(flat2(qt[:, u, 4:8, :]), bk.tile(("tq1", u))[:, :])\
                            .then_inc(bk.drained(("tq1", u)), 1)
                    for u in range(U):
                        for i in range(2):
                            hs = slice(4 * i, 4 * i + 4)
                            n = (f"s{i}", u)
                            dve.wait_ge(bk.full(n), bk.n_full(c, n))
                            nc.vector.scalar_tensor_tensor(
                                s[:, u, hs, :], bk.tile(n)[:, :].rearrange("p (h t) -> p h t", h=4), HD ** -0.5,
                                mask[:, :].unsqueeze(1).to_broadcast([P, 4, P]), ALU.mult, ALU.add)\
                                .then_inc(bk.drained(n), 1)
                            dve.wait_ge(bk.drained(n), bk.n_out(c, n))
                            nc.vector.tensor_reduce(nm[:, u, hs], s[:, u, hs, :], AX.X, ALU.max, negate=True)\
                                .then_inc(s_nm.sem, 1)
                    for u in range(U):
                        dve.wait_ge(s_ex.sem, s_ex.value(c, H * (u + 1) - 1))
                        nc.vector.reciprocal(rc[:, u, :], sm[:, u, :]).then_inc(s_rc.sem, 1)

                    def residual(u):
                        dve.wait_ge(bk.full(("y", u)), bk.n_full(c, ("y", u)))
                        nc.vector.scalar_tensor_tensor(nrm.xn[:, u, :], bk.tile(("y", u))[:, 0:D], 1 / WS,
                                                                  nrm.xn[:, u, :], ALU.mult, ALU.add)\
                            .then_inc(bk.drained(("y", u)), 1)

                    for u in range(U):
                        dve.wait_ge(bk.full(("p1", u)), bk.n_full(c, ("p1", u)))
                        nc.vector.tensor_copy(flat2(pt[:, u, 4:8, :]), bk.tile(("p1", u))[:, :])\
                            .then_inc(bk.drained(("p1", u)), 1)
                        for i in range(2):
                            n = (f"o{i}", u)
                            dve.wait_ge(s_oh.sem, s_oh.value(c, 2 * u + i))
                            nc.vector.tensor_tensor(flat2(ol[:, u % 2, 4 * i:4 * i + 4, :]), bk.tile(n)[:, :],
                                                               flat2(oh[:, u % 2, 4 * i:4 * i + 4, :]), ALU.subtract)\
                                .then_inc(bk.drained(n), 1)
                        if u:
                            residual(u - 1)
                    residual(U - 1)
                    for u in range(U):
                        dve.wait_ge(bk.drained(("y", u)), bk.n_out(c, ("y", u)))
                        nc.vector.tensor_tensor(row(c, u), row(c, u), nrm.xn[:, u, :], ALU.add).then_inc(s_rs.sem, 1)
                    dve.wait_ge(s_rm.sem, s_rm.value(c, 5))
                    for u in range(U):
                        nc.vector.scalar_tensor_tensor(xr[:, u, :], nrm.xn[:, u, :], rms[:, 1, u:u + 1], g2[:, :],
                                                       ALU.mult, ALU.mult).then_inc(s_hn.sem, 1)
                    dve.wait_ge(s_hn.sem, s_hn.value(c, U - 1))
                    nc.vector.tensor_copy(hn[:, bass.ds(c * U, U), :], xr[:, :, :]).then_inc(s_hr.sem, 1)
                    xt2.vector(dve, c, bk)
                    top.vector(dve, c, bk.tile(("g",)), None, bk, ("g",))
                    dve.wait_ge(top.s_g.sem, top.s_g.value(c, 0))
                    nc.vector.tensor_copy(gates[:, bass.ds(c * U, U), :], top.gates[:, :, :]).then_inc(s_ga.sem, 1)
                    nc.vector.tensor_copy(masks[:, bass.ds(c * U, U), :], top.mask[:, :, :]).then_inc(s_ga.sem, 1)
                    dve.drain().then_inc(ends["dve"], 1)
                    for n in ends:
                        if n != "dve":
                            dve.wait_ge(ends[n], c + 1)

            @block.tensor
            def _(pe):
                pe.wait_ge(w_done, 1)
                with pe.Fori(0, CHUNKS) as c:
                    xt.tensor(pe, c, bk, xr, s_xr)
                    for kd in range(KD):
                        pe.wait_ge(bk.drained(("x", kd)), bk.n_out(c, ("x", kd)))
                    for n, u in projected:
                        at = {"kv": 1024, "q0": 0, "q1": 512}[n]
                        pe.wait_ge(bk.drained((n, u)), bk.n_free(c, (n, u)))
                        for kd in range(KD):
                            last = three(nc, bk.tile((n, u))[:, :],
                                         (xt.xh[:, kd, u * P:(u + 1) * P], xt.xl[:, kd, u * P:(u + 1) * P]),
                                         (wh[:, kd, at:at + 512], wl[:, kd, at:at + 512]), kd == 0, kd == KD - 1)
                        last.then_inc(bk.full((n, u)), 1)
                    for u in range(U):
                        pe.wait_ge(s_rq.sem, s_rq.value(c, u))
                        for n, at, m in (("tk", H, KVH), ("tq0", 0, 4), ("tq1", 4, 4)):
                            pe.wait_ge(bk.drained((n, u)), bk.n_free(c, (n, u)))
                            for i in range(m):
                                last = nc.tensor.transpose(bk.tile((n, u))[:, i * P:(i + 1) * P], qk[:, u, at + i, :],
                                                           core.ident[:, :])
                            last.then_inc(bk.full((n, u)), 1)
                    for u in range(U):
                        for i in range(2):
                            n = (f"s{i}", u)
                            pe.wait_ge(bk.drained(("tk", u)), bk.n_out(c, ("tk", u)))
                            pe.wait_ge(bk.drained((f"tq{i}", u)), bk.n_out(c, (f"tq{i}", u)))
                            pe.sem_inc(core.tensor_waits, 1)
                            pe.wait_ge(bk.drained(n), bk.n_free(c, n))
                            for j in range(4):
                                last = nc.tensor.matmul(bk.tile(n)[:, j * P:(j + 1) * P], qt[:, u, 4 * i + j, :],
                                                        qt[:, u, H + i, :], start=True, stop=True)
                            last.then_inc(bk.full(n), 1)

                    def project(u):
                        pe.wait_ge(s_oh.sem, s_oh.value(c, 2 * u + 1))
                        for i in range(2):
                            pe.wait_ge(bk.drained((f"o{i}", u)), bk.n_out(c, (f"o{i}", u)))
                        pe.sem_inc(core.tensor_waits, 1)
                        pe.wait_ge(bk.drained(("y", u)), bk.n_free(c, ("y", u)))
                        for h in range(H):
                            last = three(nc, bk.tile(("y", u))[:, 0:D], (oh[:, u % 2, h, :], ol[:, u % 2, h, :]),
                                         (woh[:, h, :], wol[:, h, :]), h == 0, h == H - 1)
                        last.then_inc(bk.full(("y", u)), 1)

                    for u in range(U):
                        pe.wait_ge(s_pr.sem, s_pr.value(c, u))
                        for i in range(2):
                            n = (f"p{i}", u)
                            pe.wait_ge(bk.drained(n), bk.n_free(c, n))
                            for j in range(4):
                                last = nc.tensor.transpose(bk.tile(n)[:, j * P:(j + 1) * P], s[:, u, 4 * i + j, :],
                                                           core.ident[:, :])
                            last.then_inc(bk.full(n), 1)
                        pe.wait_ge(s_vq.sem, s_vq.value(c, u))
                        for i in range(2):
                            n = (f"o{i}", u)
                            pe.wait_ge(bk.drained((f"p{i}", u)), bk.n_out(c, (f"p{i}", u)))
                            pe.sem_inc(core.tensor_waits, 1)
                            pe.wait_ge(bk.drained(n), bk.n_free(c, n))
                            nc.tensor.matmul(bk.tile(n)[:, :], vq[:, u, i, :], flat2(pt[:, u, 4 * i:4 * i + 4, :]),
                                                       start=True, stop=True)\
                                .then_inc(bk.full(n), 1)
                        if u:
                            project(u - 1)
                    project(U - 1)
                    xt2.tensor(pe, c, bk, xr, s_hn)
                    for kd in range(KD):
                        pe.wait_ge(bk.drained(("x2", kd)), bk.n_out(c, ("x2", kd)))
                    pe.wait_ge(bk.drained(("g",)), bk.n_free(c, ("g",)))
                    for u in range(U):
                        for kd in range(KD):
                            last = three(nc, bk.tile(("g",))[:, u * 8:(u + 1) * 8],
                                         (xt2.xh[:, kd, u * P:(u + 1) * P], xt2.xl[:, kd, u * P:(u + 1) * P]),
                                         (wgh[:, kd, :], wgl[:, kd, :]), kd == 0, kd == KD - 1)
                    last.then_inc(bk.full(("g",)), 1)
                    pe.drain().then_inc(ends["pe"], 1)
                    for n in ends:
                        if n != "pe":
                            pe.wait_ge(ends[n], c + 1)
        bk.close(CHUNKS)
    core.end_phase()


def route(core, a, hn, gates, masks, slot, share, tile_expert):
    nc = core.nc
    with ExitStack() as ctx:
        def sb(name, shape, dt):
            return ctx.enter_context(nc.sbuf_tensor(name, shape, dt))

        tri = sb("rt_before", [P, P], F32)
        ones = sb("rt_ones", [P, P], F32)
        number = sb("rt_tile_number", [P, MTILES, E1], F32)
        zero = sb("rt_zero", [P, TILES], F32)
        rank = sb("rt_rank", [P, TILES, E1], F32)
        tot = sb("rt_total", [P, TILES, E1], F32)
        incl = sb("rt_inclusive", [P, TILES, E1], F32)
        need = sb("rt_tiles_needed", [P, E1], F32)
        cum = sb("rt_tiles_to", [P, E1], F32)
        offs = sb("rt_first_row", [P, E1], F32)
        mp = sb("rt_masked_row", [P, TILES, E1], F32)
        sl = sb("rt_slots", [P, TILES, 2], F32)
        past = sb("rt_past", [P, MTILES, E1], F32)
        te = sb("rt_tile_expert", [P, MTILES], F32)
        sm = sb("rt_slot_sum", [P, TILES], F32)
        bk = Banks(core, [("rank", 0), ("tot", 1)])
        loaded = core.sem("rt_loaded")
        spilled = core.sem("rt_h_stored")
        step = core.sem("rt_vector_steps")
        scattered = core.sem("rt_rows_scattered")

        def over_tiles(x):
            return x.unsqueeze(1).to_broadcast([P, TILES, E1])

        def over_experts(x):
            return x.unsqueeze(2).to_broadcast([P, TILES, E1])

        with nc.Block() as block:
            @block.sync
            def _(sp):
                sp.dma_start(tri[:, :], a["before"]).then_inc(loaded, 16)
                sp.dma_start(number[:, :, :], a["tile_number"].partition_broadcast(P)).then_inc(loaded, 16)
                sp.dma_start(a["h_rows"], core.h[:, 0:TILES, :]).then_inc(spilled, 16)
                sp.wait_ge(spilled, 16)

            @block.tensor
            def _(pe):
                pe.wait_ge(loaded, 32)
                pe.wait_ge(step, 1)
                for n, w in (("rank", tri), ("tot", ones)):
                    pe.wait_ge(bk.drained((n)), bk.n_free(0, (n)))
                    nc.tensor.matmul(bk.tile(n)[:, 0:TILES * E1], w[:, :],
                                               masks[:, :, :].rearrange("p t e -> p (t e)"), start=True, stop=True)\
                        .then_inc(bk.full(n), 1)

            @block.vector
            def _(dve):
                v, done = nc.vector, [0]

                def then(ins, n=1):
                    done[0] += 1
                    ins.then_inc(step, 1)
                    dve.wait_ge(step, done[0])

                then(v.memset(ones[:, :], 1.0))
                then(v.memset(zero[:, :], 0.0))
                dve.wait_ge(bk.full("rank"), bk.n_full(0, "rank"))
                v.tensor_copy(rank[:, :, :].rearrange("p t e -> p (t e)"), bk.tile("rank")[:, 0:TILES * E1])\
                    .then_inc(bk.drained("rank"), 1)
                dve.wait_ge(bk.full("tot"), bk.n_full(0, "tot"))
                v.tensor_copy(tot[:, :, :].rearrange("p t e -> p (t e)"), bk.tile("tot")[:, 0:TILES * E1])\
                    .then_inc(bk.drained("tot"), 1)
                dve.wait_ge(bk.drained("rank"), bk.n_out(0, "rank"))
                dve.wait_ge(bk.drained("tot"), bk.n_out(0, "tot"))
                dve.wait_ge(loaded, 32)
                for e in range(E1):
                    then(v.tensor_tensor_scan(incl[:, :, e], tot[:, :, e], zero[:, :], 0.0, ALU.add, ALU.add))
                cnt = incl[:, TILES - 1, :]
                then(v.tensor_scalar(need[:, :], cnt, 1 / MT, (MT - 1) / MT - 0.5 + 0.5 / MT, ALU.mult, ALU.add))
                then(v.tensor_scalar(need[:, :], need[:, :], ROUND, ROUND, ALU.add, ALU.subtract))
                then(v.tensor_tensor_scan(cum[:, :], need[:, :], zero[:, 0:E1], 0.0, ALU.add, ALU.add))
                then(v.tensor_tensor(offs[:, :], cum[:, :], need[:, :], ALU.subtract))
                then(v.tensor_scalar(offs[:, :], offs[:, :], float(MT), None, ALU.mult))
                then(v.tensor_tensor(rank[:, :, :], rank[:, :, :], incl[:, :, :], ALU.add))
                then(v.tensor_tensor(rank[:, :, :], rank[:, :, :], tot[:, :, :], ALU.subtract))
                then(v.tensor_tensor(rank[:, :, :], rank[:, :, :], over_tiles(offs[:, :]), ALU.add))
                then(v.tensor_tensor(mp[:, :, :], rank[:, :, :], masks[:, :, :], ALU.mult))
                then(v.tensor_reduce(sl[:, :, 1], mp[:, :, :], AX.X, ALU.max))
                then(v.tensor_reduce(sm[:, :], mp[:, :, :], AX.X, ALU.add))
                then(v.tensor_tensor(sl[:, :, 0], sm[:, :], sl[:, :, 1], ALU.subtract))
                then(v.tensor_copy(slot[:, :, :], sl[:, :, :]))
                core.slots_at = done[0]
                for i in range(2):
                    then(v.tensor_tensor(mp[:, :, :], rank[:, :, :], over_experts(sl[:, :, i]), ALU.is_equal))
                    then(v.tensor_tensor(mp[:, :, :], mp[:, :, :], gates[:, :, :], ALU.mult))
                    then(v.tensor_reduce(share[:, :, i], mp[:, :, :], AX.X, ALU.add))
                then(v.tensor_tensor(past[:, :, :], number[:, :, :], cum[:, :].unsqueeze(1).to_broadcast([P, MTILES, E1]),
                                     ALU.is_ge))
                then(v.tensor_reduce(te[:, :], past[:, :, :], AX.X, ALU.add))
                then(v.tensor_scalar(te[:, :], te[:, :], float(E1 - 1), None, ALU.min))
                then(v.tensor_copy(tile_expert[:, :], te[:, :]))

            @block.gpsimd
            def _(pool):
                pool.wait_ge(step, core.slots_at)
                for t in range(TILES):
                    for i in range(2):
                        pool.indirect_dma_start(out=a["rows_in"], out_offset=bass.IndirectOffsetOnAxis(ap=slot[:, t, i:i + 1], axis=0),
                                                in_=hn[:, t, :], in_offset=None).then_inc(scattered, 16)
                pool.wait_ge(scattered, 2 * TILES * 16)
        bk.close(1)
    core.end_phase()


def experts(core, a, tile_expert):
    nc = core.nc
    NJ = 2 * FB
    SL = 4
    PAIRS = MTILES // 2
    assert MTILES % 2 == 1
    with ExitStack() as ctx:
        def sb(name, shape, dt):
            return ctx.enter_context(nc.sbuf_tensor(name, shape, dt))

        w = sb("ex_weights", [P, E1 * 2 * WX], F16)
        xin = sb("ex_rows", [P, 2, 2, D], F32)
        xh = sb("ex_xh", [P, 2, KD, MT], F16)
        xl = sb("ex_xl", [P, 2, KD, MT], F16)
        sil = sb("ex_silu", [P, SL, MT], F32)
        uu = sb("ex_u", [P, SL, MT], F32)
        uh = sb("ex_uh", [P, SL, MT], F16)
        ul = sb("ex_ul", [P, SL, MT], F16)
        yo = sb("ex_y", [P, 2, 2, D], F32)

        jobs = [(("x", 0), 0), (("x", 1), 1), (("y", 0), 6), (("y", 1), 7)]
        jobs += [(("p", j), 2 + j % 4) for j in range(NJ)]
        bk = Banks(core, jobs)
        s_w = core.sem("ex_weights_loading")
        s_wr = core.sem("ex_experts_ready")
        s_x = Loads(core, "ex_rows_loaded", 2)
        s_yo = [core.sem(f"ex_y_stored_{i}") for i in range(2)]
        s_xh = Stage(core, "ex_xh_done", 2)
        s_sil = Stage(core, "ex_silu_done", NJ)
        s_uh = Stage(core, "ex_uh_done", NJ)
        s_ul = Stage(core, "ex_ul_done", NJ, base=NJ)
        s_dn = Stage(core, "ex_down_done", NJ - 2, base=NJ - 2)
        def before(c, j):
            if j >= SL:
                return c, j - SL
            return c - 1, max(i for i in range(NJ) if i % SL == j % SL)

        def down_done(eng, c, j):
            if j % FB == FB - 1:
                eng.wait_ge(bk.full(("y", j // FB)), bk.n_full(c, ("y", j // FB)))
            else:
                eng.wait_ge(s_dn.sem, s_dn.value(c, j - j // FB))

        AHEAD = 2
        TURNS = ((3, 0, 1), (10, 1, 0))

        with nc.Block() as block:
            @block.sync
            def _(sp):
                for i in range(2):
                    sp.sem_inc(s_yo[i], 1)

                turned = [bk.n_full(0, ("x", i)) - 1 for i in range(2)]

                def load(c, i):
                    tile = sp.snap(2 * c + i) if not isinstance(c, int) else 2 * c + i
                    if not (isinstance(c, int) and c == 0):
                        sp.wait_ge(bk.full(("x", i)), c + turned[i])
                    sp.dma_start(xin[:, i, :, :].rearrange("p b d -> p (b d)"),
                                 a["tiles_in"][bass.ds(tile, 1)].rearrange("a p n -> (a p) n")).then_inc(s_x.sems[i], 16)

                def store(c, i):
                    tile = sp.snap(2 * c + i) if not isinstance(c, int) else 2 * c + i
                    sp.wait_ge(bk.drained(("y", i)), bk.n_out(c, ("y", i)))
                    sp.sem_inc(core.sync_waits, 1)
                    sp.dma_start(a["tiles_out"][bass.ds(tile, 1)].rearrange("a p n -> (a p) n"),
                                 yo[:, i, :, :].rearrange("p b d -> p (b d)")).then_inc(s_yo[i], 16)

                load(0, 0)
                for e in range(E1):
                    sp.dma_start(w[:, e * 2 * WX:(e + 1) * 2 * WX], a["wx"][e]).then_inc(s_w, 16)
                    sp.wait_ge(s_w, 16 * (e + 1))
                    sp.sem_inc(s_wr, 1)
                with sp.Fori(0, PAIRS) as c:
                    load(c, 1)
                    load(c + 1, 0)
                    store(c, 0)
                    store(c, 1)
                store(PAIRS, 0)
                sp.wait_ge(s_yo[0], 16 * (PAIRS + 1) + 1)
                sp.wait_ge(s_yo[1], 16 * PAIRS + 1)

            @block.gpsimd
            def _(pool):
                pool.sem_inc(s_ul.sem, NJ)

                def low(c, j):
                    pool.wait_ge(s_uh.sem, s_uh.value(c, j))
                    nc.gpsimd.tensor_tensor(ul[:, j % SL, :], uu[:, j % SL, :], uh[:, j % SL, :], ALU.subtract)\
                        .then_inc(s_ul.sem, 1)

                with pool.Fori(0, PAIRS) as c:
                    for j in range(NJ):
                        low(c, j)
                for j in range(FB):
                    low(PAIRS, j)

            @block.scalar
            def _(act):
                def turn(c, i):
                    act.wait_ge(bk.full(("x", i)), bk.n_full(c, ("x", i)))
                    nc.scalar.copy(xh[:, i, :, :].rearrange("p k t -> p (k t)"), bk.tile(("x", i))[:, :]).then_inc(s_xh.sem, 1)

                def block_of(c, j):
                    pc, pj = before(c, j)
                    act.wait_ge(bk.drained(("p", pj)), bk.n_out(pc, ("p", pj)))
                    act.wait_ge(bk.full(("p", j)), bk.n_full(c, ("p", j)))
                    nc.scalar.activation(sil[:, j % SL, :], bk.tile(("p", j))[:, 0:MT], ACT.Silu, scale=1 / WS)\
                        .then_inc(s_sil.sem, 1)
                    down_done(act, pc, pj)
                    act.wait_ge(bk.drained(("p", j)), bk.n_out(c, ("p", j)))
                    nc.scalar.copy(uh[:, j % SL, :], uu[:, j % SL, :]).then_inc(s_uh.sem, 1)

                turn(0, 0)
                with act.Fori(0, PAIRS) as c:
                    for j in range(NJ):
                        block_of(c, j)
                        for at, dc, i in TURNS:
                            if j == at:
                                turn(c + dc, i)
                for j in range(FB):
                    block_of(PAIRS, j)

            @block.vector
            def _(dve):
                def turn(c, i):
                    dve.wait_ge(s_xh.sem, s_xh.value(c, i))
                    nc.vector.tensor_tensor(xl[:, i, :, :].rearrange("p k t -> p (k t)"), bk.tile(("x", i))[:, :],
                                                       xh[:, i, :, :].rearrange("p k t -> p (k t)"), ALU.subtract)\
                        .then_inc(bk.drained(("x", i)), 1)

                def gated(c, j):
                    pc, pj = before(c, j)
                    dve.wait_ge(s_ul.sem, s_ul.value(pc, pj))
                    dve.wait_ge(s_sil.sem, s_sil.value(c, j))
                    nc.vector.scalar_tensor_tensor(uu[:, j % SL, :], sil[:, j % SL, :], 1 / WS,
                                                   bk.tile(("p", j))[:, MT:2 * MT], ALU.mult, ALU.mult)\
                        .then_inc(bk.drained(("p", j)), 1)

                def result(c, i):
                    dve.wait_ge(s_yo[i], c * 16 + 1)
                    dve.wait_ge(bk.full(("y", i)), bk.n_full(c, ("y", i)))
                    nc.vector.tensor_scalar(yo[:, i, :, :].rearrange("p b d -> p (b d)"), bk.tile(("y", i))[:, :],
                                            1 / WS, None, ALU.mult).then_inc(bk.drained(("y", i)), 1)

                turn(0, 0)
                with dve.Fori(0, PAIRS) as c:
                    for j in range(NJ):
                        gated(c, j)
                        for at, dc, i in TURNS:
                            if j == at:
                                turn(c + dc, i)
                        if j == FB - 1 + AHEAD:
                            result(c, 0)
                    result(c, 1)
                for j in range(FB):
                    gated(PAIRS, j)
                result(PAIRS, 0)

            @block.tensor
            def _(pe):
                pe.sem_inc(s_dn.sem, NJ - 2)

                def choose(c, i):
                    n = 2 * c + i
                    e = pe.value_load(tile_expert[0:1, n:n + 1] if isinstance(n, int) else tile_expert[0:1, bass.ds(n, 1)],
                                      min_val=0, max_val=E1 - 1)
                    pe.wait_ge(s_wr, e + 1)
                    pe.sem_inc(core.tensor_waits, 1)
                    return pe.snap(e * (2 * WX))

                def turn(c, i):
                    pe.wait_ge(s_x.sems[i], s_x.value(c))
                    pe.wait_ge(bk.drained(("x", i)), bk.n_free(c, ("x", i)))
                    for kd in range(KD):
                        for b in range(2):
                            last = nc.tensor.transpose(bk.tile(("x", i))[:, kd * MT + b * P:kd * MT + (b + 1) * P],
                                                       xin[:, i, b, kd * P:(kd + 1) * P], core.ident[:, :])
                    last.then_inc(bk.full(("x", i)), 1)

                def up(c, j, at):
                    i, fb = j // FB, j % FB
                    if fb == 0:
                        pe.wait_ge(bk.drained(("x", i)), bk.n_out(c, ("x", i)))
                        pe.sem_inc(core.tensor_waits, 1)
                    pe.wait_ge(bk.drained(("p", j)), bk.n_free(c, ("p", j)))
                    for which in range(2):
                        for kd in range(KD):
                            cols = (which * KD + kd) * FFN + fb * P
                            last = three(nc, bk.tile(("p", j))[:, which * MT:(which + 1) * MT],
                                         [w[:, bass.ds(at + (s * WX + cols), P)] for s in range(2)],
                                         (xh[:, i, kd, :], xl[:, i, kd, :]), kd == 0, kd == KD - 1)
                    last.then_inc(bk.full(("p", j)), 1)

                def down(c, j, at):
                    i, fb = j // FB, j % FB
                    if fb == 0:
                        pe.wait_ge(bk.drained(("y", i)), bk.n_free(c, ("y", i)))
                    pe.wait_ge(s_ul.sem, s_ul.value(c, j))
                    for b in range(2):
                        last = three(nc, bk.tile(("y", i))[:, b * D:(b + 1) * D],
                                     (uh[:, j % SL, b * P:(b + 1) * P], ul[:, j % SL, b * P:(b + 1) * P]),
                                     [w[:, bass.ds(at + (s * WX + W13 + fb * D), D)] for s in range(2)],
                                     fb == 0 and b == 0, fb == FB - 1 and b == 1)
                    if fb == FB - 1:
                        last.then_inc(bk.full(("y", i)), 1)
                    else:
                        last.then_inc(s_dn.sem, 1)

                turn(0, 0)
                first = choose(0, 0)
                for j in range(AHEAD):
                    up(0, j, first)
                with pe.Fori(0, PAIRS) as c:
                    at = [choose(c, 0), None]
                    for j in range(NJ):
                        if j + AHEAD == FB:
                            at[1] = choose(c, 1)
                        if j + AHEAD == NJ:
                            following = choose(c + 1, 0)
                        if j + AHEAD < NJ:
                            up(c, j + AHEAD, at[(j + AHEAD) // FB])
                        else:
                            up(c + 1, j + AHEAD - NJ, following)
                        for k, dc, i in TURNS:
                            if j + AHEAD == k:
                                turn(c + dc, i)
                        down(c, j, at[j // FB])
                final = choose(PAIRS, 0)
                for j in range(FB):
                    if j + AHEAD < FB:
                        up(PAIRS, j + AHEAD, final)
                    down(PAIRS, j, final)
    core.end_phase()


def combine(core, a, slot, share, out):
    nc = core.nc
    with ExitStack() as ctx:
        def sb(name, shape, dt):
            return ctx.enter_context(nc.sbuf_tensor(name, shape, dt))

        h = sb("cb_h", [P, TILES, D], F32)
        y = sb("cb_y", [P, TILES, 2, D], F32)
        loaded = core.sem("cb_h_loaded")
        gathered = [core.sem(f"cb_gathered_{t}") for t in range(TILES)]
        added = core.sem("cb_added")
        stored = core.sem("cb_stored")
        out_v = out.rearrange("b s d -> (b s) d").rearrange("(t p) d -> p t d", p=P)
        with nc.Block() as block:
            @block.sync
            def _(sp):
                sp.dma_start(h[:, :, :], a["h_rows"]).then_inc(loaded, 16)
                for t in range(0, TILES, U):
                    sp.wait_ge(added, 2 * (t + U))
                    sp.dma_start(out_v[:, t:t + U, :], h[:, t:t + U, :]).then_inc(stored, 16)
                sp.wait_ge(stored, 16 * CHUNKS)

            @block.gpsimd
            def _(pool):
                for t in range(TILES):
                    for i in range(2):
                        pool.indirect_dma_start(out=y[:, t, i, :], out_offset=None, in_=a["rows_out"],
                                                in_offset=bass.IndirectOffsetOnAxis(ap=slot[:, t, i:i + 1], axis=0))\
                            .then_inc(gathered[t], 16)

            @block.vector
            def _(dve):
                dve.wait_ge(loaded, 16)
                for t in range(TILES):
                    dve.wait_ge(gathered[t], 32)
                    for i in range(2):
                        if i:
                            dve.wait_ge(added, 2 * t + 1)
                        nc.vector.scalar_tensor_tensor(h[:, t, :], y[:, t, i, :], share[:, t, i:i + 1], h[:, t, :],
                                                       ALU.mult, ALU.add).then_inc(added, 1)
    core.end_phase()


UPTO = 5


def store_rows(core, out):
    nc = core.nc
    stored = core.sem("rows_stored")
    with nc.Block() as block:
        @block.sync
        def _(sp):
            sp.dma_start(out.rearrange("b s d -> (b s) d").rearrange("(t p) d -> p t d", p=P), core.h[:, 0:TILES, :]).then_inc(stored, 16)
            sp.wait_ge(stored, 16)


def program(nc, a, out, upto):
    with ExitStack() as ctx:
        core = Core(nc, ctx)
        slot = core.sb("slot", [P, TILES, 2], I32)
        share = core.sb("share", [P, TILES, 2], F32)
        tile_expert = core.sb("tile_expert", [P, MTILES], I32)
        with ExitStack() as rows:
            core.h = rows.enter_context(nc.sbuf_tensor("h", [P, TILES + U, D], F32))
            prepare(core, a)
            attn0(core, a)
            if upto > 1:
                ffn0(core, a)
            if upto > 2:
                attn1(core, a)
            if upto > 3:
                hn = rows.enter_context(nc.sbuf_tensor("hn", [P, TILES, D], F32))
                gates = rows.enter_context(nc.sbuf_tensor("gates", [P, TILES, 8], F32))
                masks = rows.enter_context(nc.sbuf_tensor("expert_masks", [P, TILES, 8], F32))
                block1(core, a, hn, gates, masks)
            if upto < 5:
                store_rows(core, out)
                return
            route(core, a, hn, gates, masks, slot, share, tile_expert)
        experts(core, a, tile_expert)
        combine(core, a, slot, share, out)


def constants():
    p = np.arange(P)
    eye = np.eye(P, dtype=np.float32)
    hm = (p[:, None] // 16 == np.arange(8)[None, :]).astype(np.float32)
    vm = (p[:, None] // SEQ == (np.arange(D)[None, :] // 16) % 2).astype(np.float32)
    rows = np.zeros((16, 8, P), np.float16)
    for e in range(8):
        rows[[e, 8 + e], e, :] = 1
    pos = (p % SEQ).astype(np.float32)[:, None]
    ang = pos * np.power(np.float32(10000.0), -(np.arange(32, dtype=np.float32) / np.float32(32)))[None, :]
    cos, sin = np.cos(ang), np.sin(ang)
    rot = np.stack([np.concatenate([cos, cos], 1), np.concatenate([-sin, -sin], 1), np.concatenate([sin, sin], 1)], 1)
    inv = np.float32(1.0) / np.power(np.float32(1000000.0), np.arange(0, P, 2, dtype=np.float32) / np.float32(P))
    ang = pos * inv[None, :]
    cos, sin = np.cos(ang), np.sin(ang)
    rot2 = np.stack([np.concatenate([cos, cos], 1), np.concatenate([-sin, sin], 1)], 1)
    seen = (p[:, None] // SEQ == p[None, :] // SEQ) & (p[None, :] <= p[:, None])
    mask = np.where(seen, 0.0, NEG).astype(np.float32)
    before = (p[:, None] < p[None, :]).astype(np.float32)
    number = np.repeat(np.arange(MTILES, dtype=np.float32)[:, None], E1, 1)
    return {"before": before, "tile_number": number, "rot_a1": rot.astype(np.float32), "rot_b1": rot2.astype(np.float32), "causal_mask": mask, "ident": eye, "ident16": eye.astype(np.float16), "head_mask": hm, "v_mask": vm, "expert_rows": rows}


def kernel(**inputs):
    import numpy as _np
    import concourse.bacc as _bacc
    from concourse import mybir as _mybir
    from concourse.bass_utils import run_bass_kernel_spmd as _run

    nc = _bacc.Bacc("TRN2", target_bir_lowering=False, num_devices=1)
    raw = {n: _np.asarray(v) for n, v in inputs.items()}
    lay = dict(constants())
    lay["x"] = raw["x"].reshape(TILES, P).T
    for n in ("L0_attn_Wq", "L0_attn_Wk", "L0_attn_Wv", "L0_attn_Wo"):
        lay[n] = raw[n].T
    for n in ("L0_tok_W", "L0_tok_b", "L0_attn_bv", "L0_attn_bo"):
        lay[n] = raw[n]
    lay["bqk"] = _np.stack([raw["L0_attn_bq"].reshape(KD, P), raw["L0_attn_bk"].reshape(KD, P)]).transpose(2, 0, 1)
    first = 255 - (SEQ - 1)
    relk = _np.concatenate([raw["L0_attn_relative_k"][first:first + 2 * SEQ - 1], _np.zeros((1, 16), _np.float32)])
    lay["relk"] = _np.tile(relk.T, (8, 1))
    relv = _np.concatenate([raw["L0_attn_relative_v"][first:first + 2 * SEQ - 1], _np.zeros((1, 16), _np.float32)])
    none = _np.zeros_like(relv)
    lay["relv"] = _np.stack([_np.concatenate([relv, none], 1), _np.concatenate([none, relv], 1)], 1)
    lay["w_gate_t"] = raw["L1_ffn_w_gate"].T
    for n in inputs:
        if n not in lay and n.startswith(("L0_ffn", "L1")):
            lay[n] = raw[n]
    arrays, a = {}, {}
    for n, v in lay.items():
        v = _np.ascontiguousarray(v)
        arrays["in_" + n] = v
        a[n] = nc.dram_tensor("in_" + n, v.shape, _mybir.dt.from_np(v.dtype), kind="ExternalInput").ap()
    MH = 2 * SEQ * 16
    a["qr"] = nc.dram_tensor("qr", (TILES, P, MH), F32, kind="Internal").ap()
    a["qr_flat"] = a["qr"].rearrange("a p n -> (a p n)")
    a["skew"] = nc.dram_tensor("skew", (U, P, MH), F32, kind="Internal").ap()
    a["skew_flat"] = a["skew"].rearrange("a p n -> (a p n)")
    a["wx"] = nc.dram_tensor("wx", (E1, P, 2 * WX), F16, kind="Internal").ap()
    a["h_rows"] = nc.dram_tensor("h_rows", (P, TILES, D), F32, kind="Internal").ap()
    for n in ("in", "out"):
        rows = nc.dram_tensor("expert_rows_" + n, (MTILES * MT, D), F32, kind="Internal").ap()
        a["rows_" + n] = rows
        a["tiles_" + n] = rows.rearrange("(t p b) d -> t p (b d)", p=P, b=2)
    out = nc.dram_tensor("out_0", (64, SEQ, D), F32, kind="ExternalOutput").ap()
    program(nc, a, out, UPTO)
    r = _run(nc, [arrays], core_ids=[0])
    return r.results[0]["out_0"]
```

```python
import numpy as np
import concourse.bass as bass
from concourse import mybir
from contextlib import ExitStack

F32 = mybir.dt.float32
F16 = mybir.dt.float16
I32 = mybir.dt.int32
U32 = mybir.dt.uint32
ALU = mybir.AluOpType
ACT = mybir.ActivationFunctionType
AX = mybir.AxisListType

P = 128
SEQ = 64
TOKENS = 64 * SEQ
TILES = TOKENS // P
U = 4
CHUNKS = TILES // U
CT = U * P
D = 256
KD = D // P
EPS = 1e-5
WS = 256.0
ROUND = 12582912.0
NEG = -1e30


class Stage:

    def __init__(self, core, name, per=U, base=0):
        self.sem, self.per, self.base = core.sem(name), per, base

    def value(self, c, k):
        return c * self.per + (self.base + k + 1)


class Loads:

    def __init__(self, core, name, slots=U, parts=1):
        self.parts = parts
        self.sems = [core.sem(f"{name}_{k}") for k in range(slots)]

    def value(self, c):
        return (c + 1) * (16 * self.parts)


class Banks:

    def __init__(self, core, jobs):
        self.core, self.at, self.uses = core, {}, [0] * 8
        for n, bank in jobs:
            assert n not in self.at, n
            self.at[n] = (bank, self.uses[bank])
            self.uses[bank] += 1
        self.base = list(core.bank_uses)

    def tile(self, job):
        return self.core.psum[self.at[job][0]]

    def full(self, job):
        return self.core.full[self.at[job][0]]

    def drained(self, job):
        return self.core.drained[self.at[job][0]]

    def n_full(self, c, job):
        b, k = self.at[job]
        return c * self.uses[b] + (self.base[b] + k + 1)

    def n_free(self, c, job):
        b, k = self.at[job]
        return c * self.uses[b] + (self.base[b] + k + 1)

    def n_out(self, c, job):
        return self.n_free(c, job) + 1

    def close(self, chunks):
        for b in range(8):
            self.core.bank_uses[b] += chunks * self.uses[b]


def ring(jobs, banks):
    return [(j, banks[i % len(banks)]) for i, j in enumerate(jobs)]


class Core:

    def __init__(self, nc, ctx):
        self.nc, self.ctx, self.of_phase = nc, ctx, []
        self.psum = [ctx.enter_context(nc.psum_tensor(f"bank{b}", [P, 512], F32)) for b in range(8)]
        self.full = [self.sem(f"bank{b}_full") for b in range(8)]
        self.drained = [self.sem(f"bank{b}_drained") for b in range(8)]
        self.sync_waits = self.sem("sync_waits_passed")
        self.vector_waits = self.sem("vector_waits_passed")
        self.pool_waits = self.sem("pool_waits_passed")
        self.tensor_waits = self.sem("tensor_waits_passed")
        self.of_phase = []
        self.bank_uses = [0] * 8
        self.ident = self.sb("ident", [P, P], F32)
        self.mhalf = self.sb("minus_half", [P, U], F32)
        self.eps = self.sb("eps", [P, U], F32)

    def sem(self, name):
        self.of_phase.append(self.nc.alloc_semaphore(name))
        return self.of_phase[-1]

    def end_phase(self):
        self.nc.clear_and_free_semaphores(self.of_phase)
        self.nc.all_engine_barrier()
        self.of_phase = []

    def sb(self, name, shape, dt):
        return self.ctx.enter_context(self.nc.sbuf_tensor(name, shape, dt))


def chunk_ends(core, phase, engines):
    return {n: core.sem(f"{phase}_{n}_chunks_ended") for n in engines}


class Norm:

    def __init__(self, core, phase, sb, per_xn=U):
        nc = core.nc
        self.core = core
        self.st = sb(f"{phase}_stats", [P, U, 6], F32)
        self.mv = sb(f"{phase}_mean_var", [P, U, 2], F32)
        self.ve = sb(f"{phase}_var_eps", [P, U], F32)
        self.rs = sb(f"{phase}_rstd", [P, U], F32)
        self.xn = sb(f"{phase}_xn", [P, U, D], F32)
        self.s_st = Stage(core, f"{phase}_stats_done")
        self.s_mv = Stage(core, f"{phase}_mean_var_done")
        self.s_ve = Stage(core, f"{phase}_var_eps_done", 1)
        self.s_rs = Stage(core, f"{phase}_rstd_done", 1)
        self.s_xn = Stage(core, f"{phase}_xn_done", per_xn)

    def vector(self, dve, c, rows):
        self.vector_stats(dve, c, rows)
        self.vector_rows(dve, c, rows)

    def vector_stats(self, dve, c, rows):
        nc = self.core.nc
        dve.sem_inc(self.core.vector_waits, 1)
        for u in range(U):
            nc.vector.bn_stats(self.st[:, u, :], rows(c, u)).then_inc(self.s_st.sem, 1)
        for u in range(U):
            dve.wait_ge(self.s_st.sem, self.s_st.value(c, u))
            dve.sem_inc(self.core.vector_waits, 1)
            nc.vector.bn_aggr(self.mv[:, u, :], self.st[:, u, :]).then_inc(self.s_mv.sem, 1)

    def vector_rows(self, dve, c, rows):
        nc = self.core.nc
        dve.wait_ge(self.s_rs.sem, self.s_rs.value(c, 0))
        for u in range(U):
            nc.vector.tensor_scalar(self.xn[:, u, :], rows(c, u), self.mv[:, u, 0:1], self.rs[:, u:u + 1],
                                    ALU.subtract, ALU.mult).then_inc(self.s_xn.sem, 1)

    def gpsimd(self, pool, c):
        nc = self.core.nc
        pool.wait_ge(self.s_mv.sem, self.s_mv.value(c, U - 1))
        nc.gpsimd.tensor_tensor(self.ve[:, :], self.mv[:, :, 1], self.core.eps[:, :], ALU.add).then_inc(self.s_ve.sem, 1)
        pool.wait_ge(self.s_ve.sem, self.s_ve.value(c, 0))
        nc.gpsimd.tensor_tensor(self.rs[:, :], self.ve[:, :], self.core.mhalf[:, :], ALU.pow).then_inc(self.s_rs.sem, 1)


class Transposed:

    def __init__(self, core, phase, sb, job="x"):
        self.core, self.job = core, job
        self.xh = sb(f"{phase}_xh", [P, KD, CT], F16)
        self.xl = sb(f"{phase}_xl", [P, KD, CT], F16)
        self.s_xh = Stage(core, f"{phase}_xh_done", KD)

    def tensor(self, pe, c, banks, xn, s_xn, bc=None):
        nc, bc = self.core.nc, c if bc is None else bc
        for kd in range(KD):
            pe.wait_ge(banks.drained((self.job, kd)), banks.n_free(bc, (self.job, kd)))
            for u in range(U):
                pe.wait_ge(s_xn.sem, s_xn.value(c, u))
                last = nc.tensor.transpose(banks.tile((self.job, kd))[:, u * P:(u + 1) * P],
                                           xn[:, u, kd * P:(kd + 1) * P], self.core.ident[:, :])
            last.then_inc(banks.full((self.job, kd)), 1)

    def scalar(self, act, c, banks, bc=None):
        bc = c if bc is None else bc
        for kd in range(KD):
            act.wait_ge(banks.full((self.job, kd)), banks.n_full(bc, (self.job, kd)))
            self.core.nc.scalar.activation(self.xh[:, kd, :], banks.tile((self.job, kd))[:, :], ACT.Copy)\
                .then_inc(self.s_xh.sem, 1)

    def vector(self, dve, c, banks, bc=None):
        for kd in range(KD):
            dve.wait_ge(self.s_xh.sem, self.s_xh.value(c, kd))
            self.core.nc.vector.tensor_tensor(self.xl[:, kd, :], banks.tile((self.job, kd))[:, :],
                                                            self.xh[:, kd, :], ALU.subtract)\
                .then_inc(banks.drained((self.job, kd)), 1)


def three(nc, out, a, b, start, stop):
    nc.tensor.matmul(out, a[0], b[0], start=start, stop=False)
    nc.tensor.matmul(out, a[0], b[1], start=False, stop=False)
    return nc.tensor.matmul(out, a[1], b[0], start=False, stop=stop)


def prepare(core, a):
    nc = core.nc
    with ExitStack() as ctx:
        idx = ctx.enter_context(nc.sbuf_tensor("token_ids", [P, TILES], I32))
        loaded = core.sem("ids_loaded")
        gathered = core.sem("rows_gathered")
        filled = core.sem("constants_filled")
        with nc.Block() as block:
            @block.sync
            def _(sp):
                sp.dma_start(idx[:, :], a["x"]).then_inc(loaded, 16)
                sp.dma_start(core.ident[:, :], a["ident"]).then_inc(loaded, 16)

            @block.vector
            def _(dve):
                nc.vector.memset(core.h[:, TILES:TILES + U, :], 0.0)

            @block.gpsimd
            def _(pool):
                pool.memset(core.mhalf[:, :], -0.5).then_inc(filled, 1)
                pool.memset(core.eps[:, :], EPS).then_inc(filled, 1)
                pool.wait_ge(loaded, 32)
                for t in range(TILES):
                    pool.indirect_dma_start(out=core.h[:, t, :], out_offset=None, in_=a["L0_tok_W"],
                                            in_offset=bass.IndirectOffsetOnAxis(ap=idx[:, t:t + 1], axis=0))\
                        .then_inc(gathered, 16)
                pool.wait_ge(gathered, 16 * TILES)

            @block.tensor
            def _(pe):
                for b in range(8):
                    pe.sem_inc(core.drained[b], 1)
    core.end_phase()


def attn0(core, a):
    nc = core.nc
    H, DK = 16, 16
    HB = P // DK
    M = 2 * SEQ
    with ExitStack() as ctx:
        def sb(name, shape, dt):
            return ctx.enter_context(nc.sbuf_tensor(name, shape, dt))

        stage = sb("a0_stage", [P, 4, KD, D], F32)
        wh = sb("a0_wh", [P, 4, KD, D], F16)
        wl = sb("a0_wl", [P, 4, KD, D], F16)
        tokb = sb("a0_tokb", [P, D], F32)
        bv = sb("a0_bv", [P, D], F32)
        bo = sb("a0_bo", [P, D], F32)
        bqk = sb("a0_bqk", [P, 2, KD], F32)
        hmask = sb("a0_head_mask", [P, HB], F32)
        vmask = sb("a0_v_mask", [P, D], F32)
        relk = sb("a0_relk", [P, M], F32)
        rk = sb("a0_relk_diag", [P, M, HB], F32)
        rv = sb("a0_relv", [P, 2, 2 * DK], F32)
        nrm = Norm(core, "a0", sb)
        xt = Transposed(core, "a0", sb)
        q = sb("a0_q", [P, KD, CT], F32)
        k = sb("a0_k", [P, KD, CT], F32)
        kdg = sb("a0_k_diag", [P, 2 * U, KD, HB, SEQ], F32)
        v2 = sb("a0_v2", [P, 2 * U, D], F32)
        qr = sb("a0_qr", [P, U, M, H], F32)
        srel = sb("a0_srel", [P, U, SEQ, H], F32)
        s = sb("a0_s", [P, U, H, SEQ], F32)
        pp = qr
        mx = sb("a0_max", [P, U, H], F32)
        sm = sb("a0_sum", [P, U, H], F32)
        rc = sb("a0_rsum", [P, U, H], F32)
        at = sb("a0_at", [P, U, H // 2, P], F32)
        pt = kdg[:, :, :, :, :].rearrange("p b k h r -> p (b k h r)").rearrange("p (u h t) -> p u h t", u=U, h=H)
        oh = sb("a0_oh", [P, U, KD, P], F16)
        ol = sb("a0_ol", [P, U, KD, P], F16)

        front = [("x", kd) for kd in range(KD)] + [("q", i) for i in range(4)]
        bk0 = Banks(core, ring(front, range(8)))
        bk0.close(1)
        jobs = ring([("qr", u, i) for u in range(U) for i in range(4)] + [("v", i) for i in range(U)]
                    + [("s", u, i) for u in range(U) for i in range(2)] + front
                    + [("at", u, i) for u in range(U) for i in range(2)]
                    + [(n, v, i) for u in range(U + 1) for n, v, m in (("pt", u, 4), ("o", u, 1), ("y", u - 1, 1))
                       if 0 <= v < U for i in range(m)], range(8))
        bk = Banks(core, jobs)
        ends = chunk_ends(core, "a0", ["pe", "act", "dve", "pool", "sp"])
        loaded = core.sem("a0_loaded")
        wh_done = core.sem("a0_wh_done")
        w_done = core.sem("a0_w_done")
        masks = core.sem("a0_rk_done")
        pz = core.sem("a0_zeros_filled")
        pzo = core.sem("a0_zeros_stored")
        s_hb = Stage(core, "a0_h_biased")
        s_vb = Stage(core, "a0_v_masked", 2 * U)
        s_kdd = Stage(core, "a0_k_diag_even_done", U)
        s_kdp = Stage(core, "a0_k_diag_odd_done", U)
        s_qo = Loads(core, "a0_qr_stored")
        s_sr = Loads(core, "a0_srel_loaded", U, 2)
        s_mx = Stage(core, "a0_max_done")
        s_sub = Stage(core, "a0_sub_done")
        s_ex = Stage(core, "a0_exp_done")
        s_sm = Stage(core, "a0_sum_done")
        s_rc = Stage(core, "a0_rsum_done")
        s_pr = Stage(core, "a0_probs_done")
        s_rh = Stage(core, "a0_probs_by_distance_done")
        s_po = Loads(core, "a0_probs_stored", U, 2)
        s_pp = Loads(core, "a0_skewed_loaded")
        s_oh = Stage(core, "a0_oh_done")
        s_hy = Stage(core, "a0_h_added")

        def row(c, u):
            return core.h[:, bass.ds(c * U + u, 1), :].rearrange("p a d -> p (a d)")

        def k_diag(eng, t):
            return eng.tensor_tensor(kdg[:, t, :, :, :],
                                     k[:, :, t * SEQ:(t + 1) * SEQ].unsqueeze(2).to_broadcast([P, KD, HB, SEQ]),
                                     hmask[:, :].unsqueeze(1).unsqueeze(3).to_broadcast([P, KD, HB, SEQ]), ALU.mult)

        def heads(x):
            return x.rearrange("p r h -> p h r")

        def copy_qr(copy, u, i):
            kd, m = i // 2, i % 2
            return copy(qr[:, u, m * SEQ:(m + 1) * SEQ, kd * HB:(kd + 1) * HB],
                        bk.tile(("qr", u, i))[:, :].rearrange("p (m h) -> p m h", h=HB))

        def total(dve, c, u):
            dve.wait_ge(s_ex.sem, s_ex.value(c, u))
            nc.vector.tensor_reduce(sm[:, u, :], s[:, u, :, :], AX.X, ALU.add).then_inc(s_sm.sem, 1)
            dve.wait_ge(s_sm.sem, s_sm.value(c, u))
            nc.vector.reciprocal(rc[:, u, :], sm[:, u, :]).then_inc(s_rc.sem, 1)

        def project(pe, c, u):
            pe.wait_ge(bk.drained(("o", u, 0)), bk.n_out(c, ("o", u, 0)))
            pe.wait_ge(bk.drained(("y", u, 0)), bk.n_free(c, ("y", u, 0)))
            for kd in range(KD):
                last = three(nc, bk.tile(("y", u, 0))[:, 0:D], (oh[:, u, kd, :], ol[:, u, kd, :]),
                             (wh[:, 3, kd, :], wl[:, 3, kd, :]), kd == 0, kd == KD - 1)
            last.then_inc(bk.full(("y", u, 0)), 1)

        def add_y(dve, c, u):
            dve.wait_ge(bk.full(("y", u, 0)), bk.n_full(c, ("y", u, 0)))
            nc.vector.scalar_tensor_tensor(row(c, u), bk.tile(("y", u, 0))[:, 0:D], 1 / WS, row(c, u),
                                                      ALU.mult, ALU.add)\
                .then_inc(bk.drained(("y", u, 0)), 1)
            dve.wait_ge(bk.drained(("y", u, 0)), bk.n_out(c, ("y", u, 0)))
            nc.vector.tensor_tensor(row(c, u), row(c, u), bo[:, :], ALU.add).then_inc(s_hy.sem, 1)

        def biased(dve, c):
            for u in range(U):
                nc.vector.tensor_tensor(row(c, u), row(c, u), tokb[:, :], ALU.add).then_inc(s_hb.sem, 1)
            dve.wait_ge(s_hb.sem, s_hb.value(c, U - 1))

        def query_key(act, bc, banks, i):
            dst = (q, k)[i // KD]
            act.wait_ge(banks.full(("q", i)), banks.n_full(bc, ("q", i)))
            nc.scalar.activation(dst[:, i % KD, :], banks.tile(("q", i))[:, :], ACT.Identity,
                                 bias=bqk[:, i // KD, i % KD:i % KD + 1], scale=1 / WS)\
                .then_inc(banks.drained(("q", i)), 1)

        def by_distance(act, c, u):
            act.wait_ge(s_pr.sem, s_pr.value(c, u))
            nc.scalar.copy(heads(srel[:, u, :, :]), s[:, u, :, :]).then_inc(s_rh.sem, 1)

        def make_front(pe, c, banks, bc):
            xt.tensor(pe, c, banks, nrm.xn, nrm.s_xn, bc)
            for kd in range(KD):
                pe.wait_ge(banks.drained(("x", kd)), banks.n_out(bc, ("x", kd)))
            for i in range(4):
                w, o = i // KD, i % KD
                pe.wait_ge(banks.drained(("q", i)), banks.n_free(bc, ("q", i)))
                for kd in range(KD):
                    last = three(nc, banks.tile(("q", i))[:, :],
                                 (wh[:, w, kd, o * P:(o + 1) * P], wl[:, w, kd, o * P:(o + 1) * P]),
                                 (xt.xh[:, kd, :], xt.xl[:, kd, :]), kd == 0, kd == KD - 1)
                last.then_inc(banks.full(("q", i)), 1)

        def wait_front(eng, passed, banks, bc, js):
            for i in js:
                eng.wait_ge(banks.drained(("q", i)), banks.n_out(bc, ("q", i)))
                eng.sem_inc(passed, 1)

        with nc.Block() as block:
            @block.sync
            def _(sp):
                for i, w in enumerate(("L0_attn_Wq", "L0_attn_Wk", "L0_attn_Wv", "L0_attn_Wo")):
                    sp.dma_start(stage[:, i, :, :], a[w].rearrange("(k p) n -> p k n", p=P)).then_inc(loaded, 16)
                sp.dma_start(tokb[:, :], a["L0_tok_b"].partition_broadcast(P)).then_inc(loaded, 16)
                sp.dma_start(bv[:, :], a["L0_attn_bv"].partition_broadcast(P)).then_inc(loaded, 16)
                sp.dma_start(bo[:, :], a["L0_attn_bo"].partition_broadcast(P)).then_inc(loaded, 16)
                sp.dma_start(bqk[:, :, :], a["bqk"]).then_inc(loaded, 16)
                sp.dma_start(hmask[:, :], a["head_mask"]).then_inc(loaded, 16)
                sp.dma_start(vmask[:, :], a["v_mask"]).then_inc(loaded, 16)
                sp.dma_start(relk[:, :], a["relk"]).then_inc(loaded, 16)
                sp.dma_start(rv[:, :, :], a["relv"]).then_inc(loaded, 16)
                sp.wait_ge(pz, 1)
                for u in range(U):
                    sp.dma_start(a["skew"][u], qr[:, u, :, :].rearrange("p m h -> p (m h)")).then_inc(pzo, 16)
                sp.wait_ge(pzo, 16 * U)
                with sp.Fori(0, CHUNKS) as c:
                    for u in range(U):
                        tile = sp.snap(c * U + u)
                        for i in range(4):
                            sp.wait_ge(bk.drained(("qr", u, i)), bk.n_out(c, ("qr", u, i)))
                            sp.sem_inc(core.sync_waits, 1)
                        sp.dma_start(a["qr"][bass.ds(tile, 1)].rearrange("a p n -> (a p) n"),
                                     qr[:, u, :, :].rearrange("p m h -> p (m h)")).then_inc(s_qo.sems[u], 16)
                    for u in range(U):
                        starts = [sp.snap((c * U + u) * (P * M * H) + b * SEQ * M * H + (SEQ - 1) * H) for b in range(2)]
                        sp.wait_ge(s_qo.sems[u], s_qo.value(c))
                        sp.sem_inc(core.sync_waits, 1)
                        for b in range(2):
                            src = a["qr_flat"][bass.ds(starts[b], SEQ * (M * H - H))]
                            sp.dma_start(srel[b * SEQ:(b + 1) * SEQ, u, :, :].rearrange("p r h -> p (r h)"),
                                         src.rearrange("(l n) -> l n", n=M * H - H)[:, 0:SEQ * H])\
                                .then_inc(s_sr.sems[u], 16)
                    for u in range(U):
                        sp.wait_ge(s_rh.sem, s_rh.value(c, u))
                        sp.sem_inc(core.sync_waits, 1)
                        for b in range(2):
                            base = u * P * M * H + b * SEQ * M * H + (SEQ - 1) * H
                            dst = a["skew_flat"][base:base + SEQ * (M * H - H)]
                            sp.dma_start(dst.rearrange("(l n) -> l n", n=M * H - H)[:, 0:SEQ * H],
                                         srel[b * SEQ:(b + 1) * SEQ, u, :, :].rearrange("p r h -> p (r h)"))\
                                .then_inc(s_po.sems[u], 16)
                        sp.wait_ge(s_po.sems[u], s_po.value(c))
                        sp.sem_inc(core.sync_waits, 1)
                        sp.dma_start(pp[:, u, :, :].rearrange("p m h -> p (m h)"), a["skew"][u]).then_inc(s_pp.sems[u], 16)
                    for u in range(U):
                        sp.wait_ge(s_pp.sems[u], s_pp.value(c))
                        sp.sem_inc(core.sync_waits, 1)
                    sp.sem_inc(ends["sp"], 1)
                    for n in ends:
                        if n != "sp":
                            sp.wait_ge(ends[n], c + 1)
                            sp.sem_inc(core.sync_waits, 1)

            @block.gpsimd
            def _(pool):
                pool.memset(qr[:, :, :, :].rearrange("p u m h -> p (u m h)"), 0.0).then_inc(pz, 1)
                pool.wait_ge(loaded, 12 * 16)
                nc.gpsimd.tensor_tensor(rk[:, :, :], relk[:, :].unsqueeze(2).to_broadcast([P, M, HB]),
                                        hmask[:, :].unsqueeze(1).to_broadcast([P, M, HB]), ALU.mult).then_inc(masks, 1)
                nrm.gpsimd(pool, 0)
                pool.wait_ge(pzo, 16 * U)
                wait_front(pool, core.pool_waits, bk0, 0, (2, 3))
                with pool.Fori(0, CHUNKS) as c:
                    for t in range(1, 2 * U, 2):
                        k_diag(nc.gpsimd, t).then_inc(s_kdp.sem, 1)
                    nrm.gpsimd(pool, c + 1)
                    for t in range(2 * U):
                        if t % 2 == 0:
                            pool.wait_ge(bk.drained(("v", t // 2)), bk.n_out(c, ("v", t // 2)))
                        nc.gpsimd.tensor_tensor(v2[:, t, :], v2[:, t, :], vmask[:, :], ALU.mult).then_inc(s_vb.sem, 1)
                    for u in range(U):
                        pool.wait_ge(s_rc.sem, s_rc.value(c, u))
                        nc.gpsimd.tensor_tensor(s[:, u, :, :], s[:, u, :, :],
                                                rc[:, u, :].unsqueeze(2).to_broadcast([P, H, SEQ]), ALU.mult)\
                            .then_inc(s_pr.sem, 1)
                    wait_front(pool, core.pool_waits, bk, c, (2, 3))
                    pool.drain().then_inc(ends["pool"], 1)
                    for n in ends:
                        if n != "pool":
                            pool.wait_ge(ends[n], c + 1)

            @block.scalar
            def _(act):
                act.wait_ge(loaded, 12 * 16)
                flat = "p w k n -> p (w k n)"
                nc.scalar.activation(wh[:, :, :, :].rearrange(flat), stage[:, :, :, :].rearrange(flat), ACT.Copy,
                                     scale=WS).then_inc(wh_done, 1)
                xt.scalar(act, 0, bk0)
                for i in range(4):
                    query_key(act, 0, bk0, i)
                with act.Fori(0, CHUNKS) as c:
                    for u in range(U):
                        for i in (0, 2):
                            act.wait_ge(bk.full(("qr", u, i)), bk.n_full(c, ("qr", u, i)))
                            copy_qr(nc.scalar.copy, u, i).then_inc(bk.drained(("qr", u, i)), 1)
                    for u in range(U):
                        act.wait_ge(s_sub.sem, s_sub.value(c, u))
                        nc.scalar.activation(s[:, u, :, :], s[:, u, :, :], ACT.Exp).then_inc(s_ex.sem, 1)
                        if u == 0:
                            xt.scalar(act, c + 1, bk, c)
                        if u == 2:
                            query_key(act, c, bk, 0)
                            by_distance(act, c, 0)
                            query_key(act, c, bk, 1)
                    by_distance(act, c, 1)
                    query_key(act, c, bk, 2)
                    by_distance(act, c, 2)
                    query_key(act, c, bk, 3)
                    by_distance(act, c, 3)
                    for u in range(U):
                        act.wait_ge(bk.full(("at", u, 0)), bk.n_full(c, ("at", u, 0)))
                        nc.scalar.copy(at[:, u, 0:4, :].rearrange("p h t -> p (h t)"),
                                                  bk.tile(("at", u, 0))[:, :])\
                            .then_inc(bk.drained(("at", u, 0)), 1)
                    for u in range(U):
                        for i in range(3):
                            act.wait_ge(bk.full(("pt", u, i)), bk.n_full(c, ("pt", u, i)))
                            nc.scalar.copy(pt[:, u, 4 * i:4 * i + 4, :].rearrange("p h t -> p (h t)"),
                                                      bk.tile(("pt", u, i))[:, :])\
                                .then_inc(bk.drained(("pt", u, i)), 1)
                        act.wait_ge(bk.full(("o", u, 0)), bk.n_full(c, ("o", u, 0)))
                        nc.scalar.copy(oh[:, u, :, :].rearrange("p k t -> p (k t)"), bk.tile(("o", u, 0))[:, 0:D])\
                            .then_inc(s_oh.sem, 1)
                    act.drain().then_inc(ends["act"], 1)
                    for n in ends:
                        if n != "act":
                            act.wait_ge(ends[n], c + 1)

            @block.vector
            def _(dve):
                dve.wait_ge(loaded, 12 * 16)
                dve.wait_ge(wh_done, 1)
                flat = "p w k n -> p (w k n)"
                nc.vector.scalar_tensor_tensor(wl[:, :, :, :].rearrange(flat), stage[:, :, :, :].rearrange(flat), WS,
                                               wh[:, :, :, :].rearrange(flat), ALU.mult, ALU.subtract).then_inc(w_done, 1)
                biased(dve, 0)
                nrm.vector(dve, 0, row)
                xt.vector(dve, 0, bk0)
                wait_front(dve, core.vector_waits, bk0, 0, (2, 3))
                with dve.Fori(0, CHUNKS) as c:
                    for u in range(U):
                        k_diag(nc.vector, 2 * u).then_inc(s_kdd.sem, 1)
                        for i in (1, 3):
                            dve.wait_ge(bk.full(("qr", u, i)), bk.n_full(c, ("qr", u, i)))
                            copy_qr(nc.vector.tensor_copy, u, i).then_inc(bk.drained(("qr", u, i)), 1)
                    for i in range(U):
                        dve.wait_ge(bk.full(("v", i)), bk.n_full(c, ("v", i)))
                        nc.vector.scalar_tensor_tensor(
                            v2[:, 2 * i:2 * i + 2, :], bk.tile(("v", i))[:, :].rearrange("p (b n) -> p b n", b=2), 1 / WS,
                            bv[:, :].unsqueeze(1).to_broadcast([P, 2, D]), ALU.mult, ALU.add)\
                            .then_inc(bk.drained(("v", i)), 1)
                    biased(dve, c + 1)
                    nrm.vector_stats(dve, c + 1, row)
                    for u in range(U):
                        dve.wait_ge(s_sr.sems[u], s_sr.value(c))
                        for i in range(KD):
                            dve.wait_ge(bk.full(("s", u, i)), bk.n_full(c, ("s", u, i)))
                            hs = slice(i * HB, (i + 1) * HB)
                            nc.vector.scalar_tensor_tensor(
                                s[:, u, hs, :], bk.tile(("s", u, i))[:, :].rearrange("p (h r) -> p h r", h=HB),
                                DK ** -0.5, heads(srel[:, u, :, hs]), ALU.mult, ALU.add)\
                                .then_inc(bk.drained(("s", u, i)), 1)
                        for i in range(KD):
                            dve.wait_ge(bk.drained(("s", u, i)), bk.n_out(c, ("s", u, i)))
                        nc.vector.tensor_reduce(mx[:, u, :], s[:, u, :, :], AX.X, ALU.max).then_inc(s_mx.sem, 1)
                        dve.wait_ge(s_mx.sem, s_mx.value(c, u))
                        nc.vector.tensor_tensor(s[:, u, :, :], s[:, u, :, :],
                                                mx[:, u, :].unsqueeze(2).to_broadcast([P, H, SEQ]), ALU.subtract)\
                            .then_inc(s_sub.sem, 1)
                        if u == 0:
                            nrm.vector_rows(dve, c + 1, row)
                        if u:
                            total(dve, c, u - 1)
                        if u == 1:
                            xt.vector(dve, c + 1, bk, c)
                    total(dve, c, U - 1)
                    for u in range(U):
                        dve.wait_ge(bk.full(("at", u, 1)), bk.n_full(c, ("at", u, 1)))
                        nc.vector.tensor_copy(at[:, u, 4:8, :].rearrange("p h t -> p (h t)"),
                                                         bk.tile(("at", u, 1))[:, :])\
                            .then_inc(bk.drained(("at", u, 1)), 1)
                    for u in range(U):
                        dve.wait_ge(bk.full(("pt", u, 3)), bk.n_full(c, ("pt", u, 3)))
                        nc.vector.tensor_copy(pt[:, u, 12:16, :].rearrange("p h t -> p (h t)"),
                                                         bk.tile(("pt", u, 3))[:, :])\
                            .then_inc(bk.drained(("pt", u, 3)), 1)
                        if u:
                            add_y(dve, c, u - 1)
                        dve.wait_ge(s_oh.sem, s_oh.value(c, u))
                        nc.vector.tensor_tensor(ol[:, u, :, :].rearrange("p k t -> p (k t)"),
                                                           bk.tile(("o", u, 0))[:, 0:D],
                                                           oh[:, u, :, :].rearrange("p k t -> p (k t)"), ALU.subtract)\
                            .then_inc(bk.drained(("o", u, 0)), 1)
                    add_y(dve, c, U - 1)
                    wait_front(dve, core.vector_waits, bk, c, (2, 3))
                    dve.drain().then_inc(ends["dve"], 1)
                    for n in ends:
                        if n != "dve":
                            dve.wait_ge(ends[n], c + 1)

            @block.tensor
            def _(pe):
                pe.wait_ge(w_done, 1)
                pe.wait_ge(masks, 1)
                make_front(pe, 0, bk0, 0)
                pe.wait_ge(pzo, 16 * U)
                wait_front(pe, core.tensor_waits, bk0, 0, range(4))
                with pe.Fori(0, CHUNKS) as c:
                    for u in range(U):
                        for i in range(4):
                            kd, m = i // 2, i % 2
                            pe.wait_ge(bk.drained(("qr", u, i)), bk.n_free(c, ("qr", u, i)))
                            nc.tensor.matmul(bk.tile(("qr", u, i))[:, :], q[:, kd, u * P:(u + 1) * P],
                                                       rk[:, m * SEQ:(m + 1) * SEQ, :].rearrange("p m h -> p (m h)"),
                                                       start=True, stop=True)\
                                .then_inc(bk.full(("qr", u, i)), 1)
                    for i in range(U):
                        pe.wait_ge(bk.drained(("v", i)), bk.n_free(c, ("v", i)))
                        for b in range(2):
                            t = 2 * i + b
                            for e in range(2):
                                for kd in range(KD):
                                    x2 = [x[:, kd, t * SEQ:(t + 1) * SEQ] for x in (xt.xh, xt.xl)]
                                    last = three(nc, bk.tile(("v", i))[e * SEQ:(e + 1) * SEQ, b * D:(b + 1) * D], x2,
                                                 (wh[:, 2, kd, :], wl[:, 2, kd, :]), kd == 0, kd == KD - 1)
                        last.then_inc(bk.full(("v", i)), 1)
                    for u in range(U):
                        pe.wait_ge(s_kdd.sem, s_kdd.value(c, u))
                        pe.wait_ge(s_kdp.sem, s_kdp.value(c, u))
                        for i in range(KD):
                            pe.wait_ge(bk.drained(("s", u, i)), bk.n_free(c, ("s", u, i)))
                            for b in range(2):
                                t = 2 * u + b
                                last = nc.tensor.matmul(bk.tile(("s", u, i))[b * SEQ:(b + 1) * SEQ, :],
                                                        q[:, i, t * SEQ:(t + 1) * SEQ],
                                                        kdg[:, t, i, :, :].rearrange("p h r -> p (h r)"),
                                                        start=True, stop=True)
                            last.then_inc(bk.full(("s", u, i)), 1)
                    make_front(pe, c + 1, bk, c)
                    for u in range(U):
                        pe.wait_ge(s_pr.sem, s_pr.value(c, u))
                        for i in range(2):
                            pe.wait_ge(bk.drained(("at", u, i)), bk.n_free(c, ("at", u, i)))
                            for j in range(4):
                                hh = 2 * (4 * i + j)
                                last = nc.tensor.transpose(bk.tile(("at", u, i))[:, j * P:(j + 1) * P],
                                                           s[:, u, hh:hh + 2, :].rearrange("p h r -> p (h r)"), core.ident[:, :])
                            last.then_inc(bk.full(("at", u, i)), 1)
                    for u in range(U):
                        pe.wait_ge(s_pp.sems[u], s_pp.value(c))
                        for i in range(4):
                            pe.wait_ge(bk.drained(("pt", u, i)), bk.n_free(c, ("pt", u, i)))
                            for j in range(4):
                                last = nc.tensor.transpose(bk.tile(("pt", u, i))[:, j * P:(j + 1) * P],
                                                           pp[:, u, :, 4 * i + j], core.ident[:, :])
                            last.then_inc(bk.full(("pt", u, i)), 1)
                        for i in range(2):
                            pe.wait_ge(bk.drained(("at", u, i)), bk.n_out(c, ("at", u, i)))
                        pe.sem_inc(core.tensor_waits, 1)
                        for i in range(4):
                            pe.wait_ge(bk.drained(("pt", u, i)), bk.n_out(c, ("pt", u, i)))
                        pe.wait_ge(s_vb.sem, s_vb.value(c, 2 * u + 1))
                        pe.wait_ge(bk.drained(("o", u, 0)), bk.n_free(c, ("o", u, 0)))
                        for j in range(H // 2):
                            g, kd = j % 4, j // 4
                            out = bk.tile(("o", u, 0))[32 * g:32 * g + 32, kd * P:(kd + 1) * P]
                            for e in range(2):
                                nc.tensor.matmul(out, rv[:, e, :], pt[:, u, 2 * j + e, :], start=(e == 0), stop=False,
                                                 tile_position=(0, 32 * g))
                            for b in range(2):
                                last = nc.tensor.matmul(out[:, b * SEQ:(b + 1) * SEQ], v2[:, 2 * u + b, 32 * j:32 * j + 32],
                                                        at[:, u, j, b * SEQ:(b + 1) * SEQ], start=False, stop=(b == 1),
                                                        tile_position=(0, 32 * g))
                        last.then_inc(bk.full(("o", u, 0)), 1)
                        if u:
                            project(pe, c, u - 1)
                    project(pe, c, U - 1)
                    wait_front(pe, core.tensor_waits, bk, c, range(4))
                    pe.drain().then_inc(ends["pe"], 1)
                    for n in ends:
                        if n != "pe":
                            pe.wait_ge(ends[n], c + 1)
        bk.close(CHUNKS)
    core.end_phase()


QMAX = 15.0


class Quant:

    def __init__(self, core, name, sb, groups, parts=1):
        self.core, self.name, self.G = core, name, groups
        self.mx = sb(f"{name}_max", [P, groups], F32)
        self.mn = sb(f"{name}_min", [P, groups], F32)
        self.s = sb(f"{name}_scale", [P, groups], F32)
        self.inv = sb(f"{name}_inv_scale", [P, groups], F32)
        self.base = sb(f"{name}_base", [P, groups], F32)
        self.shift = sb(f"{name}_base_less_round", [P, groups], F32)
        self.parts = parts
        self.s_red = Stage(core, f"{name}_extremes", 2 * parts)
        self.s_small = Stage(core, f"{name}_scales", 8)
        self.s_w1 = Stage(core, f"{name}_rounded", groups)
        self.s_w2 = Stage(core, f"{name}_shifted", groups)
        self.s_w3 = Stage(core, f"{name}_quantised", groups)

    def extremes(self, dve, c, x, part):
        v, n = self.core.nc.vector, self.G // self.parts
        gs = slice(part * n, (part + 1) * n)
        v.tensor_reduce(self.mx[:, gs], x[:, gs, :], AX.X, ALU.max).then_inc(self.s_red.sem, 1)
        v.tensor_reduce(self.mn[:, gs], x[:, gs, :], AX.X, ALU.min).then_inc(self.s_red.sem, 1)

    def scales(self, dve, c):
        v = self.core.nc.vector
        mx, mn, s, inv, base, shift = (t[:, :] for t in (self.mx, self.mn, self.s, self.inv, self.base, self.shift))
        dve.wait_ge(self.s_red.sem, self.s_red.value(c, 2 * self.parts - 1))
        v.tensor_tensor(s, mx, mn, ALU.subtract).then_inc(self.s_small.sem, 1)
        dve.wait_ge(self.s_small.sem, self.s_small.value(c, 0))
        v.tensor_scalar(s, s, 1e-5, 1 / QMAX, ALU.max, ALU.mult).then_inc(self.s_small.sem, 1)
        dve.wait_ge(self.s_small.sem, self.s_small.value(c, 1))
        v.reciprocal(inv, s).then_inc(self.s_small.sem, 1)
        dve.wait_ge(self.s_small.sem, self.s_small.value(c, 2))
        v.tensor_tensor(base, mn, inv, ALU.mult).then_inc(self.s_small.sem, 1)
        dve.wait_ge(self.s_small.sem, self.s_small.value(c, 3))
        v.tensor_scalar(base, base, -1.0, ROUND, ALU.mult, ALU.add).then_inc(self.s_small.sem, 1)
        dve.wait_ge(self.s_small.sem, self.s_small.value(c, 4))
        v.tensor_scalar(base, base, ROUND, 0.0, ALU.subtract, ALU.max).then_inc(self.s_small.sem, 1)
        dve.wait_ge(self.s_small.sem, self.s_small.value(c, 5))
        v.tensor_scalar(base, base, QMAX, None, ALU.min).then_inc(self.s_small.sem, 1)
        dve.wait_ge(self.s_small.sem, self.s_small.value(c, 6))
        v.tensor_scalar(shift, base, ROUND, None, ALU.subtract).then_inc(self.s_small.sem, 1)

    def rounded(self, dve, c, x):
        dve.wait_ge(self.s_small.sem, self.s_small.value(c, 7))
        for g in range(self.G):
            self.core.nc.vector.tensor_scalar(x[:, g, :], x[:, g, :], self.inv[:, g:g + 1], ROUND, ALU.mult, ALU.add)\
                .then_inc(self.s_w1.sem, 1)

    def digits(self, dve, c, x, groups):
        v = self.core.nc.vector
        for g in groups:
            dve.wait_ge(self.s_w1.sem, self.s_w1.value(c, g))
            v.tensor_scalar(x[:, g, :], x[:, g, :], self.shift[:, g:g + 1], 0.0, ALU.add, ALU.max).then_inc(self.s_w2.sem, 1)
        for g in groups:
            dve.wait_ge(self.s_w2.sem, self.s_w2.value(c, g))
            v.tensor_scalar(x[:, g, :], x[:, g, :], QMAX, self.base[:, g:g + 1], ALU.min, ALU.subtract)\
                .then_inc(self.s_w3.sem, 1)

    def vector(self, dve, c, x):
        for part in range(self.parts):
            self.extremes(dve, c, x, part)
        self.scales(dve, c)
        self.rounded(dve, c, x)
        for g in range(0, self.G, 8):
            self.digits(dve, c, x, range(g, g + 8))


FFN = 896
FB = FFN // P
E1 = 8
W13 = 2 * KD * FFN
WX = W13 + FB * D
MT = 256
MTILES = 2 * TOKENS // MT + E1 - 1


class ExpertWeights:

    G = 6 * FB
    PART = 2 * FB

    def __init__(self, core, sb, bank):
        self.core = core
        self.st = sb("ew_stage", [P, self.G, P], F32)
        self.wt = sb("ew_turned", [P, 2, WX], F16)
        self.magic = sb("ew_round", [P, 1], F32)
        small = [sb(f"ew_{n}", [P, self.G], F32) for n in ("max", "min", "scale", "inv_scale", "base", "lowest", "highest")]
        self.mx, self.mn, self.s, self.inv, self.base, self.lo, self.hi = small
        self.moves, self.last_move = [], []
        for w in range(2):
            for kd in range(KD):
                for f0, n in ((0, 4), (4, 3)):
                    self.moves.append(((w * KD + kd) * FFN + f0 * P, [(w * FB + f0 + i) * KD + kd for i in range(n)]))
            self.last_move.append(len(self.moves) - 1)
        for f0 in range(0, FB, 2):
            fs = range(f0, min(f0 + 2, FB))
            self.moves.append((W13 + f0 * D, [4 * FB + db * FB + f for f in fs for db in range(KD)]))
        self.last_move.append(len(self.moves) - 1)
        self.jobs = [(("m", i), bank) for i in range(len(self.moves))]
        self.s_in = Loads(core, "ew_loaded", 3)
        self.s_red = Stage(core, "ew_extremes", 6)
        self.s_small = Stage(core, "ew_scales", 27)
        self.s_round = Stage(core, "ew_rounded", self.G)
        self.s_clip = Stage(core, "ew_clipped", self.G)
        self.s_sc = Stage(core, "ew_scaled", self.G)
        self.s_hi = Stage(core, "ew_high_done", len(self.moves))
        self.s_out = core.sem("ew_stored")

    def groups(self, part, half):
        first = part * self.PART + half * FB
        return range(first, first + FB)

    def load(self, sp, c, bk, a, part):
        e = sp.snap(c) if not isinstance(c, int) else c
        last = ("m", self.last_move[part])
        sp.wait_ge(bk.full(last), bk.n_full(c - 1, last))
        sp.sem_inc(self.core.sync_waits, 1)
        st = self.st[:, part * self.PART:(part + 1) * self.PART, :]
        if part < 2:
            w = a["L1_ffn_w1"] if part == 0 else a["L1_ffn_w3"]
            sp.dma_start(st.rearrange("p (f k) n -> p f (k n)", f=FB),
                         w[bass.ds(e, 1)].rearrange("a (f p) n -> p (a f) n", p=P)).then_inc(self.s_in.sems[part], 16)
        else:
            sp.dma_start(st.rearrange("p (d f) n -> p d (f n)", d=KD),
                         a["L1_ffn_w2"][bass.ds(e, 1)].rearrange("a (d p) n -> p (a d) n", p=P))\
                .then_inc(self.s_in.sems[part], 16)

    def store(self, sp, c, bk, a):
        e = sp.snap(c) if not isinstance(c, int) else c
        last = ("m", len(self.moves) - 1)
        sp.wait_ge(bk.drained(last), bk.n_out(c, last))
        sp.sem_inc(self.core.sync_waits, 1)
        sp.dma_start(a["wx"][bass.ds(e, 1)].rearrange("a p n -> (a p) n"),
                     self.wt[:, :, :].rearrange("p s n -> p (s n)")).then_inc(self.s_out, 16)

    def extreme(self, dve, c, part, lowest):
        gs = slice(part * self.PART, (part + 1) * self.PART)
        if not lowest:
            dve.wait_ge(self.s_in.sems[part], self.s_in.value(c))
            dve.sem_inc(self.core.vector_waits, 1)
        self.core.nc.vector.tensor_reduce((self.mn if lowest else self.mx)[:, gs], self.st[:, gs, :], AX.X,
                                          ALU.min if lowest else ALU.max).then_inc(self.s_red.sem, 1)

    def scales(self, dve, c, part):
        v, n = self.core.nc.vector, part * 9
        mx, mn, s, inv, base, lo, hi = (t[:, part * self.PART:(part + 1) * self.PART] for t in
                                        (self.mx, self.mn, self.s, self.inv, self.base, self.lo, self.hi))
        dve.wait_ge(self.s_red.sem, self.s_red.value(c, 2 * part + 1))
        v.tensor_tensor(s, mx, mn, ALU.subtract).then_inc(self.s_small.sem, 1)
        dve.wait_ge(self.s_small.sem, self.s_small.value(c, n))
        v.tensor_scalar(s, s, 1e-5, 1 / QMAX, ALU.max, ALU.mult).then_inc(self.s_small.sem, 1)
        dve.wait_ge(self.s_small.sem, self.s_small.value(c, n + 1))
        v.reciprocal(inv, s).then_inc(self.s_small.sem, 1)
        dve.wait_ge(self.s_small.sem, self.s_small.value(c, n + 2))
        v.tensor_tensor(base, mn, inv, ALU.mult).then_inc(self.s_small.sem, 1)
        dve.wait_ge(self.s_small.sem, self.s_small.value(c, n + 3))
        v.tensor_scalar(base, base, -1.0, ROUND, ALU.mult, ALU.add).then_inc(self.s_small.sem, 1)
        dve.wait_ge(self.s_small.sem, self.s_small.value(c, n + 4))
        v.tensor_scalar(base, base, ROUND, 0.0, ALU.subtract, ALU.max).then_inc(self.s_small.sem, 1)
        dve.wait_ge(self.s_small.sem, self.s_small.value(c, n + 5))
        v.tensor_scalar(base, base, QMAX, -1.0, ALU.min, ALU.mult).then_inc(self.s_small.sem, 1)
        dve.wait_ge(self.s_small.sem, self.s_small.value(c, n + 6))
        v.tensor_scalar(lo, base, ROUND, None, ALU.add).then_inc(self.s_small.sem, 1)
        v.tensor_scalar(hi, base, ROUND + QMAX, None, ALU.add).then_inc(self.s_small.sem, 1)

    def rounded(self, act, c, part, half):
        act.wait_ge(self.s_small.sem, self.s_small.value(c, part * 9 + 8))
        for g in self.groups(part, half):
            self.core.nc.scalar.activation(self.st[:, g, :], self.st[:, g, :], ACT.Identity, bias=self.magic[:, :],
                                           scale=self.inv[:, g:g + 1]).then_inc(self.s_round.sem, 1)

    def clipped(self, pool, c, part, half):
        pool.wait_ge(self.s_round.sem, self.s_round.value(c, self.groups(part, half)[-1]))
        pool.sem_inc(self.core.pool_waits, 1)
        for g in self.groups(part, half):
            self.core.nc.gpsimd.tensor_scalar(self.st[:, g, :], self.st[:, g, :], self.lo[:, g:g + 1],
                                              self.hi[:, g:g + 1], ALU.max, ALU.min).then_inc(self.s_clip.sem, 1)

    def scaled(self, dve, c, part, half):
        for g in self.groups(part, half):
            dve.wait_ge(self.s_clip.sem, self.s_clip.value(c, g))
            self.core.nc.vector.tensor_scalar(self.st[:, g, :], self.st[:, g, :], ROUND, self.s[:, g:g + 1],
                                              ALU.subtract, ALU.mult).then_inc(self.s_sc.sem, 1)

    def turn(self, pe, c, bk, i):
        gs = self.moves[i][1]
        pe.wait_ge(bk.drained(("m", i)), bk.n_free(c, ("m", i)))
        pe.wait_ge(self.s_sc.sem, self.s_sc.value(c, max(gs)))
        for j, g in enumerate(gs):
            last = self.core.nc.tensor.transpose(bk.tile(("m", i))[:, j * P:(j + 1) * P], self.st[:, g, :],
                                                 self.core.ident[:, :])
        last.then_inc(bk.full(("m", i)), 1)

    def high(self, act, c, bk, i):
        at, gs = self.moves[i]
        if i == 0:
            act.wait_ge(self.s_out, c * 16 + 1)
        act.wait_ge(bk.full(("m", i)), bk.n_full(c, ("m", i)))
        self.core.nc.scalar.activation(self.wt[:, 0, at:at + len(gs) * P], bk.tile(("m", i))[:, 0:len(gs) * P],
                                       ACT.Copy, scale=WS).then_inc(self.s_hi.sem, 1)

    def low(self, dve, c, bk, i):
        at, gs = self.moves[i]
        cols = slice(at, at + len(gs) * P)
        dve.wait_ge(self.s_hi.sem, self.s_hi.value(c, i))
        self.core.nc.vector.scalar_tensor_tensor(self.wt[:, 1, cols], bk.tile(("m", i))[:, 0:len(gs) * P], WS,
                                                 self.wt[:, 0, cols], ALU.mult, ALU.subtract)\
            .then_inc(bk.drained(("m", i)), 1)


GS = 64.0


class TopTwo:

    def __init__(self, core, phase, sb):
        self.core = core
        self.lg = sb(f"{phase}_logits", [P, U, 16], F32)
        self.top = sb(f"{phase}_top8", [P, U, 8], F32)
        self.want = sb(f"{phase}_two_values", [P, U, 8], F32)
        self.rest = sb(f"{phase}_replaced", [P, U, 16], F32)
        self.ex = sb(f"{phase}_gate_exp", [P, U, 8], F32)
        self.gates = sb(f"{phase}_gates", [P, U, 8], F32)
        self.mask = sb(f"{phase}_two_mask", [P, U, 8], F32)
        self.sm = sb(f"{phase}_gate_sum", [P, U], F32)
        self.rc = sb(f"{phase}_gate_rsum", [P, U], F32)
        self.s_top = Stage(core, f"{phase}_top8_done")
        self.s_want = Stage(core, f"{phase}_two_values_done", 1)
        self.s_rest = Stage(core, f"{phase}_replaced_done")
        self.s_sub = Stage(core, f"{phase}_logits_minus_max", 1)
        self.s_ex = Stage(core, f"{phase}_gate_exp_done", 1)
        self.s_sel = Stage(core, f"{phase}_two_selected", 2)
        self.s_sm = Stage(core, f"{phase}_gate_sum_done", 2)
        self.s_g = Stage(core, f"{phase}_gates_done", 1)

    def prepare(self, dve):
        self.core.nc.vector.memset(self.want[:, :, :], 3e38)
        self.core.nc.vector.memset(self.lg[:, :, 8:16], 3e38)

    def wide(self, x):
        return x.unsqueeze(2).to_broadcast([P, U, 8])

    def vector(self, dve, c, bank, bias, banks, job, bc=None):
        nc, bc = self.core.nc, c if bc is None else bc
        lg = self.lg[:, :, 0:8]
        ps = bank[:, 0:8 * U].rearrange("p (u e) -> p u e", u=U)
        dve.wait_ge(banks.full(job), banks.n_full(bc, job))
        if bias is None:
            nc.vector.tensor_scalar(lg, ps, 1 / WS, None, ALU.mult).then_inc(banks.drained(job), 1)
        else:
            nc.vector.scalar_tensor_tensor(lg, ps, 1 / WS, bias, ALU.mult, ALU.add).then_inc(banks.drained(job), 1)
        dve.wait_ge(banks.drained(job), banks.n_out(bc, job))
        dve.sem_inc(self.core.vector_waits, 1)
        for u in range(U):
            nc.vector.max(self.top[:, u, :], self.lg[:, u, 0:8]).then_inc(self.s_top.sem, 1)
        dve.wait_ge(self.s_top.sem, self.s_top.value(c, U - 1))
        nc.vector.tensor_copy(self.want[:, :, 0:2], self.top[:, :, 0:2]).then_inc(self.s_want.sem, 1)
        nc.vector.tensor_tensor(self.ex[:, :, :], lg, self.top[:, :, 0:1].to_broadcast([P, U, 8]), ALU.subtract)\
            .then_inc(self.s_sub.sem, 1)
        dve.wait_ge(self.s_want.sem, self.s_want.value(c, 0))
        dve.sem_inc(self.core.vector_waits, 1)
        for u in range(U):
            nc.vector.match_replace(self.rest[:, u, :], self.want[:, u, :], self.lg[:, u, :], NEG)\
                .then_inc(self.s_rest.sem, 1)
        dve.wait_ge(self.s_rest.sem, self.s_rest.value(c, U - 1))
        nc.vector.tensor_tensor(self.mask[:, :, :], self.rest[:, :, 0:8], lg, ALU.not_equal).then_inc(self.s_sel.sem, 1)
        dve.wait_ge(self.s_sel.sem, self.s_sel.value(c, 0))
        dve.wait_ge(self.s_ex.sem, self.s_ex.value(c, 0))
        nc.vector.tensor_tensor(self.gates[:, :, :], self.mask[:, :, :], self.ex[:, :, :], ALU.mult)\
            .then_inc(self.s_sel.sem, 1)
        dve.wait_ge(self.s_sel.sem, self.s_sel.value(c, 1))
        nc.vector.tensor_reduce(self.sm[:, :], self.gates[:, :, :], AX.X, ALU.add).then_inc(self.s_sm.sem, 1)
        dve.wait_ge(self.s_sm.sem, self.s_sm.value(c, 0))
        nc.vector.reciprocal(self.rc[:, :], self.sm[:, :]).then_inc(self.s_sm.sem, 1)
        dve.wait_ge(self.s_sm.sem, self.s_sm.value(c, 1))
        nc.vector.tensor_tensor(self.gates[:, :, :], self.gates[:, :, :], self.wide(self.rc[:, :]), ALU.mult)\
            .then_inc(self.s_g.sem, 1)

    def scalar(self, act, c):
        act.wait_ge(self.s_sub.sem, self.s_sub.value(c, 0))
        self.core.nc.scalar.activation(self.ex[:, :, :], self.ex[:, :, :], ACT.Exp).then_inc(self.s_ex.sem, 1)


def ffn0(core, a):
    nc = core.nc
    E, R, HD = 10, 8, 128
    SL = 5
    AHEAD = 2
    with ExitStack() as ctx:
        def sb(name, shape, dt):
            return ctx.enter_context(nc.sbuf_tensor(name, shape, dt))

        st13 = sb("f0_stage13", [P, 2, E, KD, HD], F32)
        st2 = sb("f0_stage2", [P, E, D], F32)
        w13h = sb("f0_w13h", [P, 2, E, KD, HD], F16)
        w13l = sb("f0_w13l", [P, 2, E, KD, HD], F16)
        w2h = sb("f0_w2h", [P, E, D], F16)
        w2l = sb("f0_w2l", [P, E, D], F16)
        str_ = sb("f0_stage_router", [P, KD, R], F32)
        rwh = sb("f0_rwh", [P, KD, R], F16)
        rwl = sb("f0_rwl", [P, KD, R], F16)
        rb = sb("f0_router_b", [P, R], F32)
        sel = sb("f0_expert_rows", [2 * R, R, P], F16)
        identh = sb("f0_ident16", [P, P], F16)
        nrm = Norm(core, "f0", sb)
        xt = Transposed(core, "f0", sb)
        top = TopTwo(core, "f0", sb)
        g2 = sb("f0_gates_split", [P, U, 2 * R], F16)
        gs = sb("f0_gates_scaled", [P, U, R], F32)
        gt = sb("f0_gates_t", [2 * R, CT], F16)
        sil = sb("f0_silu", [P, SL, CT], F32)
        uu = sb("f0_u", [P, SL, CT], F32)
        uh = sb("f0_uh", [P, SL, CT], F16)
        ul = sb("f0_ul", [P, SL, CT], F16)
        ew = ExpertWeights(core, sb, 5)

        order = [("g",), ("p1", 0), ("p3", 0), ("p1", 1), ("p3", 1), ("gt",), ("gb", 0), ("gb", 1)]
        for e in range(AHEAD, E):
            order += [("p1", e), ("p3", e)] + ([("gb", e)] if e < R else [])
        order += [("x", 0), ("x", 1)]
        jobs = ring(order, range(5))
        bk0 = Banks(core, jobs[-2:])
        bk0.close(1)
        bk = Banks(core, jobs + [(("y", 0), 6), (("y", 1), 7)] + ew.jobs)
        turns = {(3, 0): 0, (3, 1): 1, (4, 0): 2, (4, 1): 3, (5, 1): 4, (6, 0): 5, (6, 1): 6, (7, 0): 7,
                 (7, 1): 8, (8, 0): 9, (8, 1): 10, (9, 0): 11}
        rounds = {1: (0, 0), 2: (0, 1), 3: (1, 0), 4: (1, 1), 5: (2, 0), 6: (2, 1)}
        scalings = {3: (0, 0), 4: (0, 1), 5: (1, 0), 6: (1, 1), 7: (2, 0), 8: (2, 1)}
        loaded = core.sem("f0_loaded")
        magic = core.sem("f0_round_constant_filled")
        act_waits = core.sem("f0_scalar_waits_passed")
        wh_done = core.sem("f0_wh_done")
        w_done = core.sem("f0_w_done")
        s_gs = Stage(core, "f0_gates_scaled_done", 1)
        s_gh = Stage(core, "f0_gates_high_done", 1)
        s_gl = Stage(core, "f0_gates_low_done", 1)
        s_uh = Stage(core, "f0_uh_done", E)
        s_ul = Stage(core, "f0_ul_done", E, base=E)
        s_ye = Stage(core, "f0_down_done", E - 1, base=E - 1)

        def row(c, u):
            return core.h[:, bass.ds(c * U + u, 1), :].rearrange("p a d -> p (a d)")

        def before(c, e):
            return (c, e - SL) if e >= SL else (c - 1, e + SL)

        def flat(x):
            return x.rearrange("p w e k n -> p (w e k n)")

        def flat3(x):
            return x.rearrange("p e n -> p (e n)")

        with nc.Block() as block:
            @block.sync
            def _(sp):
                for i, n in enumerate(("w1", "w3")):
                    sp.dma_start(st13[:, i, 0:R, :, :], a["L0_ffn_routed_" + n].rearrange("e (k p) n -> p e k n", p=P))\
                        .then_inc(loaded, 16)
                    sp.dma_start(st13[:, i, R:E, :, :], a["L0_ffn_shared_" + n].rearrange("e (k p) n -> p e k n", p=P))\
                        .then_inc(loaded, 16)
                sp.dma_start(st2[:, 0:R, :], a["L0_ffn_routed_w2"].rearrange("e p n -> p e n")).then_inc(loaded, 16)
                sp.dma_start(st2[:, R:E, :], a["L0_ffn_shared_w2"].rearrange("e p n -> p e n")).then_inc(loaded, 16)
                sp.dma_start(str_[:, :, :], a["L0_ffn_router_w"].rearrange("(k p) n -> p k n", p=P)).then_inc(loaded, 16)
                sp.dma_start(rb[:, :], a["L0_ffn_router_b"].partition_broadcast(P)).then_inc(loaded, 16)
                sp.dma_start(sel[:, :, :], a["expert_rows"]).then_inc(loaded, 16)
                sp.dma_start(identh[:, :], a["ident16"]).then_inc(loaded, 16)

                sp.sem_inc(ew.s_out, 1)
                for part in range(2):
                    ew.load(sp, 0, bk, a, part)
                with sp.Fori(0, CHUNKS - 1) as c:
                    ew.load(sp, c, bk, a, 2)
                    for part in range(2):
                        ew.load(sp, c + 1, bk, a, part)
                    ew.store(sp, c, bk, a)
                ew.load(sp, CHUNKS - 1, bk, a, 2)
                ew.store(sp, CHUNKS - 1, bk, a)
                sp.wait_ge(ew.s_out, CHUNKS * 16 + 1)

            @block.gpsimd
            def _(pool):
                nrm.gpsimd(pool, 0)
                with pool.Fori(0, CHUNKS) as c:
                    for e in range(E):
                        if e in rounds:
                            ew.clipped(pool, c, *rounds[e])
                        if e == 6:
                            nrm.gpsimd(pool, c + 1)

            @block.scalar
            def _(act):
                act.wait_ge(loaded, 10 * 16)
                nc.scalar.activation(rwh[:, :, :], str_[:, :, :], ACT.Copy, scale=WS).then_inc(wh_done, 1)
                nc.scalar.activation(flat(w13h[:, :, :, :, :]), flat(st13[:, :, :, :, :]), ACT.Copy, scale=WS).then_inc(wh_done, 1)
                nc.scalar.activation(flat3(w2h[:, :, :]), flat3(st2[:, :, :]), ACT.Copy, scale=WS).then_inc(wh_done, 1)
                xt.scalar(act, 0, bk0)
                act.wait_ge(magic, 1)

                def high(c, e):
                    pc, p = before(c, e)
                    made = ("gb", e) if e < R else ("p3", e)
                    act.wait_ge(bk.drained(made), bk.n_out(c, made))
                    act.sem_inc(act_waits, 1)
                    if p == E - 1:
                        act.wait_ge(bk.full(("y", 1)), bk.n_full(pc, ("y", 1)))
                    else:
                        act.wait_ge(s_ye.sem, s_ye.value(pc, p))
                    nc.scalar.copy(uh[:, e % SL, :], uu[:, e % SL, :]).then_inc(s_uh.sem, 1)

                with act.Fori(0, CHUNKS) as c:
                    top.scalar(act, c)
                    act.wait_ge(s_gs.sem, s_gs.value(c, 0))
                    nc.scalar.activation(g2[:, :, 0:R], gs[:, :, :], ACT.Copy).then_inc(s_gh.sem, 1)
                    for e in range(E):
                        for (step, place), i in turns.items():
                            if step + AHEAD == e and place == 0:
                                ew.high(act, c, bk, i)
                        pc, p = before(c, e)
                        act.wait_ge(bk.drained(("p3", p)), bk.n_out(pc, ("p3", p)))
                        act.sem_inc(act_waits, 1)
                        act.wait_ge(bk.full(("p1", e)), bk.n_full(c, ("p1", e)))
                        nc.scalar.activation(sil[:, e % SL, :], bk.tile(("p1", e))[:, :], ACT.Silu, scale=1 / WS)\
                            .then_inc(bk.drained(("p1", e)), 1)
                        if e == 0:
                            act.wait_ge(bk.full(("gt",)), bk.n_full(c, ("gt",)))
                            nc.scalar.activation(gt[:, :], bk.tile(("gt",))[:, :].bitcast(F16)[0:2 * R, 0:CT], ACT.Copy)\
                                .then_inc(bk.drained(("gt",)), 1)
                        if e:
                            high(c, e - 1)
                        if e in rounds:
                            ew.rounded(act, c, *rounds[e])
                        for (step, place), i in turns.items():
                            if step + AHEAD == e and place > 0:
                                ew.high(act, c, bk, i)
                    high(c, E - 1)
                    for (step, place), i in turns.items():
                        if step == E - AHEAD:
                            ew.high(act, c, bk, i)
                    xt.scalar(act, c + 1, bk, c)
                    for (step, place), i in turns.items():
                        if step > E - AHEAD:
                            ew.high(act, c, bk, i)

            @block.vector
            def _(dve):
                top.prepare(dve)
                dve.sem_inc(s_ul.sem, E)
                dve.wait_ge(wh_done, 3)
                nc.vector.scalar_tensor_tensor(rwl[:, :, :], str_[:, :, :], WS, rwh[:, :, :], ALU.mult, ALU.subtract)\
                    .then_inc(w_done, 1)
                nc.vector.scalar_tensor_tensor(flat(w13l[:, :, :, :, :]), flat(st13[:, :, :, :, :]), WS,
                                               flat(w13h[:, :, :, :, :]), ALU.mult, ALU.subtract).then_inc(w_done, 1)
                nc.vector.scalar_tensor_tensor(flat3(w2l[:, :, :]), flat3(st2[:, :, :]), WS, flat3(w2h[:, :, :]),
                                               ALU.mult, ALU.subtract).then_inc(w_done, 1)
                nc.vector.memset(ew.magic[:, :], ROUND).then_inc(magic, 1)
                nrm.vector(dve, 0, row)
                xt.vector(dve, 0, bk0)

                def low(c, e):
                    dve.wait_ge(s_uh.sem, s_uh.value(c, e))
                    nc.vector.tensor_tensor(ul[:, e % SL, :], uu[:, e % SL, :], uh[:, e % SL, :], ALU.subtract)\
                        .then_inc(s_ul.sem, 1)

                with dve.Fori(0, CHUNKS) as c:
                    top.vector(dve, c, bk.tile(("g",)), rb[:, :].unsqueeze(1).to_broadcast([P, U, R]), bk, ("g",))
                    dve.wait_ge(top.s_g.sem, top.s_g.value(c, 0))
                    nc.vector.tensor_scalar(gs[:, :, :], top.gates[:, :, :], GS, None, ALU.mult).then_inc(s_gs.sem, 1)
                    dve.wait_ge(s_gh.sem, s_gh.value(c, 0))
                    nc.vector.tensor_tensor(g2[:, :, R:2 * R], gs[:, :, :], g2[:, :, 0:R], ALU.subtract).then_inc(s_gl.sem, 1)
                    for e in range(E):
                        for (step, place), i in turns.items():
                            if step + AHEAD == e and place == 0:
                                ew.low(dve, c, bk, i)
                        dve.wait_ge(bk.drained(("p1", e)), bk.n_out(c, ("p1", e)))
                        dve.wait_ge(bk.full(("p3", e)), bk.n_full(c, ("p3", e)))
                        pc, p = before(c, e)
                        dve.wait_ge(s_ul.sem, s_ul.value(pc, p))
                        nc.vector.scalar_tensor_tensor(uu[:, e % SL, :], sil[:, e % SL, :], (1 if e < R else GS) / WS,
                                                       bk.tile(("p3", e))[:, :], ALU.mult, ALU.mult)\
                            .then_inc(bk.drained(("p3", e)), 1)
                        if e < R:
                            dve.wait_ge(bk.drained(("p3", e)), bk.n_out(c, ("p3", e)))
                            dve.wait_ge(bk.full(("gb", e)), bk.n_full(c, ("gb", e)))
                            nc.vector.tensor_tensor(uu[:, e % SL, :], uu[:, e % SL, :], bk.tile(("gb", e))[:, :], ALU.mult)\
                                .then_inc(bk.drained(("gb", e)), 1)
                        if e:
                            low(c, e - 1)
                        if e < 6:
                            ew.extreme(dve, c, e // 2, e % 2)
                            if e % 2:
                                ew.scales(dve, c, e // 2)
                        if e in scalings:
                            ew.scaled(dve, c, *scalings[e])
                        if e == 6:
                            nrm.vector_stats(dve, c + 1, row)
                        if e == 8:
                            nrm.vector_rows(dve, c + 1, row)
                        for (step, place), i in turns.items():
                            if step + AHEAD == e and place > 0:
                                ew.low(dve, c, bk, i)
                    low(c, E - 1)
                    for (step, place), i in turns.items():
                        if step == E - AHEAD:
                            ew.low(dve, c, bk, i)
                    xt.vector(dve, c + 1, bk, c)
                    for (step, place), i in turns.items():
                        if step > E - AHEAD:
                            ew.low(dve, c, bk, i)
                    for i in range(2):
                        rows = core.h[:, bass.ds(c * U + 2 * i, 2), :]
                        dve.wait_ge(bk.full(("y", i)), bk.n_full(c, ("y", i)))
                        nc.vector.scalar_tensor_tensor(rows, bk.tile(("y", i))[:, :].rearrange("p (u d) -> p u d", u=2),
                                                       1 / (WS * GS), rows, ALU.mult, ALU.add)\
                            .then_inc(bk.drained(("y", i)), 1)

            @block.tensor
            def _(pe):
                pe.wait_ge(w_done, 3)

                def up(c, e):
                    for i, n in enumerate(("p1", "p3")):
                        pe.wait_ge(bk.drained((n, e)), bk.n_free(c, (n, e)))
                        for kd in range(KD):
                            last = three(nc, bk.tile((n, e))[:, :], (w13h[:, i, e, kd, :], w13l[:, i, e, kd, :]),
                                         (xt.xh[:, kd, :], xt.xl[:, kd, :]), kd == 0, kd == KD - 1)
                        last.then_inc(bk.full((n, e)), 1)

                def spread(c, e):
                    pe.wait_ge(bk.drained(("gb", e)), bk.n_free(c, ("gb", e)))
                    nc.tensor.matmul(bk.tile(("gb", e))[:, :], sel[:, e, :], gt[:, :], start=True, stop=True)\
                        .then_inc(bk.full(("gb", e)), 1)

                def down(c, e):
                    pe.wait_ge(s_ul.sem, s_ul.value(c, e))
                    for u in range(U):
                        i = u // 2
                        if e == 0 and u % 2 == 0:
                            pe.wait_ge(bk.drained(("y", i)), bk.n_free(c, ("y", i)))
                        last = three(nc, bk.tile(("y", i))[:, (u % 2) * D:(u % 2 + 1) * D],
                                     (uh[:, e % SL, u * P:(u + 1) * P], ul[:, e % SL, u * P:(u + 1) * P]),
                                     (w2h[:, e, :], w2l[:, e, :]), e == 0 and u % 2 == 0, e == E - 1 and u % 2 == 1)
                        if e == E - 1 and u % 2:
                            last.then_inc(bk.full(("y", i)), 1)
                    if e < E - 1:
                        last.then_inc(s_ye.sem, 1)

                def weights(c, step, place):
                    if (step, place) in turns:
                        ew.turn(pe, c, bk, turns[step, place])

                pe.sem_inc(s_ye.sem, E - 1)
                xt.tensor(pe, 0, bk0, nrm.xn, nrm.s_xn)
                for kd in range(KD):
                    pe.wait_ge(bk0.drained(("x", kd)), bk0.n_out(0, ("x", kd)))
                with pe.Fori(0, CHUNKS) as c:
                    for kd in range(KD):
                        pe.wait_ge(bk.drained(("x", kd)), bk.n_out(c - 1, ("x", kd)))
                    pe.sem_inc(core.tensor_waits, 1)
                    pe.wait_ge(bk.drained(("g",)), bk.n_free(c, ("g",)))
                    for u in range(U):
                        for kd in range(KD):
                            last = three(nc, bk.tile(("g",))[:, u * R:(u + 1) * R],
                                         (xt.xh[:, kd, u * P:(u + 1) * P], xt.xl[:, kd, u * P:(u + 1) * P]),
                                         (rwh[:, kd, :], rwl[:, kd, :]), kd == 0, kd == KD - 1)
                    last.then_inc(bk.full(("g",)), 1)
                    for e in range(AHEAD):
                        up(c, e)
                    pe.wait_ge(bk.drained(("gt",)), bk.n_free(c, ("gt",)))
                    pe.wait_ge(s_gh.sem, s_gh.value(c, 0))
                    pe.wait_ge(s_gl.sem, s_gl.value(c, 0))
                    for u in range(U):
                        last = nc.tensor.transpose(bk.tile(("gt",))[:, :].bitcast(F16)[0:2 * R, u * P:(u + 1) * P],
                                                   g2[:, u, :], identh[:, :])
                    last.then_inc(bk.full(("gt",)), 1)
                    pe.wait_ge(bk.drained(("gt",)), bk.n_out(c, ("gt",)))
                    for e in range(AHEAD):
                        spread(c, e)
                    for e in range(E):
                        weights(c, e, 0)
                        if e + AHEAD < E:
                            up(c, e + AHEAD)
                        if e + AHEAD < R:
                            spread(c, e + AHEAD)
                        weights(c, e, 1)
                        if e + AHEAD == E:
                            xt.tensor(pe, c + 1, bk, nrm.xn, nrm.s_xn, c)
                        down(c, e)
        bk.close(CHUNKS)
    core.end_phase()


def attn1(core, a):
    nc = core.nc
    Z = 13
    assert MTILES * MT % (Z * P) == 0
    NH, DH, ROT = 2, 128, 32
    with ExitStack() as ctx:
        def sb(name, shape, dt):
            return ctx.enter_context(nc.sbuf_tensor(name, shape, dt))

        st = sb("a1_stage", [P, KD, 3, NH, DH], F32)
        sto = sb("a1_stage_wo", [P, KD, D], F32)
        wh = sb("a1_wh", [P, KD, 3, NH, DH], F16)
        wl = sb("a1_wl", [P, KD, 3, NH, DH], F16)
        woh = sb("a1_woh", [P, KD, D], F16)
        wol = sb("a1_wol", [P, KD, D], F16)
        rot = sb("a1_cos_sin", [P, 3, 2 * ROT], F32)
        mask = sb("a1_mask", [P, P], F32)
        nrm = Norm(core, "a1", sb)
        xt = Transposed(core, "a1", sb)
        qk = sb("a1_qk", [P, U, 2 * NH, DH], F32)
        v = sb("a1_v", [P, U, NH * DH], F32)
        tc = sb("a1_cos_part", [P, U, 2 * NH, 2 * ROT], F32)
        ts = sb("a1_sin_part", [P, U, 2 * NH, 2 * ROT], F32)
        qt = sb("a1_qt", [P, U, 2 * NH, P], F32)
        s = sb("a1_s", [P, U, NH, P], F32)
        nm = sb("a1_minus_max", [P, U, NH], F32)
        sm = sb("a1_sum", [P, U, NH], F32)
        rc = sb("a1_rsum", [P, U, NH], F32)
        pt = sb("a1_pt", [P, U, NH, P], F32)
        oh = sb("a1_oh", [P, U, NH, P], F16)
        ol = sb("a1_ol", [P, U, NH, P], F16)

        front = [("x", kd) for kd in range(KD)]
        bk0 = Banks(core, ring(front, range(8)))
        bk0.close(1)
        jobs = [(n, u) for u in range(U) for n in ("qk", "v")]
        jobs += [(n, u) for n in ("t", "s") for u in range(U)] + front
        jobs += [(n, u) for n in ("pt", "o", "y") for u in range(U)]
        bk = Banks(core, ring(jobs, range(8)))
        ends = chunk_ends(core, "a1", ["pe", "act", "dve", "pool"])
        zero = sb("a1_zero_rows", [P, Z * D], F32)
        zeroed = core.sem("a1_zeros_filled")
        cleared = core.sem("a1_expert_rows_cleared")
        loaded = core.sem("a1_loaded")
        wh_done = core.sem("a1_wh_done")
        w_done = core.sem("a1_w_done")
        s_ts = Stage(core, "a1_sin_parts_done", 3 * U)
        s_qr = Stage(core, "a1_rotated")
        s_nm = Stage(core, "a1_minus_max_done")
        s_ex = Stage(core, "a1_exp_done", NH * U)
        s_rc = Stage(core, "a1_rsum_done")
        s_pr = Stage(core, "a1_probs_done")
        s_oh = Stage(core, "a1_oh_done")

        def row(c, u):
            return core.h[:, bass.ds(c * U + u, 1), :].rearrange("p a d -> p (a d)")

        def flat(x):
            return x.rearrange("p k w h n -> p (k w h n)")

        def flat2(x):
            return x.rearrange("p a b -> p (a b)")

        with nc.Block() as block:
            @block.sync
            def _(sp):
                for i, n in enumerate(("wq", "wk", "wv")):
                    for h in range(NH):
                        sp.dma_start(st[:, :, i, h, :], a["L1_attn_" + n][h].rearrange("(k p) n -> p k n", p=P))\
                            .then_inc(loaded, 16)
                sp.dma_start(sto[:, :, :], a["L1_attn_wo"].rearrange("(k p) n -> p k n", p=P)).then_inc(loaded, 16)
                sp.dma_start(rot[:, :, :], a["rot_a1"]).then_inc(loaded, 16)
                sp.dma_start(mask[:, :], a["causal_mask"]).then_inc(loaded, 16)
                sp.wait_ge(zeroed, 1)
                n = MTILES * MT // (Z * P)
                for i in range(n):
                    sp.dma_start(a["rows_in"][i * Z * P:(i + 1) * Z * P, :].rearrange("(p z) d -> p (z d)", z=Z), zero[:, :])\
                        .then_inc(cleared, 16)
                sp.wait_ge(cleared, 16 * n)

            @block.gpsimd
            def _(pool):
                pool.memset(zero[:, :], 0.0).then_inc(zeroed, 1)
                pool.wait_ge(loaded, 9 * 16)
                nrm.gpsimd(pool, 0)
                with pool.Fori(0, CHUNKS) as c:
                    nrm.gpsimd(pool, c + 1)
                    for u in range(U):
                        pool.wait_ge(bk.drained(("qk", u)), bk.n_out(c, ("qk", u)))
                        nc.gpsimd.tensor_tensor(ts[:, u, :, 0:ROT], qk[:, u, :, ROT:2 * ROT],
                                                rot[:, 1, 0:ROT].unsqueeze(1).to_broadcast([P, 2 * NH, ROT]), ALU.mult)\
                            .then_inc(s_ts.sem, 1)
                        nc.gpsimd.tensor_tensor(ts[:, u, :, ROT:2 * ROT], qk[:, u, :, 0:ROT],
                                                rot[:, 2, 0:ROT].unsqueeze(1).to_broadcast([P, 2 * NH, ROT]), ALU.mult)\
                            .then_inc(s_ts.sem, 1)
                        nc.gpsimd.tensor_tensor(tc[:, u, :, :], qk[:, u, :, 0:2 * ROT],
                                                rot[:, 0, :].unsqueeze(1).to_broadcast([P, 2 * NH, 2 * ROT]), ALU.mult)\
                            .then_inc(s_ts.sem, 1)
                    for u in range(U):
                        pool.wait_ge(s_rc.sem, s_rc.value(c, u))
                        nc.gpsimd.tensor_tensor(s[:, u, :, :], s[:, u, :, :],
                                                rc[:, u, :].unsqueeze(2).to_broadcast([P, NH, P]), ALU.mult)\
                            .then_inc(s_pr.sem, 1)
                    pool.drain().then_inc(ends["pool"], 1)
                    for n in ends:
                        if n != "pool":
                            pool.wait_ge(ends[n], c + 1)

            @block.scalar
            def _(act):
                act.wait_ge(loaded, 9 * 16)
                nc.scalar.activation(flat(wh[:, :, :, :, :]), flat(st[:, :, :, :, :]), ACT.Copy, scale=WS).then_inc(wh_done, 1)
                nc.scalar.activation(flat2(woh[:, :, :]), flat2(sto[:, :, :]), ACT.Copy, scale=WS).then_inc(wh_done, 1)
                xt.scalar(act, 0, bk0)
                with act.Fori(0, CHUNKS) as c:
                    for u in range(U):
                        act.wait_ge(bk.full(("qk", u)), bk.n_full(c, ("qk", u)))
                        nc.scalar.activation(qk[:, u, :, :].rearrange("p h n -> p (h n)"), bk.tile(("qk", u))[:, :],
                                                        ACT.Copy, scale=1 / WS)\
                            .then_inc(bk.drained(("qk", u)), 1)
                        act.wait_ge(bk.full(("v", u)), bk.n_full(c, ("v", u)))
                        nc.scalar.activation(v[:, u, :], bk.tile(("v", u))[:, 0:D], ACT.Copy, scale=1 / WS)\
                            .then_inc(bk.drained(("v", u)), 1)
                    for u in range(U):
                        act.wait_ge(bk.full(("t", u)), bk.n_full(c, ("t", u)))
                        nc.scalar.copy(flat2(qt[:, u, :, :]), bk.tile(("t", u))[:, :]).then_inc(bk.drained(("t", u)), 1)
                    for u in range(U):
                        act.wait_ge(s_nm.sem, s_nm.value(c, u))
                        for h in range(NH):
                            nc.scalar.activation(s[:, u, h, :], s[:, u, h, :], ACT.Exp, bias=nm[:, u, h:h + 1],
                                                 accum_out=sm[:, u, h:h + 1]).then_inc(s_ex.sem, 1)
                    xt.scalar(act, c + 1, bk, c)
                    for u in range(U):
                        act.wait_ge(bk.full(("o", u)), bk.n_full(c, ("o", u)))
                        nc.scalar.copy(flat2(oh[:, u, :, :]), bk.tile(("o", u))[:, 0:D]).then_inc(s_oh.sem, 1)
                    act.drain().then_inc(ends["act"], 1)
                    for n in ends:
                        if n != "act":
                            act.wait_ge(ends[n], c + 1)

            @block.vector
            def _(dve):
                dve.wait_ge(wh_done, 2)
                nc.vector.scalar_tensor_tensor(flat(wl[:, :, :, :, :]), flat(st[:, :, :, :, :]), WS, flat(wh[:, :, :, :, :]),
                                               ALU.mult, ALU.subtract).then_inc(w_done, 1)
                nc.vector.scalar_tensor_tensor(flat2(wol[:, :, :]), flat2(sto[:, :, :]), WS, flat2(woh[:, :, :]),
                                               ALU.mult, ALU.subtract).then_inc(w_done, 1)
                nrm.vector(dve, 0, row)
                xt.vector(dve, 0, bk0)
                with dve.Fori(0, CHUNKS) as c:
                    nrm.vector(dve, c + 1, row)
                    for u in range(U):
                        dve.wait_ge(s_ts.sem, s_ts.value(c, 3 * u + 2))
                        nc.vector.tensor_tensor(qk[:, u, :, 0:2 * ROT], tc[:, u, :, :], ts[:, u, :, :], ALU.add)\
                            .then_inc(s_qr.sem, 1)
                    for u in range(U):
                        dve.wait_ge(bk.full(("s", u)), bk.n_full(c, ("s", u)))
                        nc.vector.scalar_tensor_tensor(
                            s[:, u, :, :], bk.tile(("s", u))[:, 0:NH * P].rearrange("p (h t) -> p h t", h=NH), 1 / DH,
                            mask[:, :].unsqueeze(1).to_broadcast([P, NH, P]), ALU.mult, ALU.add)\
                            .then_inc(bk.drained(("s", u)), 1)
                        dve.wait_ge(bk.drained(("s", u)), bk.n_out(c, ("s", u)))
                        nc.vector.tensor_reduce(nm[:, u, :], s[:, u, :, :], AX.X, ALU.max, negate=True).then_inc(s_nm.sem, 1)
                    for u in range(U):
                        dve.wait_ge(s_ex.sem, s_ex.value(c, NH * u + 1))
                        nc.vector.reciprocal(rc[:, u, :], sm[:, u, :]).then_inc(s_rc.sem, 1)
                    xt.vector(dve, c + 1, bk)
                    for u in range(U):
                        dve.wait_ge(bk.full(("pt", u)), bk.n_full(c, ("pt", u)))
                        nc.vector.tensor_copy(flat2(pt[:, u, :, :]), bk.tile(("pt", u))[:, 0:NH * P])\
                            .then_inc(bk.drained(("pt", u)), 1)
                    for u in range(U):
                        dve.wait_ge(s_oh.sem, s_oh.value(c, u))
                        nc.vector.tensor_tensor(flat2(ol[:, u, :, :]), bk.tile(("o", u))[:, 0:D],
                                                           flat2(oh[:, u, :, :]), ALU.subtract)\
                            .then_inc(bk.drained(("o", u)), 1)
                    for u in range(U):
                        dve.wait_ge(bk.full(("y", u)), bk.n_full(c, ("y", u)))
                        nc.vector.scalar_tensor_tensor(row(c, u), bk.tile(("y", u))[:, 0:D], 1 / WS, row(c, u),
                                                                  ALU.mult, ALU.add)\
                            .then_inc(bk.drained(("y", u)), 1)
                    dve.drain().then_inc(ends["dve"], 1)
                    for n in ends:
                        if n != "dve":
                            dve.wait_ge(ends[n], c + 1)

            @block.tensor
            def _(pe):
                pe.wait_ge(w_done, 2)
                xt.tensor(pe, 0, bk0, nrm.xn, nrm.s_xn)
                for kd in range(KD):
                    pe.wait_ge(bk0.drained(("x", kd)), bk0.n_out(0, ("x", kd)))
                pe.sem_inc(core.tensor_waits, 1)
                with pe.Fori(0, CHUNKS) as c:
                    for u in range(U):
                        for n, w, m in (("qk", 0, 4 * DH), ("v", 2, 2 * DH)):
                            pe.wait_ge(bk.drained((n, u)), bk.n_free(c, (n, u)))
                            for kd in range(KD):
                                ws = [x[:, kd, w:(2 if w == 0 else 3), :, :].rearrange("p w h n -> p (w h n)") for x in (wh, wl)]
                                last = three(nc, bk.tile((n, u))[:, 0:m],
                                             (xt.xh[:, kd, u * P:(u + 1) * P], xt.xl[:, kd, u * P:(u + 1) * P]),
                                             ws, kd == 0, kd == KD - 1)
                            last.then_inc(bk.full((n, u)), 1)
                    for u in range(U):
                        pe.wait_ge(bk.drained(("t", u)), bk.n_free(c, ("t", u)))
                        pe.wait_ge(s_qr.sem, s_qr.value(c, u))
                        pe.wait_ge(bk.drained(("v", u)), bk.n_out(c, ("v", u)))
                        for i in range(2 * NH):
                            last = nc.tensor.transpose(bk.tile(("t", u))[:, i * P:(i + 1) * P], qk[:, u, i, :], core.ident[:, :])
                        last.then_inc(bk.full(("t", u)), 1)
                    for u in range(U):
                        pe.wait_ge(bk.drained(("t", u)), bk.n_out(c, ("t", u)))
                        pe.wait_ge(bk.drained(("s", u)), bk.n_free(c, ("s", u)))
                        for h in range(NH):
                            last = nc.tensor.matmul(bk.tile(("s", u))[:, h * P:(h + 1) * P], qt[:, u, h, :], qt[:, u, NH + h, :],
                                                    start=True, stop=True)
                        last.then_inc(bk.full(("s", u)), 1)
                    xt.tensor(pe, c + 1, bk, nrm.xn, nrm.s_xn, c)
                    for u in range(U):
                        pe.wait_ge(s_pr.sem, s_pr.value(c, u))
                        pe.wait_ge(bk.drained(("pt", u)), bk.n_free(c, ("pt", u)))
                        for h in range(NH):
                            last = nc.tensor.transpose(bk.tile(("pt", u))[:, h * P:(h + 1) * P], s[:, u, h, :], core.ident[:, :])
                        last.then_inc(bk.full(("pt", u)), 1)
                    for u in range(U):
                        pe.wait_ge(bk.drained(("pt", u)), bk.n_out(c, ("pt", u)))
                        pe.wait_ge(bk.drained(("o", u)), bk.n_free(c, ("o", u)))
                        for h in range(NH):
                            last = nc.tensor.matmul(bk.tile(("o", u))[:, h * P:(h + 1) * P], v[:, u, h * DH:(h + 1) * DH],
                                                    pt[:, u, h, :], start=True, stop=True)
                        last.then_inc(bk.full(("o", u)), 1)
                    for u in range(U):
                        pe.wait_ge(bk.drained(("o", u)), bk.n_out(c, ("o", u)))
                        pe.wait_ge(bk.drained(("y", u)), bk.n_free(c, ("y", u)))
                        for h in range(NH):
                            last = three(nc, bk.tile(("y", u))[:, 0:D], (oh[:, u, h, :], ol[:, u, h, :]),
                                         (woh[:, h, :], wol[:, h, :]), h == 0, h == NH - 1)
                        last.then_inc(bk.full(("y", u)), 1)
                    pe.drain().then_inc(ends["pe"], 1)
                    for n in ends:
                        if n != "pe":
                            pe.wait_ge(ends[n], c + 1)
        bk.close(CHUNKS)
    core.end_phase()


def block1_weights(core, a, wh, wl, woh, wol):
    nc = core.nc
    with ExitStack() as ctx:
        def sb(name, shape, dt):
            return ctx.enter_context(nc.sbuf_tensor(name, shape, dt))

        st = sb("bw_stage", [P, 40, P], F32)
        qn = Quant(core, "bw", sb, 40)
        moves = []
        for kd in range(KD):
            for f in range(0, 12, 4):
                moves.append((wh[:, kd, f * P:(f + 4) * P], wl[:, kd, f * P:(f + 4) * P], [2 * (f + i) + kd for i in range(4)]))
        for g in range(0, 8, 2):
            moves.append((woh[:, g:g + 2, :].rearrange("p g n -> p (g n)"), wol[:, g:g + 2, :].rearrange("p g n -> p (g n)"),
                          [24 + 8 * db + g + i for i in range(2) for db in range(2)]))
        bk = Banks(core, ring([("m", i) for i in range(len(moves))], range(8)))
        loaded = core.sem("bw_loaded")
        scaled = core.sem("bw_scaled")
        s_hi = Stage(core, "bw_high_done", len(moves))
        with nc.Block() as block:
            @block.sync
            def _(sp):
                for at, n, rows in ((0, "w_q", 8), (16, "w_k", 2), (20, "w_v", 2)):
                    sp.dma_start(st[:, at:at + 2 * rows, :].rearrange("p (r g) k -> p r (g k)", r=rows),
                                 a["L1_ffn_" + n].rearrange("(r p) n -> p r n", p=P)).then_inc(loaded, 16)
                sp.dma_start(st[:, 24:40, :].rearrange("p (r g) k -> p r (g k)", r=2),
                             a["L1_ffn_w_o"].rearrange("(r p) n -> p r n", p=P)).then_inc(loaded, 16)

            @block.vector
            def _(dve):
                dve.wait_ge(loaded, 64)
                qn.extremes(dve, 0, st[:, :, :], 0)
                qn.scales(dve, 0)
                qn.rounded(dve, 0, st[:, :, :])
                for g in range(0, 40, 8):
                    qn.digits(dve, 0, st[:, :, :], range(g, g + 8))
                for i, (hi, lo, _) in enumerate(moves):
                    dve.wait_ge(s_hi.sem, s_hi.value(0, i))
                    nc.vector.scalar_tensor_tensor(lo, bk.tile(("m", i))[:, :], WS, hi, ALU.mult, ALU.subtract)\
                        .then_inc(bk.drained(("m", i)), 1)

            @block.scalar
            def _(act):
                for g in range(40):
                    act.wait_ge(qn.s_w3.sem, qn.s_w3.value(0, g))
                    nc.scalar.activation(st[:, g, :], st[:, g, :], ACT.Copy, scale=qn.s[:, g:g + 1]).then_inc(scaled, 1)
                for i, (hi, lo, _) in enumerate(moves):
                    act.wait_ge(bk.full(("m", i)), bk.n_full(0, ("m", i)))
                    nc.scalar.activation(hi, bk.tile(("m", i))[:, :], ACT.Copy, scale=WS).then_inc(s_hi.sem, 1)

            @block.tensor
            def _(pe):
                for i, (_, _, groups) in enumerate(moves):
                    pe.wait_ge(bk.drained(("m", i)), bk.n_free(0, ("m", i)))
                    pe.wait_ge(scaled, max(groups) + 1)
                    for j, g in enumerate(groups):
                        last = nc.tensor.transpose(bk.tile(("m", i))[:, j * P:(j + 1) * P], st[:, g, :], core.ident[:, :])
                    last.then_inc(bk.full(("m", i)), 1)
        bk.close(1)
    core.end_phase()


def block1(core, a, hn, gates, masks):
    nc = core.nc
    H, KVH, HD = 8, 2, 128
    with ExitStack() as ctx:
        def sb(name, shape, dt):
            return ctx.enter_context(nc.sbuf_tensor(name, shape, dt))

        NQ = H + 2 * KVH
        wh = sb("b1_wh", [P, KD, NQ * HD], F16)
        wl = sb("b1_wl", [P, KD, NQ * HD], F16)
        woh = sb("b1_woh", [P, H, D], F16)
        wol = sb("b1_wol", [P, H, D], F16)
        block1_weights(core, a, wh, wl, woh, wol)

        stg = sb("b1_stage_gate", [P, KD, 8], F32)
        wgh = sb("b1_gate_high", [P, KD, 8], F16)
        wgl = sb("b1_gate_low", [P, KD, 8], F16)
        rot = sb("b1_cos_sin", [P, 2, HD], F32)
        mask = sb("b1_mask", [P, P], F32)
        g1 = sb("b1_g1", [P, D], F32)
        g2 = sb("b1_g2", [P, D], F32)
        nrm = Norm(core, "b1", sb)
        xt = Transposed(core, "b1", sb)
        xt2 = Transposed(core, "b1b", sb, "x2")
        top = TopTwo(core, "b1", sb)
        qn = Quant(core, "b1kv", sb, U * 2 * KVH)
        xr = sb("b1_xr", [P, U, D], F32)
        xk = sb("b1_x_kept", [P, U, D], F32)
        hr = sb("b1_hn_rows", [P, U, D], F32)
        ssq = sb("b1_sum_squares", [P, 2, U], F32)
        rms = sb("b1_rms", [P, 2, U], F32)
        inv_d = sb("b1_one_over_d", [P, U], F32)
        qk = sb("b1_qk", [P, U, H + KVH, HD], F32)
        kv = sb("b1_kv", [P, U, 2 * KVH, HD], F32)
        vq = sb("b1_v", [P, U, KVH, HD], F32)
        ts = sb("b1_sin_part", [P, 2, H + KVH, HD], F32)
        qt = sb("b1_qt", [P, U, H + KVH, P], F32)
        s = sb("b1_s", [P, U, H, P], F32)
        nm = sb("b1_minus_max", [P, U, H], F32)
        sm = sb("b1_sum", [P, U, H], F32)
        rc = sb("b1_rsum", [P, U, H], F32)
        pt = qt[:, :, 0:H, :]
        oh = sb("b1_oh", [P, 2, H, P], F16)
        ol = sb("b1_ol", [P, 2, H, P], F16)

        projected = [("kv", u) for u in range(U)] + [(n, u) for u in range(U) for n in ("q0", "q1")]
        front = [("x", kd) for kd in range(KD)] + projected
        turned = [[(n, u) for n in ("tk", "tq0", "tq1")] for u in range(U)]
        bk0 = Banks(core, ring(front + sum(turned, []), range(8)))
        bk0.close(1)
        scores = [(n, u) for u in range(U) for n in ("s0", "s1")]
        values = [(n, v) for u in range(U + 1) for n, v in (("p0", u), ("p1", u), ("o0", u), ("o1", u), ("y", u - 1)) if 0 <= v < U]
        x2 = [("x2", kd) for kd in range(KD)]
        bk_loop = Banks(core, ring(scores + front + values + turned[0] + turned[1] + x2 + turned[2] + [("g",)] + turned[3],
                                   range(8)))
        bk_loop.close(CHUNKS - 1)
        bk_last = Banks(core, ring(scores + values + x2 + [("g",)], range(8)))
        bk_last.close(1)
        ends = chunk_ends(core, "b1", ["pe", "act", "dve", "pool"])
        loaded = core.sem("b1_loaded")
        wh_done = core.sem("b1_wh_done")
        w_done = core.sem("b1_w_done")
        filled = core.sem("b1_one_over_d_filled")
        s_sq = [Stage(core, f"b1_squares{i}_done") for i in range(2)]
        s_rm = [Stage(core, f"b1_rms{i}_done", 3) for i in range(2)]
        s_xk = Stage(core, "b1_x_kept_done", 1)
        s_xr = Stage(core, "b1_xr_done")
        s_kq = Stage(core, "b1_k_scaled")
        s_vq = Stage(core, "b1_v_scaled")
        s_ts = Stage(core, "b1_sin_parts_done", 2 * U)
        s_cq = Stage(core, "b1_cos_parts_done")
        s_rq = Stage(core, "b1_rotated")
        s_nm = Stage(core, "b1_minus_max_done", 2 * U)
        s_ex = Stage(core, "b1_exp_done", H * U)
        s_rc = Stage(core, "b1_rsum_done")
        s_pr = Stage(core, "b1_probs_done")
        s_oh = Stage(core, "b1_oh_done", 2 * U)
        s_hn = Stage(core, "b1_hn_done")
        s_ga = Stage(core, "b1_gates_kept", 2)
        s_hr = Stage(core, "b1_hn_kept", 1)
        s_rs = Stage(core, "b1_h_added")

        def row(c, u, t=core.h):
            return t[:, bass.ds(c * U + u, 1), :].rearrange("p a d -> p (a d)")

        def flat2(x):
            return x.rearrange("p a b -> p (a b)")

        def halves(x):
            return x.rearrange("p h (f n) -> p h f n", f=2)

        def root_mean(pool, c, i):
            pool.wait_ge(s_sq[i].sem, s_sq[i].value(c, U - 1))
            ms = rms[:, i, :]
            nc.gpsimd.tensor_tensor(ms, ssq[:, i, :], inv_d[:, :], ALU.mult).then_inc(s_rm[i].sem, 1)
            pool.wait_ge(s_rm[i].sem, s_rm[i].value(c, 0))
            nc.gpsimd.tensor_tensor(ms, ms, core.eps[:, :], ALU.add).then_inc(s_rm[i].sem, 1)
            pool.wait_ge(s_rm[i].sem, s_rm[i].value(c, 1))
            nc.gpsimd.tensor_tensor(ms, ms, core.mhalf[:, :], ALU.pow).then_inc(s_rm[i].sem, 1)

        def sin_parts(pool, c, u):
            for f in range(2):
                nc.gpsimd.tensor_tensor(halves(ts[:, u % 2, :, :])[:, :, f, :], halves(qk[:, u, :, :])[:, :, 1 - f, :],
                                        rot[:, 1, f * 64:(f + 1) * 64].unsqueeze(1).to_broadcast([P, H + KVH, 64]),
                                        ALU.mult).then_inc(s_ts.sem, 1)

        def squares(act, c):
            for u in range(U):
                act.wait_ge(nrm.s_xn.sem, nrm.s_xn.value(c, u))
                nc.scalar.activation(xr[:, u, :], nrm.xn[:, u, :], ACT.Square, accum_out=ssq[:, 0, u:u + 1])\
                    .then_inc(s_sq[0].sem, 1)

        def evacuate(act, bc, banks):
            for n, u in projected:
                act.wait_ge(banks.full((n, u)), banks.n_full(bc, (n, u)))
                dst = flat2(kv[:, u, :, :]) if n == "kv" else flat2(qk[:, u, 4 * int(n[1]):4 * int(n[1]) + 4, :])
                nc.scalar.activation(dst, banks.tile((n, u))[:, :], ACT.Copy, scale=1 / WS)\
                    .then_inc(banks.drained((n, u)), 1)

        def scaled(act, c, first):
            for u in range(U):
                for i in range(KVH):
                    g = u * 2 * KVH + first + i
                    act.wait_ge(qn.s_w3.sem, qn.s_w3.value(c, g))
                    dst = vq[:, u, i, :] if first else qk[:, u, H + i, :]
                    ins = nc.scalar.activation(dst, kv[:, u, first + i, :], ACT.Copy, scale=qn.s[:, g:g + 1])
                ins.then_inc((s_vq if first else s_kq).sem, 1)

        def rotate(dve, c, u):
            dve.wait_ge(s_ts.sem, s_ts.value(c, 2 * u + 1))
            nc.vector.tensor_tensor(qk[:, u, :, :], qk[:, u, :, :],
                                    rot[:, 0, :].unsqueeze(1).to_broadcast([P, H + KVH, HD]), ALU.mult)\
                .then_inc(s_cq.sem, 1)
            dve.wait_ge(s_cq.sem, s_cq.value(c, u))
            nc.vector.tensor_tensor(qk[:, u, :, :], qk[:, u, :, :], ts[:, u % 2, :, :], ALU.add)\
                .then_inc(s_rq.sem, 1)

        def turn(pe, c, banks, bc, u):
            pe.wait_ge(s_rq.sem, s_rq.value(c, u))
            for n, at, m in (("tk", H, KVH), ("tq0", 0, 4), ("tq1", 4, 4)):
                pe.wait_ge(banks.drained((n, u)), banks.n_free(bc, (n, u)))
                for i in range(m):
                    last = nc.tensor.transpose(banks.tile((n, u))[:, i * P:(i + 1) * P], qk[:, u, at + i, :],
                                               core.ident[:, :])
                last.then_inc(banks.full((n, u)), 1)

        def keep_turned(act, bc, banks, u):
            act.wait_ge(banks.full(("tq0", u)), banks.n_full(bc, ("tq0", u)))
            nc.scalar.copy(flat2(qt[:, u, 0:4, :]), banks.tile(("tq0", u))[:, :]).then_inc(banks.drained(("tq0", u)), 1)

        def keep_turned_too(dve, bc, banks, u):
            dve.wait_ge(banks.full(("tk", u)), banks.n_full(bc, ("tk", u)))
            nc.vector.tensor_copy(flat2(qt[:, u, H:H + KVH, :]), banks.tile(("tk", u))[:, 0:KVH * P])\
                .then_inc(banks.drained(("tk", u)), 1)
            dve.wait_ge(banks.full(("tq1", u)), banks.n_full(bc, ("tq1", u)))
            nc.vector.tensor_copy(flat2(qt[:, u, 4:8, :]), banks.tile(("tq1", u))[:, :])\
                .then_inc(banks.drained(("tq1", u)), 1)

        def xr_rows(dve, c):
            dve.wait_ge(s_rm[0].sem, s_rm[0].value(c, 2))
            for u in range(U):
                nc.vector.scalar_tensor_tensor(xr[:, u, :], nrm.xn[:, u, :], rms[:, 0, u:u + 1], g1[:, :],
                                               ALU.mult, ALU.mult).then_inc(s_xr.sem, 1)

        def make_front(pe, c, banks, bc):
            xt.tensor(pe, c, banks, xr, s_xr, bc)
            for kd in range(KD):
                pe.wait_ge(banks.drained(("x", kd)), banks.n_out(bc, ("x", kd)))
            pe.sem_inc(core.tensor_waits, 1)
            for n, u in projected:
                at = {"kv": 1024, "q0": 0, "q1": 512}[n]
                pe.wait_ge(banks.drained((n, u)), banks.n_free(bc, (n, u)))
                for kd in range(KD):
                    last = three(nc, banks.tile((n, u))[:, :],
                                 (xt.xh[:, kd, u * P:(u + 1) * P], xt.xl[:, kd, u * P:(u + 1) * P]),
                                 (wh[:, kd, at:at + 512], wl[:, kd, at:at + 512]), kd == 0, kd == KD - 1)
                last.then_inc(banks.full((n, u)), 1)

        kvg = kv[:, :, :, :].rearrange("p u i n -> p (u i) n")

        with nc.Block() as block:
            @block.sync
            def _(sp):
                sp.dma_start(stg[:, :, :], a["w_gate_t"].rearrange("(k p) e -> p k e", p=P)).then_inc(loaded, 16)
                sp.dma_start(rot[:, :, :], a["rot_b1"]).then_inc(loaded, 16)
                sp.dma_start(mask[:, :], a["causal_mask"]).then_inc(loaded, 16)
                sp.dma_start(g1[:, :], a["L1_ffn_g1"].partition_broadcast(P)).then_inc(loaded, 16)
                sp.dma_start(g2[:, :], a["L1_ffn_g2"].partition_broadcast(P)).then_inc(loaded, 16)

            @block.gpsimd
            def _(pool):
                pool.memset(inv_d[:, :], 1 / D).then_inc(filled, 1)
                pool.wait_ge(loaded, 5 * 16)
                pool.wait_ge(filled, 1)
                nrm.gpsimd(pool, 0)
                root_mean(pool, 0, 0)
                for u in range(U):
                    pool.wait_ge(s_kq.sem, s_kq.value(0, u))
                    for n in ("q0", "q1"):
                        pool.wait_ge(bk0.drained((n, u)), bk0.n_out(0, (n, u)))
                        pool.sem_inc(core.pool_waits, 1)
                for u in range(2):
                    sin_parts(pool, 0, u)
                for u in range(2, U):
                    pool.wait_ge(s_rq.sem, s_rq.value(0, u - 2))
                    sin_parts(pool, 0, u)

                def chunk(c, b, bk, more):
                    if more:
                        nrm.gpsimd(pool, c + 1)
                        root_mean(pool, c + 1, 0)
                    for u in range(U):
                        pool.wait_ge(s_rc.sem, s_rc.value(c, u))
                        nc.gpsimd.tensor_tensor(s[:, u, :, :], s[:, u, :, :],
                                                rc[:, u, :].unsqueeze(2).to_broadcast([P, H, P]), ALU.mult).then_inc(s_pr.sem, 1)
                    if more:
                        for u in range(U):
                            pool.wait_ge(s_kq.sem, s_kq.value(c + 1, u))
                        pool.wait_ge(bk.drained(("q0", U - 1)), bk.n_out(b, ("q0", U - 1)))
                        pool.sem_inc(core.pool_waits, 1)
                        pool.wait_ge(bk.drained(("q1", U - 1)), bk.n_out(b, ("q1", U - 1)))
                        pool.sem_inc(core.pool_waits, 1)
                        for u in range(2):
                            sin_parts(pool, c + 1, u)
                    root_mean(pool, c, 1)
                    if more:
                        for u in range(2, U):
                            pool.wait_ge(s_rq.sem, s_rq.value(c + 1, u - 2))
                            sin_parts(pool, c + 1, u)
                    pool.drain().then_inc(ends["pool"], 1)
                    for n in ends:
                        if n != "pool":
                            pool.wait_ge(ends[n], c + 1)

                with pool.Fori(0, CHUNKS - 1) as c:
                    chunk(c, c, bk_loop, True)
                chunk(CHUNKS - 1, 0, bk_last, False)

            @block.scalar
            def _(act):
                act.wait_ge(loaded, 5 * 16)
                nc.scalar.activation(wgh[:, :, :], stg[:, :, :], ACT.Copy, scale=WS).then_inc(wh_done, 1)
                squares(act, 0)
                xt.scalar(act, 0, bk0)
                evacuate(act, 0, bk0)
                for first in (0, KVH):
                    scaled(act, 0, first)
                for u in range(U):
                    keep_turned(act, 0, bk0, u)

                def chunk(c, b, bk, more):
                    nc.scalar.copy(xk[:, :, :], nrm.xn[:, :, :]).then_inc(s_xk.sem, 1)
                    if more:
                        squares(act, c + 1)
                    for u in range(U):
                        for h in range(H):
                            if h % 4 == 0:
                                act.wait_ge(s_nm.sem, s_nm.value(c, 2 * u + h // 4))
                            nc.scalar.activation(s[:, u, h, :], s[:, u, h, :], ACT.Exp, bias=nm[:, u, h:h + 1],
                                                 accum_out=sm[:, u, h:h + 1]).then_inc(s_ex.sem, 1)
                        if u == 2 and more:
                            xt.scalar(act, c + 1, bk, b)
                    if more:
                        evacuate(act, b, bk)
                    for u in range(U):
                        act.wait_ge(bk.full(("p0", u)), bk.n_full(b, ("p0", u)))
                        nc.scalar.copy(flat2(pt[:, u, 0:4, :]), bk.tile(("p0", u))[:, :]).then_inc(bk.drained(("p0", u)), 1)
                        for i in range(2):
                            if u >= 2 and i == 0:
                                act.wait_ge(bk.full(("y", u - 2)), bk.n_full(b, ("y", u - 2)))
                            act.wait_ge(bk.full((f"o{i}", u)), bk.n_full(b, (f"o{i}", u)))
                            nc.scalar.copy(flat2(oh[:, u % 2, 4 * i:4 * i + 4, :]), bk.tile((f"o{i}", u))[:, :])\
                                .then_inc(s_oh.sem, 1)
                        if u == 0 and more:
                            scaled(act, c + 1, 0)
                    for u in range(U):
                        act.wait_ge(s_rs.sem, s_rs.value(c, u))
                        nc.scalar.activation(hr[:, u, :], xk[:, u, :], ACT.Square, accum_out=ssq[:, 1, u:u + 1])\
                            .then_inc(s_sq[1].sem, 1)
                    if more:
                        scaled(act, c + 1, KVH)
                        keep_turned(act, b, bk, 0)
                        keep_turned(act, b, bk, 1)
                    xt2.scalar(act, c, bk, b)
                    if more:
                        keep_turned(act, b, bk, 2)
                    top.scalar(act, c)
                    if more:
                        keep_turned(act, b, bk, 3)
                    act.drain().then_inc(ends["act"], 1)
                    for n in ends:
                        if n != "act":
                            act.wait_ge(ends[n], c + 1)

                with act.Fori(0, CHUNKS - 1) as c:
                    chunk(c, c, bk_loop, True)
                chunk(CHUNKS - 1, 0, bk_last, False)

            @block.vector
            def _(dve):
                top.prepare(dve)
                dve.wait_ge(wh_done, 1)
                nc.vector.scalar_tensor_tensor(wgl[:, :, :], stg[:, :, :], WS, wgh[:, :, :], ALU.mult, ALU.subtract)\
                    .then_inc(w_done, 1)
                nrm.vector(dve, 0, row)
                xr_rows(dve, 0)
                xt.vector(dve, 0, bk0)
                for u in range(U):
                    dve.wait_ge(bk0.drained(("kv", u)), bk0.n_out(0, ("kv", u)))
                qn.vector(dve, 0, kvg)
                for u in range(U):
                    rotate(dve, 0, u)
                for u in range(U):
                    keep_turned_too(dve, 0, bk0, u)

                def chunk(c, b, bk, more):
                    if more:
                        nrm.vector_stats(dve, c + 1, row)
                    for u in range(U):
                        if u == 1 and more:
                            dve.wait_ge(s_xk.sem, s_xk.value(c, 0))
                            dve.sem_inc(core.vector_waits, 1)
                            nrm.vector_rows(dve, c + 1, row)
                        if u == 3 and more:
                            xr_rows(dve, c + 1)
                        for i in range(2):
                            hs = slice(4 * i, 4 * i + 4)
                            n = (f"s{i}", u)
                            dve.wait_ge(bk.full(n), bk.n_full(b, n))
                            nc.vector.scalar_tensor_tensor(
                                s[:, u, hs, :], bk.tile(n)[:, :].rearrange("p (h t) -> p h t", h=4), HD ** -0.5,
                                mask[:, :].unsqueeze(1).to_broadcast([P, 4, P]), ALU.mult, ALU.add)\
                                .then_inc(bk.drained(n), 1)
                            dve.wait_ge(bk.drained(n), bk.n_out(b, n))
                            nc.vector.tensor_reduce(nm[:, u, hs], s[:, u, hs, :], AX.X, ALU.max, negate=True)\
                                .then_inc(s_nm.sem, 1)
                    if more:
                        xt.vector(dve, c + 1, bk)
                    for u in range(U):
                        dve.wait_ge(s_ex.sem, s_ex.value(c, H * (u + 1) - 1))
                        nc.vector.reciprocal(rc[:, u, :], sm[:, u, :]).then_inc(s_rc.sem, 1)

                    if more:
                        for v in range(U):
                            dve.wait_ge(bk.drained(("kv", v)), bk.n_out(b, ("kv", v)))
                            dve.sem_inc(core.vector_waits, 1)
                        qn.vector(dve, c + 1, kvg)

                    def residual(u):
                        dve.wait_ge(bk.full(("y", u)), bk.n_full(b, ("y", u)))
                        nc.vector.scalar_tensor_tensor(xk[:, u, :], bk.tile(("y", u))[:, 0:D], 1 / WS,
                                                       xk[:, u, :], ALU.mult, ALU.add)\
                            .then_inc(bk.drained(("y", u)), 1)

                    for u in range(U):
                        dve.wait_ge(bk.full(("p1", u)), bk.n_full(b, ("p1", u)))
                        nc.vector.tensor_copy(flat2(pt[:, u, 4:8, :]), bk.tile(("p1", u))[:, :])\
                            .then_inc(bk.drained(("p1", u)), 1)
                        for i in range(2):
                            n = (f"o{i}", u)
                            dve.wait_ge(s_oh.sem, s_oh.value(c, 2 * u + i))
                            nc.vector.tensor_tensor(flat2(ol[:, u % 2, 4 * i:4 * i + 4, :]), bk.tile(n)[:, :],
                                                               flat2(oh[:, u % 2, 4 * i:4 * i + 4, :]), ALU.subtract)\
                                .then_inc(bk.drained(n), 1)
                        if u:
                            residual(u - 1)
                    residual(U - 1)
                    for u in range(U):
                        dve.wait_ge(bk.drained(("y", u)), bk.n_out(b, ("y", u)))
                        nc.vector.tensor_tensor(row(c, u), row(c, u), xk[:, u, :], ALU.add).then_inc(s_rs.sem, 1)
                    if more:
                        rotate(dve, c + 1, 0)
                    dve.wait_ge(s_rm[1].sem, s_rm[1].value(c, 2))
                    for u in range(U):
                        nc.vector.scalar_tensor_tensor(hr[:, u, :], xk[:, u, :], rms[:, 1, u:u + 1], g2[:, :],
                                                       ALU.mult, ALU.mult).then_inc(s_hn.sem, 1)
                    dve.wait_ge(s_hn.sem, s_hn.value(c, U - 1))
                    nc.vector.tensor_copy(hn[:, bass.ds(c * U, U), :], hr[:, :, :]).then_inc(s_hr.sem, 1)
                    if more:
                        rotate(dve, c + 1, 1)
                        keep_turned_too(dve, b, bk, 0)
                    xt2.vector(dve, c, bk)
                    if more:
                        rotate(dve, c + 1, 2)
                        keep_turned_too(dve, b, bk, 1)
                        rotate(dve, c + 1, 3)
                        keep_turned_too(dve, b, bk, 2)
                    top.vector(dve, c, bk.tile(("g",)), None, bk, ("g",), b)
                    dve.wait_ge(top.s_g.sem, top.s_g.value(c, 0))
                    nc.vector.tensor_copy(gates[:, bass.ds(c * U, U), :], top.gates[:, :, :]).then_inc(s_ga.sem, 1)
                    nc.vector.tensor_copy(masks[:, bass.ds(c * U, U), :], top.mask[:, :, :]).then_inc(s_ga.sem, 1)
                    if more:
                        keep_turned_too(dve, b, bk, 3)
                    dve.drain().then_inc(ends["dve"], 1)
                    for n in ends:
                        if n != "dve":
                            dve.wait_ge(ends[n], c + 1)

                with dve.Fori(0, CHUNKS - 1) as c:
                    chunk(c, c, bk_loop, True)
                chunk(CHUNKS - 1, 0, bk_last, False)

            @block.tensor
            def _(pe):
                pe.wait_ge(w_done, 1)
                make_front(pe, 0, bk0, 0)
                for u in range(U):
                    turn(pe, 0, bk0, 0, u)
                for job in sum(turned, []):
                    pe.wait_ge(bk0.drained(job), bk0.n_out(0, job))
                    pe.sem_inc(core.tensor_waits, 1)

                def chunk(c, b, bk, more):
                    for u in range(U):
                        for i in range(2):
                            n = (f"s{i}", u)
                            pe.wait_ge(bk.drained(n), bk.n_free(b, n))
                            for j in range(4):
                                last = nc.tensor.matmul(bk.tile(n)[:, j * P:(j + 1) * P], qt[:, u, 4 * i + j, :],
                                                        qt[:, u, H + i, :], start=True, stop=True)
                            last.then_inc(bk.full(n), 1)

                    if more:
                        make_front(pe, c + 1, bk, b)

                    def project(u):
                        pe.wait_ge(s_oh.sem, s_oh.value(c, 2 * u + 1))
                        for i in range(2):
                            pe.wait_ge(bk.drained((f"o{i}", u)), bk.n_out(b, (f"o{i}", u)))
                        pe.sem_inc(core.tensor_waits, 1)
                        pe.wait_ge(bk.drained(("y", u)), bk.n_free(b, ("y", u)))
                        for h in range(H):
                            last = three(nc, bk.tile(("y", u))[:, 0:D], (oh[:, u % 2, h, :], ol[:, u % 2, h, :]),
                                         (woh[:, h, :], wol[:, h, :]), h == 0, h == H - 1)
                        last.then_inc(bk.full(("y", u)), 1)

                    for u in range(U):
                        pe.wait_ge(s_pr.sem, s_pr.value(c, u))
                        for i in range(2):
                            n = (f"p{i}", u)
                            pe.wait_ge(bk.drained(n), bk.n_free(b, n))
                            for j in range(4):
                                last = nc.tensor.transpose(bk.tile(n)[:, j * P:(j + 1) * P], s[:, u, 4 * i + j, :],
                                                           core.ident[:, :])
                            last.then_inc(bk.full(n), 1)
                        pe.wait_ge(s_vq.sem, s_vq.value(c, u))
                        for i in range(2):
                            n = (f"o{i}", u)
                            pe.wait_ge(bk.drained((f"p{i}", u)), bk.n_out(b, (f"p{i}", u)))
                            pe.sem_inc(core.tensor_waits, 1)
                            pe.wait_ge(bk.drained(n), bk.n_free(b, n))
                            nc.tensor.matmul(bk.tile(n)[:, :], vq[:, u, i, :], flat2(pt[:, u, 4 * i:4 * i + 4, :]),
                                                       start=True, stop=True)\
                                .then_inc(bk.full(n), 1)
                        if u:
                            project(u - 1)
                    project(U - 1)
                    if more:
                        turn(pe, c + 1, bk, b, 0)
                        turn(pe, c + 1, bk, b, 1)
                    xt2.tensor(pe, c, bk, hr, s_hn, b)
                    if more:
                        turn(pe, c + 1, bk, b, 2)
                    for kd in range(KD):
                        pe.wait_ge(bk.drained(("x2", kd)), bk.n_out(b, ("x2", kd)))
                    pe.wait_ge(bk.drained(("g",)), bk.n_free(b, ("g",)))
                    for u in range(U):
                        for kd in range(KD):
                            last = three(nc, bk.tile(("g",))[:, u * 8:(u + 1) * 8],
                                         (xt2.xh[:, kd, u * P:(u + 1) * P], xt2.xl[:, kd, u * P:(u + 1) * P]),
                                         (wgh[:, kd, :], wgl[:, kd, :]), kd == 0, kd == KD - 1)
                    last.then_inc(bk.full(("g",)), 1)
                    if more:
                        turn(pe, c + 1, bk, b, 3)
                    pe.drain().then_inc(ends["pe"], 1)
                    for n in ends:
                        if n != "pe":
                            pe.wait_ge(ends[n], c + 1)

                with pe.Fori(0, CHUNKS - 1) as c:
                    chunk(c, c, bk_loop, True)
                chunk(CHUNKS - 1, 0, bk_last, False)
    core.end_phase()


def route(core, a, hn, gates, masks, slot, share, tile_expert):
    nc = core.nc
    with ExitStack() as ctx:
        def sb(name, shape, dt):
            return ctx.enter_context(nc.sbuf_tensor(name, shape, dt))

        tri = sb("rt_before", [P, P], F32)
        ones = sb("rt_ones", [P, P], F32)
        number = sb("rt_tile_number", [P, MTILES, E1], F32)
        zero = sb("rt_zero", [P, TILES], F32)
        rank = sb("rt_rank", [P, TILES, E1], F32)
        tot = sb("rt_total", [P, TILES, E1], F32)
        incl = sb("rt_inclusive", [P, TILES, E1], F32)
        need = sb("rt_tiles_needed", [P, E1], F32)
        cum = sb("rt_tiles_to", [P, E1], F32)
        offs = sb("rt_first_row", [P, E1], F32)
        mp = sb("rt_masked_row", [P, TILES, E1], F32)
        sl = sb("rt_slots", [P, TILES, 2], F32)
        past = sb("rt_past", [P, MTILES, E1], F32)
        te = sb("rt_tile_expert", [P, MTILES], F32)
        sm = sb("rt_slot_sum", [P, TILES], F32)
        bk = Banks(core, [("rank", 0), ("tot", 1)])
        loaded = core.sem("rt_loaded")
        spilled = core.sem("rt_h_stored")
        step = core.sem("rt_vector_steps")
        scattered = core.sem("rt_rows_scattered")

        def over_tiles(x):
            return x.unsqueeze(1).to_broadcast([P, TILES, E1])

        def over_experts(x):
            return x.unsqueeze(2).to_broadcast([P, TILES, E1])

        with nc.Block() as block:
            @block.sync
            def _(sp):
                sp.dma_start(tri[:, :], a["before"]).then_inc(loaded, 16)
                sp.dma_start(number[:, :, :], a["tile_number"].partition_broadcast(P)).then_inc(loaded, 16)
                sp.dma_start(a["h_rows"], core.h[:, 0:TILES, :]).then_inc(spilled, 16)
                sp.wait_ge(spilled, 16)

            @block.tensor
            def _(pe):
                pe.wait_ge(loaded, 32)
                pe.wait_ge(step, 1)
                for n, w in (("rank", tri), ("tot", ones)):
                    pe.wait_ge(bk.drained((n)), bk.n_free(0, (n)))
                    nc.tensor.matmul(bk.tile(n)[:, 0:TILES * E1], w[:, :],
                                               masks[:, :, :].rearrange("p t e -> p (t e)"), start=True, stop=True)\
                        .then_inc(bk.full(n), 1)

            @block.vector
            def _(dve):
                v, done = nc.vector, [0]

                def then(ins, n=1):
                    done[0] += 1
                    ins.then_inc(step, 1)
                    dve.wait_ge(step, done[0])

                then(v.memset(ones[:, :], 1.0))
                then(v.memset(zero[:, :], 0.0))
                dve.wait_ge(bk.full("rank"), bk.n_full(0, "rank"))
                v.tensor_copy(rank[:, :, :].rearrange("p t e -> p (t e)"), bk.tile("rank")[:, 0:TILES * E1])\
                    .then_inc(bk.drained("rank"), 1)
                dve.wait_ge(bk.full("tot"), bk.n_full(0, "tot"))
                v.tensor_copy(tot[:, :, :].rearrange("p t e -> p (t e)"), bk.tile("tot")[:, 0:TILES * E1])\
                    .then_inc(bk.drained("tot"), 1)
                dve.wait_ge(bk.drained("rank"), bk.n_out(0, "rank"))
                dve.wait_ge(bk.drained("tot"), bk.n_out(0, "tot"))
                dve.wait_ge(loaded, 32)
                for e in range(E1):
                    then(v.tensor_tensor_scan(incl[:, :, e], tot[:, :, e], zero[:, :], 0.0, ALU.add, ALU.add))
                cnt = incl[:, TILES - 1, :]
                then(v.tensor_scalar(need[:, :], cnt, 1 / MT, (MT - 1) / MT - 0.5 + 0.5 / MT, ALU.mult, ALU.add))
                then(v.tensor_scalar(need[:, :], need[:, :], ROUND, ROUND, ALU.add, ALU.subtract))
                then(v.tensor_tensor_scan(cum[:, :], need[:, :], zero[:, 0:E1], 0.0, ALU.add, ALU.add))
                then(v.tensor_tensor(offs[:, :], cum[:, :], need[:, :], ALU.subtract))
                then(v.tensor_scalar(offs[:, :], offs[:, :], float(MT), None, ALU.mult))
                then(v.tensor_tensor(rank[:, :, :], rank[:, :, :], incl[:, :, :], ALU.add))
                then(v.tensor_tensor(rank[:, :, :], rank[:, :, :], tot[:, :, :], ALU.subtract))
                then(v.tensor_tensor(rank[:, :, :], rank[:, :, :], over_tiles(offs[:, :]), ALU.add))
                then(v.tensor_tensor(mp[:, :, :], rank[:, :, :], masks[:, :, :], ALU.mult))
                then(v.tensor_reduce(sl[:, :, 1], mp[:, :, :], AX.X, ALU.max))
                then(v.tensor_reduce(sm[:, :], mp[:, :, :], AX.X, ALU.add))
                then(v.tensor_tensor(sl[:, :, 0], sm[:, :], sl[:, :, 1], ALU.subtract))
                then(v.tensor_copy(slot[:, :, :], sl[:, :, :]))
                core.slots_at = done[0]
                for i in range(2):
                    then(v.tensor_tensor(mp[:, :, :], rank[:, :, :], over_experts(sl[:, :, i]), ALU.is_equal))
                    then(v.tensor_tensor(mp[:, :, :], mp[:, :, :], gates[:, :, :], ALU.mult))
                    then(v.tensor_reduce(share[:, :, i], mp[:, :, :], AX.X, ALU.add))
                then(v.tensor_tensor(past[:, :, :], number[:, :, :], cum[:, :].unsqueeze(1).to_broadcast([P, MTILES, E1]),
                                     ALU.is_ge))
                then(v.tensor_reduce(te[:, :], past[:, :, :], AX.X, ALU.add))
                then(v.tensor_scalar(te[:, :], te[:, :], float(E1 - 1), None, ALU.min))
                then(v.tensor_copy(tile_expert[:, :], te[:, :]))

            @block.gpsimd
            def _(pool):
                pool.wait_ge(step, core.slots_at)
                for t in range(TILES):
                    for i in range(2):
                        pool.indirect_dma_start(out=a["rows_in"], out_offset=bass.IndirectOffsetOnAxis(ap=slot[:, t, i:i + 1], axis=0),
                                                in_=hn[:, t, :], in_offset=None).then_inc(scattered, 16)
                pool.wait_ge(scattered, 2 * TILES * 16)
        bk.close(1)
    core.end_phase()


def experts(core, a, tile_expert):
    nc = core.nc
    NJ = 2 * FB
    SL = 4
    PAIRS = MTILES // 2
    assert MTILES % 2 == 1
    with ExitStack() as ctx:
        def sb(name, shape, dt):
            return ctx.enter_context(nc.sbuf_tensor(name, shape, dt))

        w = sb("ex_weights", [P, E1 * 2 * WX], F16)
        xin = sb("ex_rows", [P, 2, 2, D], F32)
        xh = sb("ex_xh", [P, 2, KD, MT], F16)
        xl = sb("ex_xl", [P, 2, KD, MT], F16)
        sil = sb("ex_silu", [P, SL, MT], F32)
        uu = sb("ex_u", [P, SL, MT], F32)
        uh = sb("ex_uh", [P, SL, MT], F16)
        ul = sb("ex_ul", [P, SL, MT], F16)
        yo = sb("ex_y", [P, 2, 2, D], F32)

        jobs = [(("x", 0), 0), (("x", 1), 1), (("y", 0), 6), (("y", 1), 7)]
        jobs += [(("p", j), 2 + j % 4) for j in range(NJ)]
        bk = Banks(core, jobs)
        s_w = core.sem("ex_weights_loading")
        s_wr = core.sem("ex_experts_ready")
        s_x = Loads(core, "ex_rows_loaded", 2)
        s_yo = [core.sem(f"ex_y_stored_{i}") for i in range(2)]
        act_waits = core.sem("ex_scalar_waits_passed")
        s_xh = Stage(core, "ex_xh_done", 2)
        s_sil = Stage(core, "ex_silu_done", NJ)
        s_uh = Stage(core, "ex_uh_done", NJ)
        s_ul = Stage(core, "ex_ul_done", NJ, base=NJ)
        s_dn = Stage(core, "ex_down_done", NJ - 2, base=NJ - 2)
        def before(c, j):
            if j >= SL:
                return c, j - SL
            return c - 1, max(i for i in range(NJ) if i % SL == j % SL)

        def down_done(eng, c, j):
            if j % FB == FB - 1:
                eng.wait_ge(bk.full(("y", j // FB)), bk.n_full(c, ("y", j // FB)))
            else:
                eng.wait_ge(s_dn.sem, s_dn.value(c, j - j // FB))

        AHEAD = 2
        STORE = (FB + 4, 4)
        TURNS = ((3, 0, 1), (10, 1, 0))

        with nc.Block() as block:
            @block.sync
            def _(sp):
                for i in range(2):
                    sp.sem_inc(s_yo[i], 1)
                for e in range(E1):
                    sp.dma_start(w[:, e * 2 * WX:(e + 1) * 2 * WX], a["wx"][e]).then_inc(s_w, 16)
                    sp.wait_ge(s_w, 16 * (e + 1))
                    sp.sem_inc(s_wr, 1)
                sp.wait_ge(s_yo[0], 16 * (PAIRS + 1) + 1)
                sp.wait_ge(s_yo[1], 16 * PAIRS + 1)

            @block.gpsimd
            def _(pool):
                pool.sem_inc(s_ul.sem, NJ)

                def low(c, j):
                    pool.wait_ge(s_uh.sem, s_uh.value(c, j))
                    nc.gpsimd.tensor_tensor(ul[:, j % SL, :], uu[:, j % SL, :], uh[:, j % SL, :], ALU.subtract)\
                        .then_inc(s_ul.sem, 1)

                with pool.Fori(0, PAIRS) as c:
                    for j in range(NJ):
                        low(c, j)
                for j in range(FB):
                    low(PAIRS, j)

            @block.scalar
            def _(act):
                def load(c, i):
                    tile = act.snap(2 * c + i) if not isinstance(c, int) else 2 * c + i
                    act.dma_start(xin[:, i, :, :].rearrange("p b d -> p (b d)"),
                                  a["tiles_in"][bass.ds(tile, 1)].rearrange("a p n -> (a p) n")).then_inc(s_x.sems[i], 16)

                def store(c, i):
                    tile = act.snap(2 * c + i) if not isinstance(c, int) else 2 * c + i
                    act.wait_ge(bk.drained(("y", i)), bk.n_out(c, ("y", i)))
                    act.sem_inc(act_waits, 1)
                    act.dma_start(a["tiles_out"][bass.ds(tile, 1)].rearrange("a p n -> (a p) n"),
                                  yo[:, i, :, :].rearrange("p b d -> p (b d)")).then_inc(s_yo[i], 16)

                def turn(c, i):
                    act.wait_ge(bk.full(("x", i)), bk.n_full(c, ("x", i)))
                    nc.scalar.copy(xh[:, i, :, :].rearrange("p k t -> p (k t)"), bk.tile(("x", i))[:, :]).then_inc(s_xh.sem, 1)

                def block_of(c, j):
                    pc, pj = before(c, j)
                    act.wait_ge(bk.drained(("p", pj)), bk.n_out(pc, ("p", pj)))
                    act.wait_ge(bk.full(("p", j)), bk.n_full(c, ("p", j)))
                    nc.scalar.activation(sil[:, j % SL, :], bk.tile(("p", j))[:, 0:MT], ACT.Silu, scale=1 / WS)\
                        .then_inc(s_sil.sem, 1)
                    down_done(act, pc, pj)
                    act.wait_ge(bk.drained(("p", j)), bk.n_out(c, ("p", j)))
                    nc.scalar.copy(uh[:, j % SL, :], uu[:, j % SL, :]).then_inc(s_uh.sem, 1)

                def pair(c, first=False, last=False):
                    for j in range(NJ):
                        block_of(c, j)
                        for at, dc, i in TURNS:
                            if j == at:
                                turn(c + dc, i)
                                if not last:
                                    load(c + dc + 1, i)
                        if j == STORE[0]:
                            store(c, 0)
                        if j == STORE[1] and not first:
                            store(c - 1, 1)

                load(0, 0)
                load(0, 1)
                turn(0, 0)
                load(1, 0)
                pair(0, first=True)
                with act.Fori(1, PAIRS - 1) as c:
                    pair(c)
                pair(PAIRS - 1, last=True)
                for j in range(FB):
                    block_of(PAIRS, j)
                    if j == STORE[1]:
                        store(PAIRS - 1, 1)
                store(PAIRS, 0)

            @block.vector
            def _(dve):
                def turn(c, i):
                    dve.wait_ge(s_xh.sem, s_xh.value(c, i))
                    nc.vector.tensor_tensor(xl[:, i, :, :].rearrange("p k t -> p (k t)"), bk.tile(("x", i))[:, :],
                                                       xh[:, i, :, :].rearrange("p k t -> p (k t)"), ALU.subtract)\
                        .then_inc(bk.drained(("x", i)), 1)

                def gated(c, j):
                    pc, pj = before(c, j)
                    dve.wait_ge(s_ul.sem, s_ul.value(pc, pj))
                    dve.wait_ge(s_sil.sem, s_sil.value(c, j))
                    nc.vector.scalar_tensor_tensor(uu[:, j % SL, :], sil[:, j % SL, :], 1 / WS,
                                                   bk.tile(("p", j))[:, MT:2 * MT], ALU.mult, ALU.mult)\
                        .then_inc(bk.drained(("p", j)), 1)

                def result(c, i):
                    dve.wait_ge(s_yo[i], c * 16 + 1)
                    dve.wait_ge(bk.full(("y", i)), bk.n_full(c, ("y", i)))
                    nc.vector.tensor_scalar(yo[:, i, :, :].rearrange("p b d -> p (b d)"), bk.tile(("y", i))[:, :],
                                            1 / WS, None, ALU.mult).then_inc(bk.drained(("y", i)), 1)

                turn(0, 0)
                with dve.Fori(0, PAIRS) as c:
                    for j in range(NJ):
                        gated(c, j)
                        for at, dc, i in TURNS:
                            if j == at:
                                turn(c + dc, i)
                        if j == FB - 1 + AHEAD:
                            result(c, 0)
                    result(c, 1)
                for j in range(FB):
                    gated(PAIRS, j)
                result(PAIRS, 0)

            @block.tensor
            def _(pe):
                pe.sem_inc(s_dn.sem, NJ - 2)

                def choose(c, i):
                    n = 2 * c + i
                    e = pe.value_load(tile_expert[0:1, n:n + 1] if isinstance(n, int) else tile_expert[0:1, bass.ds(n, 1)],
                                      min_val=0, max_val=E1 - 1)
                    pe.wait_ge(s_wr, e + 1)
                    pe.sem_inc(core.tensor_waits, 1)
                    return pe.snap(e * (2 * WX))

                def turn(c, i):
                    pe.wait_ge(s_x.sems[i], s_x.value(c))
                    pe.wait_ge(bk.drained(("x", i)), bk.n_free(c, ("x", i)))
                    for kd in range(KD):
                        for b in range(2):
                            last = nc.tensor.transpose(bk.tile(("x", i))[:, kd * MT + b * P:kd * MT + (b + 1) * P],
                                                       xin[:, i, b, kd * P:(kd + 1) * P], core.ident[:, :])
                    last.then_inc(bk.full(("x", i)), 1)

                def up(c, j, at):
                    i, fb = j // FB, j % FB
                    if fb == 0:
                        pe.wait_ge(bk.drained(("x", i)), bk.n_out(c, ("x", i)))
                        pe.sem_inc(core.tensor_waits, 1)
                    pe.wait_ge(bk.drained(("p", j)), bk.n_free(c, ("p", j)))
                    for which in range(2):
                        for kd in range(KD):
                            cols = (which * KD + kd) * FFN + fb * P
                            last = three(nc, bk.tile(("p", j))[:, which * MT:(which + 1) * MT],
                                         [w[:, bass.ds(at + (s * WX + cols), P)] for s in range(2)],
                                         (xh[:, i, kd, :], xl[:, i, kd, :]), kd == 0, kd == KD - 1)
                    last.then_inc(bk.full(("p", j)), 1)

                def down(c, j, at):
                    i, fb = j // FB, j % FB
                    if fb == 0:
                        pe.wait_ge(bk.drained(("y", i)), bk.n_free(c, ("y", i)))
                    pe.wait_ge(s_ul.sem, s_ul.value(c, j))
                    for b in range(2):
                        last = three(nc, bk.tile(("y", i))[:, b * D:(b + 1) * D],
                                     (uh[:, j % SL, b * P:(b + 1) * P], ul[:, j % SL, b * P:(b + 1) * P]),
                                     [w[:, bass.ds(at + (s * WX + W13 + fb * D), D)] for s in range(2)],
                                     fb == 0 and b == 0, fb == FB - 1 and b == 1)
                    if fb == FB - 1:
                        last.then_inc(bk.full(("y", i)), 1)
                    else:
                        last.then_inc(s_dn.sem, 1)

                turn(0, 0)
                first = choose(0, 0)
                for j in range(AHEAD):
                    up(0, j, first)
                with pe.Fori(0, PAIRS) as c:
                    at = [choose(c, 0), None]
                    for j in range(NJ):
                        if j + AHEAD == FB:
                            at[1] = choose(c, 1)
                        if j + AHEAD == NJ:
                            following = choose(c + 1, 0)
                        if j + AHEAD < NJ:
                            up(c, j + AHEAD, at[(j + AHEAD) // FB])
                        else:
                            up(c + 1, j + AHEAD - NJ, following)
                        for k, dc, i in TURNS:
                            if j + AHEAD == k:
                                turn(c + dc, i)
                        down(c, j, at[j // FB])
                final = choose(PAIRS, 0)
                for j in range(FB):
                    if j + AHEAD < FB:
                        up(PAIRS, j + AHEAD, final)
                    down(PAIRS, j, final)
    core.end_phase()


def combine(core, a, slot, share, out):
    nc = core.nc
    with ExitStack() as ctx:
        def sb(name, shape, dt):
            return ctx.enter_context(nc.sbuf_tensor(name, shape, dt))

        h = sb("cb_h", [P, TILES, D], F32)
        y = sb("cb_y", [P, TILES, 2, D], F32)
        loaded = core.sem("cb_h_loaded")
        gathered = [core.sem(f"cb_gathered_{t}") for t in range(TILES)]
        added = core.sem("cb_added")
        stored = core.sem("cb_stored")
        out_v = out.rearrange("b s d -> (b s) d").rearrange("(t p) d -> p t d", p=P)
        with nc.Block() as block:
            @block.sync
            def _(sp):
                sp.dma_start(h[:, :, :], a["h_rows"]).then_inc(loaded, 16)
                for t in range(0, TILES, U):
                    sp.wait_ge(added, 2 * (t + U))
                    sp.dma_start(out_v[:, t:t + U, :], h[:, t:t + U, :]).then_inc(stored, 16)
                sp.wait_ge(stored, 16 * CHUNKS)

            @block.gpsimd
            def _(pool):
                for t in range(TILES):
                    for i in range(2):
                        pool.indirect_dma_start(out=y[:, t, i, :], out_offset=None, in_=a["rows_out"],
                                                in_offset=bass.IndirectOffsetOnAxis(ap=slot[:, t, i:i + 1], axis=0))\
                            .then_inc(gathered[t], 16)

            @block.vector
            def _(dve):
                dve.wait_ge(loaded, 16)
                for t in range(TILES):
                    dve.wait_ge(gathered[t], 32)
                    for i in range(2):
                        if i:
                            dve.wait_ge(added, 2 * t + 1)
                        nc.vector.scalar_tensor_tensor(h[:, t, :], y[:, t, i, :], share[:, t, i:i + 1], h[:, t, :],
                                                       ALU.mult, ALU.add).then_inc(added, 1)
    core.end_phase()


UPTO = 5


def store_rows(core, out):
    nc = core.nc
    stored = core.sem("rows_stored")
    with nc.Block() as block:
        @block.sync
        def _(sp):
            sp.dma_start(out.rearrange("b s d -> (b s) d").rearrange("(t p) d -> p t d", p=P), core.h[:, 0:TILES, :]).then_inc(stored, 16)
            sp.wait_ge(stored, 16)


def program(nc, a, out, upto):
    with ExitStack() as ctx:
        core = Core(nc, ctx)
        slot = core.sb("slot", [P, TILES, 2], I32)
        share = core.sb("share", [P, TILES, 2], F32)
        tile_expert = core.sb("tile_expert", [P, MTILES], I32)
        with ExitStack() as rows:
            core.h = rows.enter_context(nc.sbuf_tensor("h", [P, TILES + U, D], F32))
            prepare(core, a)
            attn0(core, a)
            if upto > 1:
                ffn0(core, a)
            if upto > 2:
                attn1(core, a)
            if upto > 3:
                hn = rows.enter_context(nc.sbuf_tensor("hn", [P, TILES, D], F32))
                gates = rows.enter_context(nc.sbuf_tensor("gates", [P, TILES, 8], F32))
                masks = rows.enter_context(nc.sbuf_tensor("expert_masks", [P, TILES, 8], F32))
                block1(core, a, hn, gates, masks)
            if upto < 5:
                store_rows(core, out)
                return
            route(core, a, hn, gates, masks, slot, share, tile_expert)
        experts(core, a, tile_expert)
        combine(core, a, slot, share, out)


def constants():
    p = np.arange(P)
    eye = np.eye(P, dtype=np.float32)
    hm = (p[:, None] // 16 == np.arange(8)[None, :]).astype(np.float32)
    vm = (p[:, None] // SEQ == (np.arange(D)[None, :] // 16) % 2).astype(np.float32)
    rows = np.zeros((16, 8, P), np.float16)
    for e in range(8):
        rows[[e, 8 + e], e, :] = 1
    pos = (p % SEQ).astype(np.float32)[:, None]
    ang = pos * np.power(np.float32(10000.0), -(np.arange(32, dtype=np.float32) / np.float32(32)))[None, :]
    cos, sin = np.cos(ang), np.sin(ang)
    rot = np.stack([np.concatenate([cos, cos], 1), np.concatenate([-sin, -sin], 1), np.concatenate([sin, sin], 1)], 1)
    inv = np.float32(1.0) / np.power(np.float32(1000000.0), np.arange(0, P, 2, dtype=np.float32) / np.float32(P))
    ang = pos * inv[None, :]
    cos, sin = np.cos(ang), np.sin(ang)
    rot2 = np.stack([np.concatenate([cos, cos], 1), np.concatenate([-sin, sin], 1)], 1)
    seen = (p[:, None] // SEQ == p[None, :] // SEQ) & (p[None, :] <= p[:, None])
    mask = np.where(seen, 0.0, NEG).astype(np.float32)
    before = (p[:, None] < p[None, :]).astype(np.float32)
    number = np.repeat(np.arange(MTILES, dtype=np.float32)[:, None], E1, 1)
    return {"before": before, "tile_number": number, "rot_a1": rot.astype(np.float32), "rot_b1": rot2.astype(np.float32), "causal_mask": mask, "ident": eye, "ident16": eye.astype(np.float16), "head_mask": hm, "v_mask": vm, "expert_rows": rows}


def kernel(**inputs):
    import numpy as _np
    import concourse.bacc as _bacc
    from concourse import mybir as _mybir
    from concourse.bass_utils import run_bass_kernel_spmd as _run

    nc = _bacc.Bacc("TRN2", target_bir_lowering=False, num_devices=1)
    raw = {n: _np.asarray(v) for n, v in inputs.items()}
    lay = dict(constants())
    lay["x"] = raw["x"].reshape(TILES, P).T
    for n in ("L0_attn_Wq", "L0_attn_Wk", "L0_attn_Wv", "L0_attn_Wo"):
        lay[n] = raw[n].T
    for n in ("L0_tok_W", "L0_tok_b", "L0_attn_bv", "L0_attn_bo"):
        lay[n] = raw[n]
    lay["bqk"] = _np.stack([raw["L0_attn_bq"].reshape(KD, P), raw["L0_attn_bk"].reshape(KD, P)]).transpose(2, 0, 1)
    first = 255 - (SEQ - 1)
    relk = _np.concatenate([raw["L0_attn_relative_k"][first:first + 2 * SEQ - 1], _np.zeros((1, 16), _np.float32)])
    lay["relk"] = _np.tile(relk.T, (8, 1))
    relv = _np.concatenate([raw["L0_attn_relative_v"][first:first + 2 * SEQ - 1], _np.zeros((1, 16), _np.float32)])
    none = _np.zeros_like(relv)
    lay["relv"] = _np.stack([_np.concatenate([relv, none], 1), _np.concatenate([none, relv], 1)], 1)
    lay["w_gate_t"] = raw["L1_ffn_w_gate"].T
    for n in inputs:
        if n not in lay and n.startswith(("L0_ffn", "L1")):
            lay[n] = raw[n]
    arrays, a = {}, {}
    for n, v in lay.items():
        v = _np.ascontiguousarray(v)
        arrays["in_" + n] = v
        a[n] = nc.dram_tensor("in_" + n, v.shape, _mybir.dt.from_np(v.dtype), kind="ExternalInput").ap()
    MH = 2 * SEQ * 16
    a["qr"] = nc.dram_tensor("qr", (TILES, P, MH), F32, kind="Internal").ap()
    a["qr_flat"] = a["qr"].rearrange("a p n -> (a p n)")
    a["skew"] = nc.dram_tensor("skew", (U, P, MH), F32, kind="Internal").ap()
    a["skew_flat"] = a["skew"].rearrange("a p n -> (a p n)")
    a["wx"] = nc.dram_tensor("wx", (E1, P, 2 * WX), F16, kind="Internal").ap()
    a["h_rows"] = nc.dram_tensor("h_rows", (P, TILES, D), F32, kind="Internal").ap()
    for n in ("in", "out"):
        rows = nc.dram_tensor("expert_rows_" + n, (MTILES * MT, D), F32, kind="Internal").ap()
        a["rows_" + n] = rows
        a["tiles_" + n] = rows.rearrange("(t p b) d -> t p (b d)", p=P, b=2)
    out = nc.dram_tensor("out_0", (64, SEQ, D), F32, kind="ExternalOutput").ap()
    program(nc, a, out, UPTO)
    r = _run(nc, [arrays], core_ids=[0])
    return r.results[0]["out_0"]
```
